# Optimizing a Trainium2 kernel written in Bass

```python
import numpy as np
import jax
import jax.numpy as jnp

def _softmax(x, axis=-1):
    return jax.nn.softmax(x, axis=axis)

def _gelu(x):
    return jax.nn.gelu(x, approximate=True)

def _silu(x):
    return jax.nn.silu(x)

def _sigmoid(x):
    return jax.nn.sigmoid(x)

def _layernorm(x, axis=-1, eps=1e-05):
    m = jnp.mean(x, axis=axis, keepdims=True)
    v = jnp.var(x, axis=axis, keepdims=True)
    return (x - m) / jnp.sqrt(v + eps)

def _scatter_add(tgt, idx, src, axis=0):
    return tgt.at[idx].add(src)

def _segment_sum(src, seg, n):
    return jax.ops.segment_sum(src, seg, n)
kernel_name = 'mk_macaron_d1_jaxref_r8_b209a5'

def setup_inputs(seed: int=0):
    np.random.seed(seed)
    _w = jnp.asarray

    def _L0_attn_setup():
        import jax, jax.numpy as jnp
        import numpy as np
        NUM_HEADS = 32
        MAX_BIAS_LENGTH = 128
        ROPE_BASE = 10000.0

        def _rope_cos_sin(seq_len, head_dim, dtype):
            half = head_dim // 2
            inv_freq = 1.0 / ROPE_BASE ** (jnp.arange(0, half, dtype=jnp.float32) / half)
            t = jnp.arange(seq_len, dtype=jnp.float32)
            freqs = jnp.outer(t, inv_freq)
            return (jnp.cos(freqs).astype(dtype), jnp.sin(freqs).astype(dtype))

        def _apply_rope(x, cos, sin):
            half = x.shape[-1] // 2
            x1, x2 = (x[..., :half], x[..., half:])
            c = cos[None, :, None, :]
            s = sin[None, :, None, :]
            return jnp.concatenate([x1 * c - x2 * s, x1 * s + x2 * c], axis=-1)
        key = jax.random.key(seed)
        ks = jax.random.split(key, 7)
        B, S, Dm = (2, 256, 256)
        std = 1.0 / np.sqrt(Dm)
        return {'hidden_states': jax.random.normal(ks[0], (B, S, Dm), jnp.float32), 'Wq': jax.random.normal(ks[1], (Dm, Dm), jnp.float32) * std, 'Wk': jax.random.normal(ks[2], (Dm, Dm), jnp.float32) * std, 'Wv': jax.random.normal(ks[3], (Dm, Dm), jnp.float32) * std, 'Wo': jax.random.normal(ks[4], (Dm, Dm), jnp.float32) * std, 'learnable_bias': jax.random.normal(ks[5], (NUM_HEADS, MAX_BIAS_LENGTH), jnp.float32) * 0.001, 'softmax_offset': jnp.zeros((NUM_HEADS,), jnp.float32)}
    _L0_attn_in = _L0_attn_setup()

    def _L0_ffn_setup():
        import jax, jax.numpy as jnp
        import numpy as np
        E, K, H, I = (64, 6, 256, 176)
        NS = 2
        IS = NS * I
        CAP = 32
        T_TOKENS = (1, 128)
        SCALE = 0.02

        def _moe_infer(x, gate_w, w_gate, w_up, w_down):
            T = x.shape[0]
            TK = T * K
            logits = x @ gate_w.T
            scores = jax.nn.softmax(logits, axis=-1)
            topk_w, topk_i = jax.lax.top_k(scores, K)
            flat_i = topk_i.reshape(-1)
            flat_w = topk_w.reshape(-1)
            token_ids = jnp.arange(TK, dtype=jnp.int32) // K
            order = jnp.argsort(flat_i)
            sorted_e = flat_i[order]
            counts = jnp.bincount(flat_i, length=E)
            starts = jnp.concatenate([jnp.zeros((1,), counts.dtype), jnp.cumsum(counts)[:-1]])
            pos_sorted = jnp.arange(TK) - starts[sorted_e]
            pos = jnp.zeros((TK,), jnp.int32).at[order].set(pos_sorted.astype(jnp.int32))
            valid = pos < CAP
            slot = jnp.where(valid, pos, CAP)
            buf = jnp.zeros((E, CAP + 1, H), x.dtype).at[flat_i, slot].set(x[token_ids])
            g = jnp.einsum('ech,ehi->eci', buf, w_gate)
            u = jnp.einsum('ech,ehi->eci', buf, w_up)
            y = jnp.einsum('eci,eih->ech', jax.nn.silu(g) * u, w_down)
            out_slots = y[flat_i, slot] * (flat_w * valid)[:, None]
            return out_slots.reshape(T, K, H).sum(axis=1)
        key = jax.random.key(seed)
        ks = jax.random.split(key, 8)
        f32 = jnp.float32
        return {'hidden_states': jax.random.normal(ks[0], (*T_TOKENS, H), f32), 'gate_w': jax.random.normal(ks[1], (E, H), f32) * SCALE, 'w_gate': jax.random.normal(ks[2], (E, H, I), f32) * SCALE, 'w_up': jax.random.normal(ks[3], (E, H, I), f32) * SCALE, 'w_down': jax.random.normal(ks[4], (E, I, H), f32) * SCALE, 'sw_gate': jax.random.normal(ks[5], (H, IS), f32) * SCALE, 'sw_up': jax.random.normal(ks[6], (H, IS), f32) * SCALE, 'sw_down': jax.random.normal(ks[7], (IS, H), f32) * SCALE}
    _L0_ffn_in = _L0_ffn_setup()
    _d = {'L0_attn_hidden_states': _L0_attn_in['hidden_states'], 'L0_attn_Wq': _L0_attn_in['Wq'], 'L0_attn_Wk': _L0_attn_in['Wk'], 'L0_attn_Wv': _L0_attn_in['Wv'], 'L0_attn_Wo': _L0_attn_in['Wo'], 'L0_attn_learnable_bias': _L0_attn_in['learnable_bias'], 'L0_attn_softmax_offset': _L0_attn_in['softmax_offset'], 'L0_ffn_gate_w': _L0_ffn_in['gate_w'], 'L0_ffn_w_gate': _L0_ffn_in['w_gate'], 'L0_ffn_w_up': _L0_ffn_in['w_up'], 'L0_ffn_w_down': _L0_ffn_in['w_down'], 'L0_ffn_sw_gate': _L0_ffn_in['sw_gate'], 'L0_ffn_sw_up': _L0_ffn_in['sw_up'], 'L0_ffn_sw_down': _L0_ffn_in['sw_down']}
    _x0 = _d['L0_attn_hidden_states']
    _d['L0_attn_hidden_states'] = jax.random.normal(jax.random.fold_in(jax.random.key(seed), 1), (4, 256, 256), dtype=_x0.dtype)
    del _x0
    return _d

def reference(L0_attn_hidden_states, L0_attn_Wq, L0_attn_Wk, L0_attn_Wv, L0_attn_Wo, L0_attn_learnable_bias, L0_attn_softmax_offset, L0_ffn_gate_w, L0_ffn_w_gate, L0_ffn_w_up, L0_ffn_w_down, L0_ffn_sw_gate, L0_ffn_sw_up, L0_ffn_sw_down):

    def _L0_attn_ref(hidden_states, Wq, Wk, Wv, Wo, learnable_bias, softmax_offset):
        import jax, jax.numpy as jnp
        import numpy as np
        NUM_HEADS = 32
        MAX_BIAS_LENGTH = 128
        ROPE_BASE = 10000.0

        def _rope_cos_sin(seq_len, head_dim, dtype):
            half = head_dim // 2
            inv_freq = 1.0 / ROPE_BASE ** (jnp.arange(0, half, dtype=jnp.float32) / half)
            t = jnp.arange(seq_len, dtype=jnp.float32)
            freqs = jnp.outer(t, inv_freq)
            return (jnp.cos(freqs).astype(dtype), jnp.sin(freqs).astype(dtype))

        def _apply_rope(x, cos, sin):
            half = x.shape[-1] // 2
            x1, x2 = (x[..., :half], x[..., half:])
            c = cos[None, :, None, :]
            s = sin[None, :, None, :]
            return jnp.concatenate([x1 * c - x2 * s, x1 * s + x2 * c], axis=-1)
        B, S, Dm = hidden_states.shape
        H = NUM_HEADS
        D = Dm // H
        scale = D ** (-0.5)
        q = (hidden_states @ Wq.T).reshape(B, S, H, D)
        k = (hidden_states @ Wk.T).reshape(B, S, H, D)
        v = (hidden_states @ Wv.T).reshape(B, S, H, D)
        cos, sin = _rope_cos_sin(S, D, q.dtype)
        q = _apply_rope(q, cos, sin)
        k = _apply_rope(k, cos, sin)
        q = q.transpose(0, 2, 1, 3)
        k = k.transpose(0, 2, 1, 3)
        v = v.transpose(0, 2, 1, 3)
        scores = jnp.einsum('bhid,bhjd->bhij', q, k) * scale
        i = jnp.arange(S)[:, None]
        j = jnp.arange(S)[None, :]
        diag = i - j
        causal = diag >= 0
        in_band = causal & (diag < MAX_BIAS_LENGTH)
        bias = jnp.where(in_band, learnable_bias[:, jnp.clip(diag, 0, MAX_BIAS_LENGTH - 1)], 0.0)
        scores = scores + bias[None]
        scores = jnp.where(causal[None, None], scores, -jnp.inf)
        off = softmax_offset[None, :, None]
        m = jnp.maximum(jnp.max(scores, axis=-1), off)
        p = jnp.exp(scores - m[..., None])
        denom = jnp.sum(p, axis=-1) + jnp.exp(off - m)
        out = jnp.einsum('bhij,bhjd->bhid', p, v) / denom[..., None]
        out = out.transpose(0, 2, 1, 3).reshape(B, S, Dm)
        return out @ Wo.T

    def _L0_ffn_ref(hidden_states, gate_w, w_gate, w_up, w_down, sw_gate, sw_up, sw_down):
        import jax, jax.numpy as jnp
        import numpy as np
        E, K, H, I = (64, 6, 256, 176)
        NS = 2
        IS = NS * I
        CAP = 32
        T_TOKENS = (1, 128)
        SCALE = 0.02

        def _moe_infer(x, gate_w, w_gate, w_up, w_down):
            T = x.shape[0]
            TK = T * K
            logits = x @ gate_w.T
            scores = jax.nn.softmax(logits, axis=-1)
            topk_w, topk_i = jax.lax.top_k(scores, K)
            flat_i = topk_i.reshape(-1)
            flat_w = topk_w.reshape(-1)
            token_ids = jnp.arange(TK, dtype=jnp.int32) // K
            order = jnp.argsort(flat_i)
            sorted_e = flat_i[order]
            counts = jnp.bincount(flat_i, length=E)
            starts = jnp.concatenate([jnp.zeros((1,), counts.dtype), jnp.cumsum(counts)[:-1]])
            pos_sorted = jnp.arange(TK) - starts[sorted_e]
            pos = jnp.zeros((TK,), jnp.int32).at[order].set(pos_sorted.astype(jnp.int32))
            valid = pos < CAP
            slot = jnp.where(valid, pos, CAP)
            buf = jnp.zeros((E, CAP + 1, H), x.dtype).at[flat_i, slot].set(x[token_ids])
            g = jnp.einsum('ech,ehi->eci', buf, w_gate)
            u = jnp.einsum('ech,ehi->eci', buf, w_up)
            y = jnp.einsum('eci,eih->ech', jax.nn.silu(g) * u, w_down)
            out_slots = y[flat_i, slot] * (flat_w * valid)[:, None]
            return out_slots.reshape(T, K, H).sum(axis=1)
        orig_shape = hidden_states.shape
        x = hidden_states.reshape(-1, orig_shape[-1])
        y = _moe_infer(x, gate_w, w_gate, w_up, w_down).reshape(orig_shape)
        shared = jax.nn.silu(hidden_states @ sw_gate) * (hidden_states @ sw_up) @ sw_down
        return y + shared
    x = L0_attn_hidden_states
    x = x + 0.5 * _L0_ffn_ref(_layernorm(x, axis=-1), L0_ffn_gate_w, L0_ffn_w_gate, L0_ffn_w_up, L0_ffn_w_down, L0_ffn_sw_gate, L0_ffn_sw_up, L0_ffn_sw_down)
    x = x + _L0_attn_ref(_layernorm(x, axis=-1), L0_attn_Wq, L0_attn_Wk, L0_attn_Wv, L0_attn_Wo, L0_attn_learnable_bias, L0_attn_softmax_offset)
    x = x + 0.5 * _L0_ffn_ref(_layernorm(x, axis=-1), L0_ffn_gate_w, L0_ffn_w_gate, L0_ffn_w_up, L0_ffn_w_down, L0_ffn_sw_gate, L0_ffn_sw_up, L0_ffn_sw_down)
    return x

_drawn_inputs = setup_inputs


def setup_inputs(seed=0):
    import zlib

    import numpy as np

    out = dict(_drawn_inputs(seed))
    spreads = {'L0_attn_softmax_offset': (0.0, 0.8)}
    factors = {'L0_attn_learnable_bias': 64.0,
     'L0_ffn_gate_w': 8.0,
     'L0_ffn_w_gate': 8.0,
     'L0_ffn_w_up': 8.0,
     'L0_ffn_w_down': 8.0,
     'L0_ffn_sw_gate': 2.929,
     'L0_ffn_sw_up': 2.894,
     'L0_ffn_sw_down': 2.892}
    for name, (base, spread) in spreads.items():
        noise = np.random.default_rng([zlib.crc32(name.encode()), seed]).standard_normal(out[name].shape)
        drawn = base * np.exp(spread * noise) if base else spread * noise
        out[name] = jnp.asarray(drawn.astype(out[name].dtype))
    for name, factor in factors.items():
        out[name] = (out[name] * factor).astype(out[name].dtype)
    return out
```

```python
from contextlib import ExitStack

import numpy as np
import concourse.bass as bass
from concourse import mybir

F32 = mybir.dt.float32
BF16 = mybir.dt.bfloat16
U32 = mybir.dt.uint32
ALU = mybir.AluOpType
ACT = mybir.ActivationFunctionType
AX_X = mybir.AxisListType.X

P = 128
B, S, DM = 4, 256, 256
T = B * S
NT = T // P
KC = DM // P
NH, HD = 32, 8
MAXB = 128
E, TOPK, I = 64, 6, 176
CAP = 32
IS = 2 * I
EC = P // CAP
NC = E // EC
RING = 4
ILO, IHI = P, I - P
EPS = 1e-5
PAD = 3.0e38
MASKED = -1.0e30
FAR = 100000.0
NF = 4
RW = NF * EC + 3
NQUAD = T // S * NH // 4
SH = [P, P, IS - 2 * P]


PROBS_TURN = [1, 1, 0, 1, 0, 1, 1, 0]
QK_TURN = 0


class Chunk:

    def __init__(self, i, scale, c):
        self.i, self.scale, self.c = i, scale, c

    def times(self, k, plus=0):
        return self.i * (self.scale * k) + k * (self.c + plus)

    def rounds(self, of, k, plus=0):
        return self.i * (self.scale // of * k) + k * (self.c // of + plus)

    def after(self, k):
        return Chunk(self.i, self.scale, self.c + k)

    def below(self, k):
        return isinstance(self.i, int) and self.c < k


def wait_count(eng, sem, value):
    if isinstance(value, int) and value <= 0:
        return
    eng.wait_ge(sem, value)


def norm_vector(vec, m, s):
    for t in range(NT):
        vec.bn_stats(m.stats[:, t, :], m.x[:, t, :]).then_inc(s.stats_done, 1)
    for t in range(NT):
        vec.wait_ge(s.stats_done, t + 1)
        vec.bn_aggr(m.moments[:, t, :], m.stats[:, t, :]).then_inc(s.moments_done, 1)
    vec.wait_ge(s.moments_done, NT)
    vec.tensor_scalar(m.var_eps[:, :], m.moments[:, :, 1], EPS, None, ALU.add).then_inc(s.var_ready, 1)
    vec.wait_ge(s.std_ready, 1)
    vec.reciprocal(m.rstd[:, :], m.std[:, :]).then_inc(s.rstd_ready, 1)
    vec.wait_ge(s.rstd_ready, 1)
    for t in range(NT):
        vec.tensor_scalar(m.xn[:, t, :], m.x[:, t, :], m.moments[:, t, 0:1], m.rstd[:, t:t + 1],
                          ALU.subtract, ALU.mult).then_inc(s.xn_ready, 1)
    for half in range(2):
        vec.wait_ge(s.xnT_psum, 2 * half + 2)
        vec.tensor_copy(m.xnT[:, 1, half * 512:half * 512 + 512], m.bank[2 * half + 1][:, :]).then_inc(s.xnT_vec, 1)


def norm_scalar(act, m, s):
    act.wait_ge(s.var_ready, 1)
    act.activation(m.std[:, :], m.var_eps[:, :], ACT.Sqrt).then_inc(s.std_ready, 1)
    for half in range(2):
        act.wait_ge(s.xnT_psum, 2 * half + 1)
        act.copy(m.xnT[:, 0, half * 512:half * 512 + 512], m.bank[2 * half][:, :]).then_inc(s.xnT_act, 1)


def norm_tensor(pe, m, s):
    for half in range(2):
        for q in range(4):
            t = 4 * half + q
            pe.wait_ge(s.xn_ready, t + 1)
            for c in range(KC):
                ins = pe.transpose(m.bank[2 * half + c][:, q * P:q * P + P],
                                   m.xn[:, t, c * P:c * P + P], m.ident[:, :])
                if q == 3:
                    ins.then_inc(s.xnT_psum, 1)


class NormSems:

    def __init__(self, sem):
        self.stats_done = sem("stats_done")
        self.moments_done = sem("moments_done")
        self.var_ready = sem("var_ready")
        self.std_ready = sem("std_ready")
        self.rstd_ready = sem("rstd_ready")
        self.xn_ready = sem("xn_ready")
        self.xnT_psum = sem("xnT_psum")
        self.xnT_vec = sem("xnT_vec")
        self.xnT_act = sem("xnT_act")


def load_expert_chunk(sp, w, m, loaded, slot, chunk):
    sp.dma_start(m.w_gu[:, slot, :], w.w_gu[chunk].squeeze(0)).then_inc(loaded[slot], 16)
    sp.dma_start(m.w_lo[:, slot, :], w.w_lo[chunk].squeeze(0)).then_inc(loaded[slot], 16)
    sp.dma_start(m.w_hi[:, slot, :], w.w_hi[chunk].squeeze(0)).then_inc(loaded[slot], 16)


def first_chunks(sp, w, m, loaded):
    for n in range(RING):
        load_expert_chunk(sp, w, m, loaded, n, slice(n, n + 1))


def feed_forward(nc, w, m, sems, tag, weights_loaded, gathered, scattered, first, last):
    with ExitStack() as ctx:
        def sb(name, shape, dt=F32):
            return ctx.enter_context(nc.sbuf_tensor(f"{tag}_{name}", shape, dt))

        def sem(name):
            return sems(name)

        onehot = sb("onehot", [P, NT, CAP, E], BF16)
        combined = onehot[:, :, :, :].rearrange("p t c e -> p (t c e)").bitcast(F32)
        choice_rows = [combined[:, i * TOPK * DM:(i + 1) * TOPK * DM] for i in range(4)]
        facts = sb("facts", [P, NT, NC, RW], BF16)
        logits = sb("logits", [P, NT, E + 2])
        replaced = sb("replaced", [P, NT, E + 2])
        top = sb("top", [P, NT, 8])
        chosen = sb("chosen", [P, NT, E], BF16)
        shifted = sb("shifted", [P, NT, E])
        expl = sb("expl", [P, NT, E])
        esum = sb("esum", [P, NT])
        rsum = sb("rsum", [P, NT])
        rank = sb("rank", [P, NT * E])
        unchosen = sb("unchosen", [P, NT * E])
        place = sb("place", [P, NT * E], BF16)
        slot_sums = sb("slot_sums", [P, NC, RW])
        own = sb("own", [P, NC, NF * EC])
        own_facts = sb("own_facts", [P, NC, NF])
        slot_weight = sb("slot_weight", [P, NC])
        slot_token = sb("slot_token", [P, NC])
        slot_far = sb("slot_far", [P, NC])
        slot_row = sb("slot_row", [P, NC])
        gather_index = sb("gather_index", [P, NC], U32)
        scatter_index = sb("scatter_index", [P, NC], U32)
        sh_silu = sb("sh_silu", [P, 2, 512])
        sh_hT = sb("sh_hT", [P, 3, 512])
        xg = sb("xg", [P, 2, DM])
        xgT = sb("xgT", [P, 2, KC * P])
        gsilu = sb("gsilu", [P, 2, I])
        h = sb("h", [P, 2, I])
        hT = sb("hT", [P, 2, 2 * P])
        y = sb("y", [P, 2, DM])
        total = sb("total", [P, 2, DM])

        s = NormSems(sem)
        (x_loaded, small_loaded, consts_ready, table_zeroed, zeros_ready, pads_ready, xn_stored, logits_psum,
         logits_sb, top_ready, replaced_ready, chosen_ready, shifted_ready, expl_ready, esum_ready, rsum_ready,
         probs_ready, weight_ready, scan_ready, counts_psum, unchosen_ready, place_ready, onehot_ready, fact_ready,
         rest_ready, slots_psum, slot_sums_ready, own_ready, slot_step, slots_ready, sh_up_psum, sh_silu_ready,
         sh_hT_ready, sh_y_psum, sh_added, xgT_psum, xgT_ready, gu_psum, silu_ready, h_ready, hT_psum, hT_ready,
         y_psum, y_ready, total_ready, x_ready, out_stored, mask_ready) = [sem(n) for n in (
             "x_loaded small_loaded consts_ready table_zeroed zeros_ready pads_ready xn_stored logits_psum "
             "logits_sb top_ready replaced_ready chosen_ready shifted_ready expl_ready esum_ready rsum_ready "
             "probs_ready weight_ready scan_ready counts_psum unchosen_ready place_ready onehot_ready fact_ready "
             "rest_ready slots_psum slot_sums_ready own_ready slot_step slots_ready sh_up_psum sh_silu_ready "
             "sh_hT_ready sh_y_psum sh_added xgT_psum xgT_ready gu_psum silu_ready h_ready hT_psum hT_ready "
             "y_psum y_ready total_ready x_ready out_stored mask_ready").split()]
        choices_loaded = [sem(f"choices_loaded{i}") for i in range(4)]

        bank = m.bank
        logits_bank = bank[4][:, :].rearrange("p (t e) -> p t e", e=E)
        counts_bank = bank[5]
        slots_bank = bank[6]
        sh_up_banks = [(bank[0], bank[1]), (bank[2], bank[3])]
        sh_y_banks = [bank[4], bank[7]]
        xgT_banks, gu_banks, hT_banks, y_banks = bank[0:2], bank[2:4], bank[4:6], bank[6:8]
        xn_rows = w.xn_dram
        table_tiles = w.table.rearrange("(t p k) d -> t p k d", p=P, k=TOPK)
        out_tiles = w.out.rearrange("b s d -> (b s) d").rearrange("(t p) d -> t p d", p=P)
        x_tiles = w.x.rearrange("(t p) d -> t p d", p=P)
        xn_tiles = w.xn_dram.rearrange("(t p) d -> t p d", p=P)

        block = ctx.enter_context(nc.Block())

        @block.sync
        def _(sp):
            if first:
                for t in range(NT):
                    sp.dma_start(m.x[:, t, :], x_tiles[t]).then_inc(x_loaded, 16)
                sp.dma_start(m.gate[:, :, :], w.gate_t.rearrange("(c p) e -> p c e", p=P)).then_inc(small_loaded, 16)
                sp.dma_start(m.sh_gate[:, :, :], w.sw_gate.rearrange("(c p) i -> p c i", p=P)).then_inc(small_loaded, 16)
                sp.dma_start(m.sh_up[:, :, :], w.sw_up.rearrange("(c p) i -> p c i", p=P)).then_inc(small_loaded, 16)
                sp.dma_start(m.sh_down[:, 0:2, :],
                             w.sw_down[0:2 * P, :].rearrange("(c p) d -> p c d", p=P)).then_inc(small_loaded, 16)
                sp.dma_start(m.sh_down[0:SH[2], 2, :], w.sw_down[2 * P:IS, :]).then_inc(small_loaded, 16)
                first_chunks(sp, w, m, weights_loaded)
            for t in range(NT):
                sp.wait_ge(s.xn_ready, t + 1)
                sp.dma_start(xn_tiles[t], m.xn[:, t, :]).then_inc(xn_stored, 16)
            for n in range(RING, NC):
                sp.wait_ge(weights_loaded[n % RING], 48 * (n // RING))
                sp.wait_ge(y_psum, n + 1 - RING)
                load_expert_chunk(sp, w, m, weights_loaded, n % RING, slice(n, n + 1))
            for p in range(2):
                sp.wait_ge(scattered[p], 16 * (NC // 2))
            for t in range(NT):
                if t >= 4:
                    sp.wait_ge(total_ready, t - 3)
                sp.dma_start(choice_rows[t % 4], table_tiles[t].rearrange("p k d -> p (k d)"))\
                  .then_inc(choices_loaded[t % 4], 16)
            if last:
                for t in range(NT):
                    sp.wait_ge(x_ready, t + 1)
                    sp.dma_start(out_tiles[t], m.x[:, t, :]).then_inc(out_stored, 16)
                sp.wait_ge(out_stored, 16 * NT)

        @block.gpsimd
        def _(pool):
            if first:
                pool.memset(m.ident[:, :], 0.0).then_inc(zeros_ready, 1)
                pool.memset(m.triangle[:, :], 1.0).then_inc(zeros_ready, 1)
                pool.memset(m.resets[:, :, :], 1.0).then_inc(zeros_ready, 1)
                pool.memset(m.zeros[:, :], 0.0).then_inc(zeros_ready, 1)
                pool.wait_ge(zeros_ready, 4)
                pool.affine_select(out=m.ident[:, :], in_=m.ident[:, :], compare_op=ALU.not_equal, fill=1.0,
                                   base=0, pattern=[[-1, P]], channel_multiplier=1).then_inc(consts_ready, 1)
                pool.affine_select(out=m.triangle[:, :], in_=m.triangle[:, :], compare_op=ALU.is_gt, fill=0.0,
                                   base=0, pattern=[[1, P]], channel_multiplier=-1).then_inc(consts_ready, 1)
                pool.memset(m.ones[:, :], 1.0).then_inc(consts_ready, 1)
                pool.memset(m.resets[:, :, 0:1], 0.0).then_inc(consts_ready, 1)
                pool.wait_ge(consts_ready, 1)
                pool.tensor_copy(m.by_expert[:, :].rearrange("p (e c) -> p e c", e=EC),
                                 m.ident[:, :].rearrange("p (c e) -> p e c", e=EC)).then_inc(consts_ready, 1)
            token = facts[:, :, :, NF * EC:]
            pool.iota(token[:, :, :, 0], pattern=[[0, NT], [0, NC]], base=0, channel_multiplier=1,
                      allow_small_or_imprecise_dtypes=True).then_inc(rest_ready, 1)
            pool.iota(token[:, :, :, 1], pattern=[[P, NT], [0, NC]], base=0, channel_multiplier=0,
                      allow_small_or_imprecise_dtypes=True).then_inc(rest_ready, 1)
            pool.memset(token[:, :, :, 2], 1.0).then_inc(rest_ready, 1)

            pool.wait_ge(xn_stored, 16 * NT)
            pool.wait_ge(slots_ready, 2)
            pool.wait_ge(table_zeroed, 16 * NT)

            def gather(n):
                if n >= 2:
                    pool.wait_ge(xgT_psum, n - 1)
                pool.indirect_dma_start(
                    out=xg[:, n % 2, :], out_offset=None, in_=xn_rows,
                    in_offset=bass.IndirectOffsetOnAxis(ap=gather_index[:, n:n + 1], axis=0),
                    bounds_check=T - 1, oob_is_err=False).then_inc(gathered[n % 2], 16)

            gather(0)
            gather(1)
            for n in range(NC):
                if n + 2 < NC:
                    gather(n + 2)
                pool.wait_ge(y_ready, n + 1)
                pool.indirect_dma_start(
                    out=w.table, out_offset=bass.IndirectOffsetOnAxis(ap=scatter_index[:, n:n + 1], axis=0),
                    in_=y[:, n % 2, :], in_offset=None,
                    bounds_check=T * TOPK - 1, oob_is_err=False).then_inc(scattered[n % 2], 16)

        @block.scalar
        def _(act):
            if first:
                act.wait_ge(zeros_ready, 4)
            for t in range(NT):
                act.dma_start(table_tiles[t], m.zeros[:, :].unsqueeze(1).to_broadcast([P, TOPK, DM]))\
                   .then_inc(table_zeroed, 16)
            norm_scalar(act, m, s)
            act.wait_ge(logits_psum, 1)
            act.copy(logits[:, :, 0:E], logits_bank).then_inc(logits_sb, 1)
            act.wait_ge(shifted_ready, 1)
            act.activation(expl[:, :, :], shifted[:, :, :], ACT.Exp).then_inc(expl_ready, 1)
            for k in range(6):
                act.wait_ge(sh_up_psum, k + 1)
                if k >= 2:
                    act.wait_ge(sh_hT_ready, k - 1)
                rows = SH[k % 3]
                act.activation(sh_silu[0:rows, k % 2, :], sh_up_banks[k % 2][0][0:rows, :], ACT.Silu)\
                   .then_inc(sh_silu_ready, 1)

            def gate(n):
                par = n.c % 2
                act.wait_ge(gu_psum, n.times(1, 1))
                wait_count(act, h_ready, n.times(1, -1))
                act.activation(gsilu[:, par, :], gu_banks[par][:, 0:I], ACT.Silu).then_inc(silu_ready, 1)

            def weigh(n):
                par = n.c % 2
                act.wait_ge(y_psum, n.times(1, 1))
                wait_count(act, scattered[par], n.rounds(2, 16))
                act.activation(y[:, par, :], y_banks[par][:, 0:DM], ACT.Copy,
                               scale=slot_weight[:, bass.ds(n.times(1), 1)]).then_inc(y_ready, 1)

            def step(n):
                gate(n)
                if not n.below(1):
                    weigh(n.after(-1))

            for c in range(3):
                step(Chunk(0, 2, c))
            with act.Fori(0, (NC - 4) // 2) as i:
                for c in (3, 4):
                    step(Chunk(i, 2, c))
            step(Chunk(0, 2, NC - 1))
            weigh(Chunk(0, 2, NC - 1))

        @block.vector
        def _(vec):
            vec.memset(logits[:, :, E:E + 2], PAD).then_inc(pads_ready, 1)
            if first:
                vec.memset(m.own_mask[:, :], 0.0).then_inc(mask_ready, 1)
                vec.wait_ge(mask_ready, 1)
                for e in range(EC):
                    vec.memset(m.own_mask[e * CAP:(e + 1) * CAP, e:e + 1], 1.0).then_inc(mask_ready, 1)
                vec.wait_ge(mask_ready, 1 + EC)
                vec.wait_ge(x_loaded, 16 * NT)
            norm_vector(vec, m, s)
            vec.wait_ge(logits_sb, 1)
            vec.wait_ge(pads_ready, 1)
            for t in range(NT):
                vec.max(top[:, t, :], logits[:, t, :]).then_inc(top_ready, 1)
            for t in range(NT):
                vec.wait_ge(top_ready, t + 1)
                vec.match_replace(replaced[:, t, :], top[:, t, :], logits[:, t, :], -PAD).then_inc(replaced_ready, 1)
            vec.wait_ge(replaced_ready, NT)
            vec.tensor_scalar(chosen[:, :, :], replaced[:, :, 0:E], -PAD, None, ALU.is_equal).then_inc(chosen_ready, 1)
            vec.tensor_tensor(shifted[:, :, :], logits[:, :, 0:E], top[:, :, 2:3].to_broadcast([P, NT, E]),
                              ALU.subtract).then_inc(shifted_ready, 1)
            vec.wait_ge(chosen_ready, 1)
            flat_chosen = chosen[:, :, :].rearrange("p t e -> p (t e)")
            vec.tensor_tensor_scan(rank[:, :], m.resets[:, :, :].rearrange("p t e -> p (t e)"), flat_chosen, 0.0,
                                   ALU.mult, ALU.add).then_inc(scan_ready, 1)
            vec.tensor_scalar(unchosen[:, :], flat_chosen, -64.0, 64.0, ALU.mult, ALU.add)\
               .then_inc(unchosen_ready, 1)
            vec.wait_ge(counts_psum, 1)
            vec.wait_ge(unchosen_ready, 1)
            vec.scalar_tensor_tensor(out=place[:, :], in0=counts_bank[:, :], scalar=64.0, in1=unchosen[:, :],
                                     op0=ALU.min, op1=ALU.add).then_inc(place_ready, 1)
            vec.wait_ge(place_ready, 1)
            for c in range(CAP):
                vec.tensor_scalar(onehot[:, :, c, :], place[:, :].rearrange("p (t e) -> p t e", e=E), float(c), None,
                                  ALU.is_equal)\
                   .then_inc(onehot_ready, 1)
            vec.wait_ge(expl_ready, 1)
            vec.tensor_reduce(esum[:, :], expl[:, :, :], AX_X, ALU.add).then_inc(esum_ready, 1)
            vec.wait_ge(esum_ready, 1)
            vec.reciprocal(rsum[:, :], esum[:, :]).then_inc(rsum_ready, 1)
            vec.wait_ge(rsum_ready, 1)
            vec.tensor_tensor(expl[:, :, :], expl[:, :, :], rsum[:, :].unsqueeze(2).to_broadcast([P, NT, E]),
                              ALU.mult).then_inc(probs_ready, 1)
            weight = expl[:, :, :].rearrange("p t (e n) -> p t n e", n=NC)

            vec.wait_ge(scan_ready, 1)
            vec.tensor_tensor(facts[:, :, :, 0:EC], rank[:, :].rearrange("p (t e n) -> p t n e", n=NC, e=EC),
                              chosen[:, :, :].rearrange("p t (e n) -> p t n e", n=NC),
                              ALU.subtract).then_inc(fact_ready, 1)
            for part in range(1, NF):
                vec.wait_ge(probs_ready, 2 * part - 1 if part > 1 else 1)
                f = facts[:, :, :, part * EC:(part + 1) * EC]
                vec.tensor_copy(f, weight).then_inc(fact_ready, 1)
                if part < NF - 1:
                    vec.wait_ge(fact_ready, part + 1)
                    vec.tensor_tensor(weight, weight, f, ALU.subtract).then_inc(probs_ready, 2)
            for bank_of_slots in (slots_bank, counts_bank):
                vec.wait_ge(slots_psum, 1 if bank_of_slots is slots_bank else 2)
                vec.tensor_copy(slot_sums[:, :, :], bank_of_slots[:, 0:NC * RW].rearrange("p (n r) -> p n r", r=RW))\
                   .then_inc(slot_sums_ready, 1)
            vec.wait_ge(slot_sums_ready, 2)
            vec.tensor_tensor(own[:, :, :].rearrange("p n (f e) -> p n f e", e=EC),
                              slot_sums[:, :, 0:NF * EC].rearrange("p n (f e) -> p n f e", e=EC),
                              m.own_mask[:, :].unsqueeze(1).unsqueeze(1).to_broadcast([P, NC, NF, EC]),
                              ALU.mult).then_inc(own_ready, 1)
            vec.wait_ge(own_ready, 1)
            vec.tensor_reduce(own_facts[:, :, :], own[:, :, :].rearrange("p n (f e) -> p n f e", e=EC), AX_X,
                              ALU.add).then_inc(slot_step, 1)
            vec.tensor_reduce(slot_token[:, :], slot_sums[:, :, NF * EC:NF * EC + 2], AX_X, ALU.add)\
               .then_inc(slot_step, 1)
            vec.tensor_scalar(slot_far[:, :], slot_sums[:, :, NF * EC + 2], -FAR, FAR, ALU.mult, ALU.add)\
               .then_inc(slot_step, 1)
            vec.wait_ge(slot_step, 3)
            vec.tensor_reduce(slot_weight[:, :], own_facts[:, :, 1:NF], AX_X, ALU.add).then_inc(slot_step, 1)
            vec.tensor_copy(gather_index[:, :], slot_token[:, :]).then_inc(slots_ready, 1)
            vec.scalar_tensor_tensor(out=slot_row[:, :], in0=slot_token[:, :], scalar=float(TOPK),
                                     in1=own_facts[:, :, 0], op0=ALU.mult, op1=ALU.add).then_inc(slot_step, 1)
            vec.wait_ge(slot_step, 5)
            vec.tensor_tensor(slot_row[:, :], slot_row[:, :], slot_far[:, :], ALU.add).then_inc(slot_step, 1)
            vec.wait_ge(slot_step, 6)
            vec.tensor_copy(scatter_index[:, :], slot_row[:, :]).then_inc(slots_ready, 1)

            for k in range(6):
                rows = SH[k % 3]
                vec.wait_ge(sh_silu_ready, k + 1)
                if k >= 3:
                    vec.wait_ge(sh_y_psum, 4)
                vec.tensor_tensor(sh_hT[0:rows, k % 3, :], sh_up_banks[k % 2][1][0:rows, :],
                                  sh_silu[0:rows, k % 2, :], ALU.mult).then_inc(sh_hT_ready, 1)
                if k % 3 == 2:
                    for t in range(k // 3 * 4, k // 3 * 4 + 4):
                        vec.wait_ge(sh_y_psum, t + 1)
                        vec.scalar_tensor_tensor(out=m.x[:, t, :], in0=sh_y_banks[t % 2][:, 0:DM], scalar=0.5,
                                                 in1=m.x[:, t, :], op0=ALU.mult, op1=ALU.add).then_inc(sh_added, 1)

            def take_rows(n):
                par = n.c % 2
                vec.wait_ge(xgT_psum, n.times(1, 1))
                wait_count(vec, gu_psum, n.times(1, -1))
                vec.tensor_copy(xgT[:, par, :], xgT_banks[par][:, 0:KC * P]).then_inc(xgT_ready, 1)

            def multiply(n):
                par = n.c % 2
                vec.wait_ge(silu_ready, n.times(1, 1))
                wait_count(vec, hT_psum, n.times(1, -1))
                vec.tensor_tensor(h[:, par, :], gu_banks[par][:, I:2 * I], gsilu[:, par, :], ALU.mult)\
                   .then_inc(h_ready, 1)

            def take_hidden(n):
                par = n.c % 2
                vec.wait_ge(hT_psum, n.times(1, 1))
                wait_count(vec, y_psum, n.times(1, -1))
                vec.tensor_copy(hT[:, par, 0:P], hT_banks[par][:, 0:P]).then_inc(hT_ready, 1)
                vec.tensor_copy(hT[0:IHI, par, P:2 * P], hT_banks[par][0:IHI, P:2 * P]).then_inc(hT_ready, 1)

            def step(n):
                multiply(n)
                if n.below(NC - 1) or not isinstance(n.i, int):
                    take_rows(n.after(1))
                take_hidden(n)

            take_rows(Chunk(0, 2, 0))
            for c in range(3):
                step(Chunk(0, 2, c))
            with vec.Fori(0, (NC - 4) // 2) as i:
                for c in (3, 4):
                    step(Chunk(i, 2, c))
            step(Chunk(0, 2, NC - 1))

            vec.wait_ge(sh_added, NT)
            for t in range(NT):
                vec.wait_ge(choices_loaded[t % 4], 16 * (t // 4 + 1))
                if t >= 2:
                    vec.wait_ge(x_ready, t - 1)
                vec.tensor_reduce(total[:, t % 2, :], choice_rows[t % 4].rearrange("p (k d) -> p d k", k=TOPK),
                                  AX_X, ALU.add).then_inc(total_ready, 1)
                vec.wait_ge(total_ready, t + 1)
                vec.scalar_tensor_tensor(out=m.x[:, t, :], in0=total[:, t % 2, :], scalar=0.5, in1=m.x[:, t, :],
                                         op0=ALU.mult, op1=ALU.add).then_inc(x_ready, 1)

        @block.tensor
        def _(pe):
            if first:
                pe.wait_ge(consts_ready, 5)
            norm_tensor(pe, m, s)
            pe.wait_ge(s.xnT_vec, 2)
            pe.wait_ge(s.xnT_act, 2)
            if first:
                pe.wait_ge(small_loaded, 16 * 5)
            for t in range(NT):
                for c in range(KC):
                    ins = pe.matmul(logits_bank[:, t, :], m.xnT[:, c, t * P:t * P + P], m.gate[:, c, :],
                                    start=(c == 0), stop=(c == KC - 1))
            ins.then_inc(logits_psum, 1)

            def shared_up(k):
                half, part = k // 3, k % 3
                cols = slice(part * P, part * P + SH[part])
                if k >= 2:
                    pe.wait_ge(sh_hT_ready, k - 1)
                for weights, to in zip((m.sh_gate, m.sh_up), sh_up_banks[k % 2]):
                    for c in range(KC):
                        ins = pe.matmul(to[0:SH[part], :], weights[:, c, cols],
                                        m.xnT[:, c, half * 512:half * 512 + 512], start=(c == 0), stop=(c == KC - 1))
                ins.then_inc(sh_up_psum, 1)

            def shared_down(half):
                pe.wait_ge(sh_hT_ready, 3 * half + 3)
                for t in range(4 * half, 4 * half + 4):
                    if t >= 2:
                        pe.wait_ge(sh_added, t - 1)
                    for part in range(3):
                        ins = pe.matmul(sh_y_banks[t % 2][:, 0:DM],
                                        sh_hT[0:SH[part], part, (t % 4) * P:(t % 4) * P + P],
                                        m.sh_down[0:SH[part], part, :], start=(part == 0), stop=(part == 2))
                    ins.then_inc(sh_y_psum, 1)

            shared_up(0)
            shared_up(1)
            pe.wait_ge(chosen_ready, 1)
            for t in range(NT):
                to = counts_bank[:, t * E:t * E + E]
                for before in range(t):
                    pe.matmul(to, m.ones[:, :], chosen[:, before, :], start=(before == 0), stop=False)
                ins = pe.matmul(to, m.triangle[:, :], chosen[:, t, :], start=(t == 0), stop=True)
            ins.then_inc(counts_psum, 1)
            pe.wait_ge(onehot_ready, CAP)
            pe.wait_ge(fact_ready, NF)
            pe.wait_ge(rest_ready, 3)
            for n in range(NC):
                for t in range(NT):
                    ins = pe.matmul(slots_bank[:, n * RW:n * RW + RW],
                                    onehot[:, t, :, :].rearrange("p c (e n) -> p n (c e)", n=NC)[:, n, :],
                                    facts[:, t, n, :], start=(t == 0), stop=(t == NT - 1))
            ins.then_inc(slots_psum, 1)
            pe.wait_ge(slot_sums_ready, 1)
            pe.matmul(counts_bank[:, 0:NC * RW], m.by_expert[:, :], slot_sums[:, :, :].rearrange("p n r -> p (n r)"),
                      start=True, stop=True).then_inc(slots_psum, 1)
            shared_up(2)
            pe.wait_ge(logits_sb, 1)
            shared_down(0)
            for k in range(3, 6):
                shared_up(k)
            shared_down(1)
            pe.wait_ge(sh_added, NT)
            pe.wait_ge(slot_sums_ready, 2)

            def rows_in(n):
                par = n.c % 2
                pe.wait_ge(gathered[par], n.rounds(2, 16, 1))
                wait_count(pe, xgT_ready, n.times(1, -1))
                for c in range(KC):
                    ins = pe.transpose(xgT_banks[par][:, c * P:c * P + P], xg[:, par, c * P:c * P + P],
                                       m.ident[:, :])
                ins.then_inc(xgT_psum, 1)

            def up(n):
                par, slot = n.c % 2, n.c % RING
                pe.wait_ge(xgT_ready, n.times(1, 1))
                pe.wait_ge(weights_loaded[slot], n.rounds(RING, 48, 1))
                wait_count(pe, h_ready, n.times(1, -1))
                wgu = m.w_gu[:, slot, :].rearrange("p (e c i) -> p e c i", c=KC, i=2 * I)
                for e in range(EC):
                    rows = slice(e * CAP, (e + 1) * CAP)
                    for c in range(KC):
                        ins = pe.matmul(gu_banks[par][rows, 0:2 * I], xgT[:, par, c * P + e * CAP:c * P + (e + 1) * CAP],
                                        wgu[:, e, c, :], start=(c == 0), stop=(c == KC - 1))
                ins.then_inc(gu_psum, 1)

            def hidden(n):
                par = n.c % 2
                pe.wait_ge(h_ready, n.times(1, 1))
                wait_count(pe, hT_ready, n.times(2, -1))
                pe.transpose(hT_banks[par][:, 0:P], h[:, par, 0:ILO], m.ident[:, :])
                pe.transpose(hT_banks[par][0:IHI, P:2 * P], h[:, par, ILO:I], m.ident[:, :]).then_inc(hT_psum, 1)

            def down(n):
                par, slot = n.c % 2, n.c % RING
                pe.wait_ge(hT_ready, n.times(2, 1))
                wait_count(pe, y_ready, n.times(1, -1))
                for e in range(EC):
                    rows = slice(e * CAP, (e + 1) * CAP)
                    wide = slice(e * DM, (e + 1) * DM)
                    pe.matmul(y_banks[par][rows, 0:DM], hT[:, par, e * CAP:(e + 1) * CAP], m.w_lo[:, slot, wide],
                              start=True, stop=False)
                    ins = pe.matmul(y_banks[par][rows, 0:DM], hT[0:IHI, par, P + e * CAP:P + (e + 1) * CAP],
                                    m.w_hi[:, slot, wide], start=False, stop=True)
                ins.then_inc(y_psum, 1)

            def step(n):
                up(n)
                if not n.below(1):
                    down(n.after(-1))
                if n.below(NC - 1) or not isinstance(n.i, int):
                    rows_in(n.after(1))
                hidden(n)

            rows_in(Chunk(0, RING, 0))
            for c in range(3):
                step(Chunk(0, RING, c))
            with pe.Fori(0, (NC - 4) // RING) as i:
                for c in range(3, RING + 3):
                    step(Chunk(i, RING, c))
            step(Chunk(0, RING, NC - 1))
            down(Chunk(0, RING, NC - 1))


def attention(nc, w, m, used, next_weights_loaded):
    with ExitStack() as ctx:
        def sb(name, shape, dt=F32):
            return ctx.enter_context(nc.sbuf_tensor(f"at_{name}", shape, dt))

        def sem(name):
            return ctx.enter_context(nc.semaphore(f"at_{name}"))

        w_qkv = sb("w_qkv", [P, KC, 3 * DM])
        w_o = sb("w_o", [P, KC, DM])
        rope_cos = sb("rope_cos", [P, 2, 2, HD])
        rope_sin = sb("rope_sin", [P, 2, 2, HD])
        by_cos = sb("by_cos", [P, 2, 2 * DM])
        by_sin = sb("by_sin", [P, 2, 2 * DM])
        qk = sb("qk", [P, NT, 2, DM])
        v = sb("v", [P, NT, NH, HD + 1])
        bias_rows = sb("bias_rows", [NH, MAXB + S])
        bias = sb("bias", [P, 8, S])
        offset = sb("offset", [P, NH])
        neg_offset_all = sb("neg_offset_all", [P, NH])
        neg_offset = sb("neg_offset", [P, 8])
        qk_pad = sb("qk_pad", [P, 2, 2, 2, 4, 32])
        v_quad = sb("v_quad", [P, 2, 2, 4 * (HD + 1)])
        qkT = sb("qkT", [P, 2, 2, 2, P])
        neg_scores = sb("neg_scores", [P, 4, P + S])
        neg_max = sb("neg_max", [P, 8, 2])
        probs = sb("probs", [P, 4, P + S])
        probsT = sb("probsT", [P, 4, P + S])
        off_shift = sb("off_shift", [P, 2, 2, 4])
        off_exp = sb("off_exp", [P, 2, 2, 4])
        denom = sb("denom", [P, 2, 4])
        rdenom = sb("rdenom", [P, 2, 4])
        heads_out = sb("heads_out", [P, 2, 2, 4 * HD])
        attn = sb("attn", [P, NT, DM])
        attnT = m.xnT

        s = NormSems(sem)
        (small_loaded, rows_zeroed, rows_masked, rows_loaded, rows_stored, bias_loaded, pad_ready, neg_off_ready,
         neg_off_staged, ones_ready, qkv_psum, cos_done, sin_done, qk_ready, v_ready, staged, qkT_psum, qkT_ready,
         s_psum, scored, exp_done, pT_psum, pT_ready, pv_psum, off_in, off_ready, den_ready, rden_ready,
         quad_out, attn_stored, attnT_psum, attnT_vec, attnT_act, o_psum, x_ready) = [sem(n) for n in (
             "small_loaded rows_zeroed rows_masked rows_loaded rows_stored bias_loaded pad_ready neg_off_ready "
             "neg_off_staged ones_ready qkv_psum cos_done sin_done qk_ready v_ready staged qkT_psum qkT_ready "
             "s_psum scored exp_done pT_psum pT_ready pv_psum off_in off_ready den_ready rden_ready "
             "quad_out attn_stored attnT_psum attnT_vec attnT_act o_psum x_ready").split()]
        bank = m.bank
        score_banks, turn_banks, pv_banks = bank[0:4], bank[4:6], bank[6:8]

        block = ctx.enter_context(nc.Block())

        @block.sync
        def _(sp):
            sp.dma_start(w_qkv[:, :, :], w.w_qkv.rearrange("(c p) n -> p c n", p=P)).then_inc(small_loaded, 16)
            sp.dma_start(w_o[:, :, :], w.w_o.rearrange("(c p) n -> p c n", p=P)).then_inc(small_loaded, 16)
            sp.dma_start(rope_cos[:, :, :, :].rearrange("p t q c -> p (t q c)"), w.rope_cos).then_inc(small_loaded, 16)
            sp.dma_start(rope_sin[:, :, :, :].rearrange("p t q c -> p (t q c)"), w.rope_sin).then_inc(small_loaded, 16)
            sp.dma_start(offset[:, :], w.offset.partition_broadcast(P)).then_inc(small_loaded, 16)
            sp.wait_ge(rows_masked, 2)
            sp.dma_start(bias_rows[:, P:2 * P], w.bias_reversed).then_inc(rows_loaded, 16)
            sp.wait_ge(rows_loaded, 16)
            sp.dma_start(w.bias_dram.rearrange("p h r -> h p r"),
                         bias_rows[:, :].unsqueeze(1).to_broadcast([NH, P, 3 * P])).then_inc(rows_stored, 16)
            sp.wait_ge(rows_stored, 16)
            first_chunks(sp, w, m, next_weights_loaded)
            for o in range(NH // 8):
                wait_count(sp, scored, o * B * 8 * 2)
                skewed = bass.AP(w.bias_dram.tensor, o * 8 * 3 * P + P - 1, [[NH * 3 * P - 1, P], [3 * P, 8], [1, S]])
                sp.dma_start(bias[:, :, :], skewed).then_inc(bias_loaded, 16)

        @block.gpsimd
        def _(pool):
            pool.sem_clear(range(min(used), max(used) + 1))
            pool.memset(bias_rows[:, 0:P], 0.0).then_inc(rows_masked, 1)
            pool.memset(bias_rows[:, 2 * P:3 * P], MASKED).then_inc(rows_masked, 1)
            pool.memset(qk_pad[:, :, :, :, :, :], 0.0).then_inc(pad_ready, 1)
            pool.memset(v[:, :, :, HD:HD + 1], 1.0).then_inc(ones_ready, 1)
            pool.memset(heads_out[:, :, :, :], 0.0).then_inc(attn_stored, 1)
            for t in range(NT):
                pool.wait_ge(cos_done, t + 1)
                pool.wait_ge(sin_done, 2 * t + 2)
                pool.tensor_tensor(qk[:, t, :, :].rearrange("p q n -> p (q n)"), by_cos[:, t % 2, :],
                                   by_sin[:, t % 2, :], ALU.add).then_inc(qk_ready, 1)
            pool.wait_ge(qk_ready, NT)
            pool.wait_ge(v_ready, NT)
            pool.wait_ge(neg_off_ready, 1)
            pool.wait_ge(pad_ready, 1)
            pool.wait_ge(ones_ready, 1)

            def stage(o, b, q2, quad, known):
                if known is None or known >= 2:
                    pool.wait_ge(qkT_psum, quad - 1)
                    pool.wait_ge(pv_psum, quad * 4 - 4)
                for tile in range(2):
                    src = qk[:, bass.ds(b * 2 + tile, 1), :, bass.ds(o * 64 + q2 * 32, 32)]\
                        .rearrange("p a q (g d) -> p (a q) g d", g=4)
                    pool.tensor_copy(qk_pad[:, q2, tile, :, :, 0:HD], src).then_inc(staged, 1)
                src = v[:, bass.ds(b * 2, 2), bass.ds(o * 8 + q2 * 4, 4), :].rearrange("p t g d -> p t (g d)")
                pool.tensor_copy(v_quad[:, q2, :, :], src).then_inc(staged, 1)

            def store(o, b, q2, quad):
                pool.wait_ge(quad_out, quad + 1)
                pool.tensor_copy(attn[:, bass.ds(b * 2, 2), bass.ds(o * 64 + q2 * 32, 32)],
                                 heads_out[:, q2, :, :]).then_inc(attn_stored, 1)

            def next_offsets(o, known):
                if known is None:
                    pool.wait_ge(off_in, o * 8)
                    pool.wait_ge(scored, o * (4 * 8 * 2))
                pool.wait_ge(bias_loaded, o * 16 + 16)
                pool.tensor_copy(neg_offset[:, :], neg_offset_all[:, bass.ds(o * 8, 8)]).then_inc(neg_off_staged, 1)
                pool.wait_ge(neg_off_staged, o + 1)

            next_offsets(0, 0)
            for b in range(B):
                for q2 in range(2):
                    quad = 2 * b + q2
                    stage(0, b, q2, quad, quad)
                    if quad >= 2:
                        store(0, b - 1, q2, quad - 2)
            with pool.Fori(1, NH // 8) as o:
                next_offsets(o, None)
                for b in range(B):
                    for q2 in range(2):
                        quad = o * 8 + (2 * b + q2)
                        stage(o, b, q2, quad, None)
                        if b == 0:
                            store(o - 1, B - 1, q2, quad - 2)
                        if b > 0:
                            store(o, b - 1, q2, quad - 2)
            for q2 in range(2):
                store(NH // 8 - 1, B - 1, q2, NQUAD - 2 + q2)

        def by_slots(eng, slot):
            for k in range(8):
                slot(0, k)
            with eng.Fori(1, NQUAD // 2) as i:
                for k in range(8):
                    slot(i, k)

        def head(i, k):
            return i * 8 + k

        def exists(i, k):
            return not isinstance(i, int) or i * 8 + k >= 0

        @block.scalar
        def _(act):
            norm_scalar(act, m, s)
            for t in range(NT):
                act.wait_ge(qkv_psum, t + 1)
                act.copy(v[:, t, :, 0:HD], bank[6 + t % 2][:, 0:DM].rearrange("p (h d) -> p h d", d=HD))\
                   .then_inc(v_ready, 1)

            def take_qkT(i, q2):
                act.wait_ge(qkT_psum, i * 2 + q2 + 1)
                wait_count(act, s_psum, i * 8 + 4 * (q2 - 1))
                act.copy(qkT[:, q2, :, :, :].rearrange("p t q n -> p (t q n)"), turn_banks[QK_TURN][:, :])\
                   .then_inc(qkT_ready, 1)

            def take_off(i, q2):
                act.wait_ge(off_in, i * 2 + q2 + 1)
                act.activation(off_exp[:, q2, :, :], off_shift[:, q2, :, :], ACT.Exp).then_inc(off_ready, 1)

            def slot(i, k):
                if k in (0, 4) and exists(i, k - 4):
                    take_off(i if k else i - 1, 0 if k else 1)
                if k == 0:
                    take_qkT(i, 0)
                if k == 3:
                    take_qkT(i, 1)
                act.wait_ge(scored, head(i, k) * 2 + 2)
                wait_count(act, pT_psum, head(i, k) - 3)
                act.activation(probs[:, k % 4, 0:P], neg_scores[:, k % 4, 0:P], ACT.Exp,
                               bias=neg_max[:, k, 0:1], scale=-1.0).then_inc(exp_done, 1)
                act.activation(probs[:, k % 4, P:P + S], neg_scores[:, k % 4, P:P + S], ACT.Exp,
                               bias=neg_max[:, k, 1:2], scale=-1.0).then_inc(exp_done, 1)

            by_slots(act, slot)
            take_off(NQUAD // 2 - 1, 1)
            for half in range(2):
                act.wait_ge(attnT_psum, 2 * half + 1)
                act.copy(attnT[:, 0, half * 512:half * 512 + 512], bank[2 * half][:, :]).then_inc(attnT_act, 1)

        @block.vector
        def _(vec):
            norm_vector(vec, m, s)
            vec.wait_ge(small_loaded, 16 * 5)
            vec.tensor_scalar(neg_offset_all[:, :], offset[:, :], -1.0, None, ALU.mult).then_inc(neg_off_ready, 1)
            for t in range(NT):
                vec.wait_ge(qkv_psum, t + 1)
                if t >= 2:
                    vec.wait_ge(qk_ready, t - 1)
                src = bank[4 + t % 2][:, :].rearrange("p (q h d) -> p q h d", q=2, d=HD)
                cos = rope_cos[:, t % 2, :, :].unsqueeze(2)
                sin = rope_sin[:, t % 2, :, :].unsqueeze(2)
                to_cos = by_cos[:, t % 2, :].rearrange("p (q h d) -> p q h d", q=2, d=HD)
                to_sin = by_sin[:, t % 2, :].rearrange("p (q h d) -> p q h d", q=2, d=HD)
                half = HD // 2
                vec.tensor_tensor(to_sin[:, :, :, 0:half], src[:, :, :, half:HD],
                                  sin[:, :, :, 0:half].to_broadcast([P, 2, NH, half]), ALU.mult).then_inc(sin_done, 1)
                vec.tensor_tensor(to_sin[:, :, :, half:HD], src[:, :, :, 0:half],
                                  sin[:, :, :, half:HD].to_broadcast([P, 2, NH, half]), ALU.mult).then_inc(sin_done, 1)
                vec.tensor_tensor(to_cos, src, cos.to_broadcast([P, 2, NH, HD]), ALU.mult).then_inc(cos_done, 1)

            def take_probsT(i, k):
                turn = PROBS_TURN[k % 8]
                vec.wait_ge(pT_psum, head(i, k) + 1)
                wait_count(vec, pv_psum, head(i, k) - 3)
                vec.tensor_copy(probsT[:, k % 4, :], turn_banks[turn][:, 0:P + S]).then_inc(pT_ready, 1)

            def finish_quad(i, q2):
                quad = i * 2 + q2
                sums = pv_banks[q2][:, 0:2 * 4 * (HD + 1)].rearrange("p (t g d) -> p t g d", t=2, g=4)
                vec.wait_ge(pv_psum, quad * 4 + 4)
                vec.wait_ge(off_ready, quad + 1)
                vec.tensor_tensor(denom[:, :, :], sums[:, :, :, HD], off_exp[:, q2, :, :], ALU.add)\
                   .then_inc(den_ready, 1)
                vec.wait_ge(den_ready, quad + 1)
                vec.reciprocal(rdenom[:, :, :], denom[:, :, :]).then_inc(rden_ready, 1)
                vec.wait_ge(rden_ready, quad + 1)
                vec.wait_ge(attn_stored, quad if not isinstance(quad, int) or quad > 0 else 1)
                vec.tensor_tensor(heads_out[:, q2, :, :].rearrange("p t (g d) -> p t g d", d=HD),
                                  sums[:, :, :, 0:HD],
                                  rdenom[:, :, :].unsqueeze(3).to_broadcast([P, 2, 4, HD]),
                                  ALU.mult).then_inc(quad_out, 1)

            def slot(i, k):
                due, free = head(i, k) + 1, head(i, k) * 2 - 6
                if not isinstance(i, int):
                    due, free = vec.to_reg(due), vec.to_reg(free)
                vec.wait_ge(bias_loaded, 16)
                vec.wait_ge(s_psum, due)
                wait_count(vec, exp_done, free)
                scores = score_banks[k % 4]
                vec.tensor_tensor_reduce(neg_scores[:, k % 4, 0:P], scores[:, 0:P], bias[:, k, P:2 * P], -1.0,
                                         neg_offset[:, k:k + 1], ALU.add, ALU.min, neg_max[:, k, 0:1])\
                   .then_inc(scored, 1)
                vec.tensor_tensor_reduce(neg_scores[:, k % 4, P:P + S], scores[:, P:P + S], bias[:, k, :], -1.0,
                                         neg_offset[:, k:k + 1], ALU.add, ALU.min, neg_max[:, k, 1:2])\
                   .then_inc(scored, 1)
                if exists(i, k - 2):
                    take_probsT(i, k - 2)
                if k in (3, 7):
                    q2 = k // 4
                    vec.wait_ge(scored, head(i, k) * 2 + 2)
                    wait_count(vec, off_ready, i * 2 + q2 - 1)
                    vec.tensor_tensor(off_shift[:, q2, :, :],
                                      neg_max[:, 4 * q2:4 * q2 + 4, :].rearrange("p g t -> p t g"),
                                      neg_offset[:, 4 * q2:4 * q2 + 4].unsqueeze(1).to_broadcast([P, 2, 4]),
                                      ALU.subtract).then_inc(off_in, 1)
                if k == 3 and exists(i, -1):
                    finish_quad(i - 1, 1)
                if k == 7:
                    finish_quad(i, 0)

            by_slots(vec, slot)
            take_probsT(NQUAD // 2, -2)
            take_probsT(NQUAD // 2, -1)
            finish_quad(NQUAD // 2 - 1, 1)
            for half in range(2):
                vec.wait_ge(attnT_psum, 2 * half + 2)
                vec.tensor_copy(attnT[:, 1, half * 512:half * 512 + 512], bank[2 * half + 1][:, :])\
                   .then_inc(attnT_vec, 1)
            for t in range(NT):
                vec.wait_ge(o_psum, t + 1)
                vec.tensor_tensor(m.x[:, t, :], bank[4 + t % 2][:, 0:DM], m.x[:, t, :], ALU.add).then_inc(x_ready, 1)

        @block.tensor
        def _(pe):
            norm_tensor(pe, m, s)
            pe.wait_ge(s.xnT_vec, 2)
            pe.wait_ge(s.xnT_act, 2)
            pe.wait_ge(small_loaded, 16 * 5)
            for t in range(NT):
                if t >= 2:
                    pe.wait_ge(cos_done, t - 1)
                    pe.wait_ge(v_ready, t - 1)
                rows = slice(t * P, t * P + P)
                for c in range(KC):
                    pe.matmul(bank[4 + t % 2][:, :], m.xnT[:, c, rows], w_qkv[:, c, 0:2 * DM],
                              start=(c == 0), stop=(c == KC - 1))
                for c in range(KC):
                    ins = pe.matmul(bank[6 + t % 2][:, 0:DM], m.xnT[:, c, rows], w_qkv[:, c, 2 * DM:3 * DM],
                                    start=(c == 0), stop=(c == KC - 1))
                ins.then_inc(qkv_psum, 1)
            pe.wait_ge(cos_done, NT)
            pe.wait_ge(v_ready, NT)

            def turn_heads(i, q2):
                pe.wait_ge(staged, i * 6 + 3 * q2 + 3)
                if exists(i, -1):
                    pe.wait_ge(pT_ready, head(i, -4 if q2 == 0 else -1) + 1)
                for tile in range(2):
                    for which in range(2):
                        at = (2 * tile + which) * P
                        ins = pe.transpose(turn_banks[QK_TURN][:, at:at + P],
                                           qk_pad[:, q2, tile, which, :, :].rearrange("p g r -> p (g r)"),
                                           m.ident[:, :])
                ins.then_inc(qkT_psum, 1)

            def score(i, k):
                q2, g = k // 4, k % 4
                rows = slice(32 * g, 32 * g + HD)
                if g == 0:
                    pe.wait_ge(qkT_ready, i * 2 + q2 + 1)
                wait_count(pe, scored, head(i, k) * 2 - 6)
                keys = qkT[rows, q2, :, 1, :]
                pe.matmul(score_banks[g][:, 0:P], qkT[rows, q2, 0, 0, :], qkT[rows, q2, 0, 1, :],
                          start=True, stop=True)
                pe.matmul(score_banks[g][:, P:P + S], qkT[rows, q2, 1, 0, :], keys, start=True, stop=True)\
                  .then_inc(s_psum, 1)

            def turn_probs(i, k, ends=False):
                turn = PROBS_TURN[k % 8]
                pe.wait_ge(exp_done, head(i, k) * 2 + 2)
                if ends:
                    pe.wait_ge(pT_ready, head(i, k) - 2)
                elif k % 8 == 7:
                    pe.wait_ge(qkT_ready, (i + k // 8) * 2 + 3)
                elif k % 8 == 2:
                    pe.wait_ge(qkT_ready, i * 2 + 2)
                elif k % 8 in (1, 6):
                    pe.wait_ge(pT_ready, head(i, k))
                else:
                    wait_count(pe, pT_ready, head(i, k) - 1)
                for j in range(3):
                    ins = pe.transpose(turn_banks[turn][:, j * P:j * P + P], probs[:, k % 4, j * P:j * P + P],
                                       m.ident[:, :])
                ins.then_inc(pT_psum, 1)

            def weigh_values(i, k):
                q2, g = k % 8 // 4, k % 4
                to = pv_banks[q2][:, 0:2 * 4 * (HD + 1)].rearrange("p (t g d) -> p t g d", t=2, g=4)
                vals = v_quad[:, q2, :, :].rearrange("p t (g d) -> p t g d", g=4)
                pe.wait_ge(pT_ready, head(i, k) + 1)
                if g == 0:
                    wait_count(pe, quad_out, i * 2 + k // 4 - 1)
                pe.matmul(to[:, 0, g, :], probsT[:, k % 4, 0:P], vals[:, 0, g, :], start=True, stop=True)
                pe.matmul(to[:, 1, g, :], probsT[:, k % 4, P:2 * P], vals[:, 0, g, :], start=True, stop=False)
                ins = pe.matmul(to[:, 1, g, :], probsT[:, k % 4, 2 * P:3 * P], vals[:, 1, g, :],
                                start=False, stop=True)
                ins.then_inc(pv_psum, 1)

            def slot(i, k):
                if k == 0:
                    turn_heads(i, 0)
                if exists(i, k - 2):
                    turn_probs(i, k - 2)
                if exists(i, k - 3):
                    weigh_values(i, k - 3)
                if k == 2:
                    turn_heads(i, 1)
                score(i, k)

            by_slots(pe, slot)
            last = NQUAD // 2
            turn_probs(last, -2)
            weigh_values(last, -3)
            turn_probs(last, -1, ends=True)
            weigh_values(last, -2)
            weigh_values(last, -1)
            pe.wait_ge(attn_stored, NQUAD + 1)
            for half in range(2):
                for q in range(4):
                    for c in range(KC):
                        ins = pe.transpose(bank[2 * half + c][:, q * P:q * P + P],
                                           attn[:, 4 * half + q, c * P:c * P + P], m.ident[:, :])
                        if q == 3:
                            ins.then_inc(attnT_psum, 1)
            pe.wait_ge(attnT_vec, 2)
            pe.wait_ge(attnT_act, 2)
            for t in range(NT):
                if t >= 2:
                    pe.wait_ge(x_ready, t - 1)
                for c in range(KC):
                    ins = pe.matmul(bank[4 + t % 2][:, 0:DM], attnT[:, c, t * P:t * P + P], w_o[:, c, :],
                                    start=(c == 0), stop=(c == KC - 1))
                ins.then_inc(o_psum, 1)


class OnChip:

    def __init__(self, sb, bank):
        self.bank = bank
        self.x = sb("x", [P, NT, DM])
        self.xn = sb("xn", [P, NT, DM])
        self.xnT = sb("xnT", [P, KC, T])
        self.stats = sb("stats", [P, NT, 6])
        self.moments = sb("moments", [P, NT, 2])
        self.var_eps = sb("var_eps", [P, NT])
        self.std = sb("std", [P, NT])
        self.rstd = sb("rstd", [P, NT])
        self.gate = sb("gate", [P, KC, E])
        self.sh_gate = sb("sh_gate", [P, KC, IS])
        self.sh_up = sb("sh_up", [P, KC, IS])
        self.sh_down = sb("sh_down", [P, 3, DM])
        self.w_gu = sb("w_gu", [P, RING, EC * KC * 2 * I])
        self.w_lo = sb("w_lo", [ILO, RING, EC * DM])
        self.w_hi = sb("w_hi", [IHI, RING, EC * DM])
        self.ident = sb("ident", [P, P])
        self.by_expert = sb("by_expert", [P, P])
        self.triangle = sb("triangle", [P, P], BF16)
        self.ones = sb("ones", [P, P], BF16)
        self.resets = sb("resets", [P, NT, E])
        self.own_mask = sb("own_mask", [P, EC])
        self.zeros = sb("zeros", [P, DM])


class Dram:

    def __init__(self, nc, given, out):
        self.x = given["x"]
        self.gate_t = given["gate_t"]
        self.w_gu, self.w_lo, self.w_hi = given["w_gu"], given["w_lo"], given["w_hi"]
        self.sw_gate, self.sw_up, self.sw_down = given["sw_gate"], given["sw_up"], given["sw_down"]
        self.w_qkv, self.w_o = given["w_qkv"], given["w_o"]
        self.bias_reversed, self.offset = given["bias_reversed"], given["offset"]
        self.rope_cos, self.rope_sin = given["rope_cos"], given["rope_sin"]
        self.out = out
        self.xn_dram = nc.dram_tensor("xn_rows", [T, DM], F32).ap()
        self.table = nc.dram_tensor("choice_table", [T * TOPK, DM], F32).ap()
        self.bias_dram = nc.dram_tensor("bias_rows_dram", [P, NH, 3 * P], F32).ap()


def build(nc, given, out):
    w = Dram(nc, given, out)
    with ExitStack() as ctx:
        def sb(name, shape, dt=F32):
            return ctx.enter_context(nc.sbuf_tensor(name, shape, dt))

        m = OnChip(sb, [ctx.enter_context(nc.psum_tensor(f"bank{i}", [P, 512], F32)) for i in range(8)])
        loaded = [[ctx.enter_context(nc.semaphore(f"ff{f}_weights{i}")) for i in range(RING)] for f in range(2)]
        gathered, scattered = ([[ctx.enter_context(nc.semaphore(f"ff{f}_{name}{i}")) for i in range(2)]
                                for f in range(2)] for name in ("gathered", "scattered"))
        ff_sems = {}

        def ff_sem(name):
            if name not in ff_sems:
                ff_sems[name] = ctx.enter_context(nc.semaphore(f"ff_{name}"))
            return ff_sems[name]

        feed_forward(nc, w, m, ff_sem, "ff0", loaded[0], gathered[0], scattered[0], True, False)
        attention(nc, w, m, [x.num for x in ff_sems.values()], loaded[1])
        feed_forward(nc, w, m, ff_sem, "ff1", loaded[1], gathered[1], scattered[1], False, True)


def rope_tables():
    half = HD // 2
    freq = 1.0 / 10000.0 ** (np.arange(half, dtype=np.float32) / np.float32(half))
    angle = np.outer(np.arange(S, dtype=np.float32), freq.astype(np.float32)).astype(np.float32)
    cos = np.concatenate([np.cos(angle), np.cos(angle)], axis=1)
    sin = np.concatenate([-np.sin(angle), np.sin(angle)], axis=1)
    scale = np.array([HD ** -0.5, 1.0], dtype=np.float32)

    def lay(table):
        table = table.astype(np.float32).reshape(2, P, 1, HD) * scale.reshape(1, 1, 2, 1)
        return np.ascontiguousarray(table.transpose(1, 0, 2, 3).reshape(P, 4 * HD).astype(np.float32))

    return lay(cos), lay(sin)


def kernel(**inputs):
    import concourse.bacc as bacc
    from concourse.bass_utils import run_bass_kernel_spmd

    a = {k: np.asarray(v) for k, v in inputs.items()}
    w_gu = np.concatenate([a["L0_ffn_w_gate"], a["L0_ffn_w_up"]], axis=2)
    w_gu = w_gu.reshape(EC, NC, KC, P, 2 * I).transpose(1, 3, 0, 2, 4).reshape(NC, P, EC * KC * 2 * I)
    w_dn = a["L0_ffn_w_down"].reshape(EC, NC, I, DM).transpose(1, 2, 0, 3).reshape(NC, I, EC * DM)
    rope_cos, rope_sin = rope_tables()
    laid = {
        "x": a["L0_attn_hidden_states"].reshape(T, DM),
        "gate_t": a["L0_ffn_gate_w"].T,
        "w_gu": w_gu, "w_lo": w_dn[:, :ILO], "w_hi": w_dn[:, ILO:],
        "sw_gate": a["L0_ffn_sw_gate"], "sw_up": a["L0_ffn_sw_up"], "sw_down": a["L0_ffn_sw_down"],
        "w_qkv": np.concatenate([a["L0_attn_Wq"].T, a["L0_attn_Wk"].T, a["L0_attn_Wv"].T], axis=1),
        "w_o": a["L0_attn_Wo"].T,
        "bias_reversed": a["L0_attn_learnable_bias"][:, ::-1],
        "offset": a["L0_attn_softmax_offset"],
        "rope_cos": rope_cos, "rope_sin": rope_sin,
    }
    nc = bacc.Bacc("TRN2", target_bir_lowering=False, num_devices=1)
    arrays, given = {}, {}
    for name, value in laid.items():
        value = np.ascontiguousarray(value)
        arrays[f"in_{name}"] = value
        given[name] = nc.dram_tensor(f"in_{name}", value.shape, mybir.dt.from_np(value.dtype),
                                     kind="ExternalInput").ap()
    build(nc, given, nc.dram_tensor("out_x", [B, S, DM], F32, kind="ExternalOutput").ap())
    r = run_bass_kernel_spmd(nc, [arrays], core_ids=[0])
    return r.results[0]["out_x"]
```

```python
from contextlib import ExitStack

import numpy as np
import concourse.bass as bass
from concourse import mybir

F32 = mybir.dt.float32
BF16 = mybir.dt.bfloat16
U32 = mybir.dt.uint32
ALU = mybir.AluOpType
ACT = mybir.ActivationFunctionType
AX_X = mybir.AxisListType.X

P = 128
B, S, DM = 4, 256, 256
T = B * S
NT = T // P
KC = DM // P
NH, HD = 32, 8
MAXB = 128
E, TOPK, I = 64, 6, 176
CAP = 32
IS = 2 * I
EC = P // CAP
NC = E // EC
KEPT = 4
RING = 6
AHEAD = 3
ILO, IHI = P, I - P
EPS = 1e-5
PAD = 3.0e38
MASKED = -1.0e30
FAR = 100000.0
NF = 4
RW = NF * EC + 3
NQUAD = T // S * NH // 4
SH = [P, P, IS - 2 * P]


class Chunk:

    def __init__(self, i, scale, c):
        self.i, self.scale, self.c = i, scale, c

    def times(self, k, plus=0):
        return self.i * (self.scale * k) + k * (self.c + plus)

    def rounds(self, of, k, plus=0):
        return self.i * (self.scale // of * k) + k * (self.c // of + plus)

    def after(self, k):
        return Chunk(self.i, self.scale, self.c + k)

    def below(self, k):
        return isinstance(self.i, int) and self.c < k


def wait_count(eng, sem, value):
    if isinstance(value, int) and value <= 0:
        return
    eng.wait_ge(sem, value)


def norm_vector(vec, m, s):
    for t in range(NT):
        vec.bn_stats(m.stats[:, t, :], m.x[:, t, :]).then_inc(s.stats_done, 1)
    for t in range(NT):
        vec.wait_ge(s.stats_done, t + 1)
        vec.bn_aggr(m.moments[:, t, :], m.stats[:, t, :]).then_inc(s.moments_done, 1)
    vec.wait_ge(s.moments_done, NT)
    vec.tensor_scalar(m.var_eps[:, :], m.moments[:, :, 1], EPS, None, ALU.add).then_inc(s.var_ready, 1)
    vec.wait_ge(s.std_ready, 1)
    vec.reciprocal(m.rstd[:, :], m.std[:, :]).then_inc(s.rstd_ready, 1)
    vec.wait_ge(s.rstd_ready, 1)
    for t in range(NT):
        vec.tensor_scalar(m.xn[:, t, :], m.x[:, t, :], m.moments[:, t, 0:1], m.rstd[:, t:t + 1],
                          ALU.subtract, ALU.mult).then_inc(s.xn_ready, 1)
    for half in range(2):
        vec.wait_ge(s.xnT_psum, 2 * half + 2)
        vec.tensor_copy(m.xnT[:, 1, half * 512:half * 512 + 512], m.bank[2 * half + 1][:, :]).then_inc(s.xnT_vec, 1)


def norm_scalar(act, m, s):
    act.wait_ge(s.var_ready, 1)
    act.activation(m.std[:, :], m.var_eps[:, :], ACT.Sqrt).then_inc(s.std_ready, 1)
    for half in range(2):
        act.wait_ge(s.xnT_psum, 2 * half + 1)
        act.copy(m.xnT[:, 0, half * 512:half * 512 + 512], m.bank[2 * half][:, :]).then_inc(s.xnT_act, 1)


def norm_tensor(pe, m, s):
    for half in range(2):
        for q in range(4):
            t = 4 * half + q
            pe.wait_ge(s.xn_ready, t + 1)
            for c in range(KC):
                ins = pe.transpose(m.bank[2 * half + c][:, q * P:q * P + P],
                                   m.xn[:, t, c * P:c * P + P], m.ident[:, :])
                if q == 3:
                    ins.then_inc(s.xnT_psum, 1)


class NormSems:

    def __init__(self, sem):
        self.stats_done = sem("stats_done")
        self.moments_done = sem("moments_done")
        self.var_ready = sem("var_ready")
        self.std_ready = sem("std_ready")
        self.rstd_ready = sem("rstd_ready")
        self.xn_ready = sem("xn_ready")
        self.xnT_psum = sem("xnT_psum")
        self.xnT_vec = sem("xnT_vec")
        self.xnT_act = sem("xnT_act")


def load_expert_chunk(sp, w, slot, loaded, n):
    chunk = slice(n, n + 1)
    sp.dma_start(slot.gu, w.w_gu[chunk].squeeze(0)).then_inc(loaded, 16)
    sp.dma_start(slot.lo, w.w_lo[chunk].squeeze(0)).then_inc(loaded, 16)
    sp.dma_start(slot.hi, w.w_hi[chunk].squeeze(0)).then_inc(loaded, 16)


def first_chunks(sp, w, m, loaded):
    for n in range(KEPT):
        load_expert_chunk(sp, w, m.slots[n], loaded[n], n)


def feed_forward(nc, w, m, sems, tag, weights_loaded, gathered, scattered, first, last):
    with ExitStack() as ctx:
        def sb(name, shape, dt=F32):
            return ctx.enter_context(nc.sbuf_tensor(f"{tag}_{name}", shape, dt))

        def sem(name):
            return sems(name)

        onehot = sb("onehot", [P, NT, CAP, E], BF16)
        flat_onehot = onehot[:, :, :, :].rearrange("p t c e -> p (t c e)").bitcast(F32)
        width, down_width = EC * KC * 2 * I, EC * DM
        slots = m.slots + [
            WeightSlot(sb("w_gu4", [P, width]), sb("w_lo4", [ILO, down_width]), sb("w_hi4", [IHI, down_width])),
            WeightSlot(flat_onehot[:, 0:width], flat_onehot[:, width:width + down_width],
                       flat_onehot[0:IHI, width + down_width:width + 2 * down_width])]
        choice_rows = [flat_onehot[:, i * TOPK * DM:(i + 1) * TOPK * DM] for i in range(4)]
        facts = sb("facts", [P, NT, NC, RW], BF16)
        logits = sb("logits", [P, NT, E + 2])
        replaced = sb("replaced", [P, NT, E + 2])
        top = sb("top", [P, NT, 8])
        chosen = sb("chosen", [P, NT, E], BF16)
        shifted = sb("shifted", [P, NT, E])
        expl = sb("expl", [P, NT, E])
        esum = sb("esum", [P, NT])
        rsum = sb("rsum", [P, NT])
        rank = sb("rank", [P, NT * E])
        unchosen = sb("unchosen", [P, NT * E])
        place = sb("place", [P, NT * E], BF16)
        slot_sums = sb("slot_sums", [P, NC, RW])
        own = sb("own", [P, NC, NF * EC])
        own_facts = sb("own_facts", [P, NC, NF])
        slot_weight = sb("slot_weight", [P, NC])
        slot_token = sb("slot_token", [P, NC])
        slot_far = sb("slot_far", [P, NC])
        slot_row = sb("slot_row", [P, NC])
        gather_index = sb("gather_index", [P, NC], U32)
        scatter_index = sb("scatter_index", [P, NC], U32)
        sh_silu = sb("sh_silu", [P, 2, 512])
        sh_hT = sb("sh_hT", [P, 3, 512])
        xg = [rank[:, 0:DM], rank[:, DM:2 * DM], unchosen[:, 0:DM]]
        xgT = sb("xgT", [P, 2, KC * P])
        gsilu = sb("gsilu", [P, 2, I])
        h = sb("h", [P, 2, I])
        hT = sb("hT", [P, 2, 2 * P])
        y = sb("y", [P, 2, DM])
        total = y

        s = NormSems(sem)
        (x_loaded, small_loaded, consts_ready, table_zeroed, zeros_ready, pads_ready, xn_stored, logits_psum,
         logits_sb, top_ready, replaced_ready, chosen_ready, shifted_ready, expl_ready, esum_ready, rsum_ready,
         probs_ready, weight_ready, scan_ready, counts_psum, unchosen_ready, place_ready, onehot_ready, fact_ready,
         rest_ready, slots_psum, slot_sums_ready, own_ready, slot_step, slots_ready, sh_up_psum, sh_silu_ready,
         sh_hT_ready, sh_y_psum, sh_added, xgT_psum, xgT_ready, gu_psum, silu_ready, h_ready, hT_psum, hT_ready,
         y_psum, y_ready, total_ready, x_ready, out_stored, mask_ready) = [sem(n) for n in (
             "x_loaded small_loaded consts_ready table_zeroed zeros_ready pads_ready xn_stored logits_psum "
             "logits_sb top_ready replaced_ready chosen_ready shifted_ready expl_ready esum_ready rsum_ready "
             "probs_ready weight_ready scan_ready counts_psum unchosen_ready place_ready onehot_ready fact_ready "
             "rest_ready slots_psum slot_sums_ready own_ready slot_step slots_ready sh_up_psum sh_silu_ready "
             "sh_hT_ready sh_y_psum sh_added xgT_psum xgT_ready gu_psum silu_ready h_ready hT_psum hT_ready "
             "y_psum y_ready total_ready x_ready out_stored mask_ready").split()]
        choices_loaded = [sem(f"choices_loaded{i}") for i in range(4)]

        bank = m.bank
        logits_bank = bank[4][:, :].rearrange("p (t e) -> p t e", e=E)
        counts_bank = bank[5]
        slots_bank = bank[6]
        sh_up_banks = [(bank[0], bank[1]), (bank[2], bank[3])] * 2 + [(bank[4], bank[5])] * 2
        sh_y_banks = [(bank[4], bank[7]), (bank[4], bank[5])]
        rows_banks, gu_banks, y_banks = bank[0:2], bank[2:4], bank[6:8]
        xn_rows = w.xn_dram
        table_tiles = w.table.rearrange("(t p k) d -> t p k d", p=P, k=TOPK)
        out_tiles = w.out.rearrange("b s d -> (b s) d").rearrange("(t p) d -> t p d", p=P)
        x_tiles = w.x.rearrange("(t p) d -> t p d", p=P)
        xn_tiles = w.xn_dram.rearrange("(t p) d -> t p d", p=P)

        def zero_table(eng, tiles):
            for t in tiles:
                eng.dma_start(table_tiles[t], m.zeros[:, :].unsqueeze(1).to_broadcast([P, TOPK, DM]))\
                   .then_inc(table_zeroed, 16)

        block = ctx.enter_context(nc.Block())

        @block.sync
        def _(sp):
            if first:
                for t in range(NT):
                    sp.dma_start(m.x[:, t, :], x_tiles[t]).then_inc(x_loaded, 16)
                sp.dma_start(m.gate[:, :, :], w.gate_t.rearrange("(c p) e -> p c e", p=P)).then_inc(small_loaded, 16)
                sp.dma_start(m.sh_gate[:, :, :], w.sw_gate.rearrange("(c p) i -> p c i", p=P)).then_inc(small_loaded, 16)
                sp.dma_start(m.sh_up[:, :, :], w.sw_up.rearrange("(c p) i -> p c i", p=P)).then_inc(small_loaded, 16)
                sp.dma_start(m.sh_down[:, 0:2, :],
                             w.sw_down[0:2 * P, :].rearrange("(c p) d -> p c d", p=P)).then_inc(small_loaded, 16)
                sp.dma_start(m.sh_down[0:SH[2], 2, :], w.sw_down[2 * P:IS, :]).then_inc(small_loaded, 16)
                first_chunks(sp, w, m, weights_loaded)
            else:
                load_expert_chunk(sp, w, slots[4], weights_loaded[4], 4)
            for t in range(NT):
                sp.wait_ge(s.xn_ready, t + 1)
                sp.dma_start(xn_tiles[t], m.xn[:, t, :]).then_inc(xn_stored, 16)
            if first:
                sp.wait_ge(gathered[AHEAD - 1], 16)
                zero_table(sp, range(NT // 2, NT))
                load_expert_chunk(sp, w, slots[4], weights_loaded[4], 4)
            sp.wait_ge(slots_psum, 1)
            load_expert_chunk(sp, w, slots[5], weights_loaded[5], 5)
            for n in range(RING, NC):
                sp.wait_ge(weights_loaded[n % RING], 48 * (n // RING))
                sp.wait_ge(y_psum, n + 1 - RING)
                load_expert_chunk(sp, w, slots[n % RING], weights_loaded[n % RING], n)
            for p in range(2):
                sp.wait_ge(scattered[p], 16 * (NC // 2))
            for t in range(NT):
                if t >= 4:
                    sp.wait_ge(total_ready, t - 3)
                sp.dma_start(choice_rows[t % 4], table_tiles[t].rearrange("p k d -> p (k d)"))\
                  .then_inc(choices_loaded[t % 4], 16)
            if last:
                for t in range(NT):
                    sp.wait_ge(x_ready, t + 1)
                    sp.dma_start(out_tiles[t], m.x[:, t, :]).then_inc(out_stored, 16)
                sp.wait_ge(out_stored, 16 * NT)

        @block.gpsimd
        def _(pool):
            if first:
                pool.memset(m.ident[:, :], 0.0).then_inc(zeros_ready, 1)
                pool.memset(m.triangle[:, :], 1.0).then_inc(zeros_ready, 1)
                pool.memset(m.resets[:, :, :], 1.0).then_inc(zeros_ready, 1)
                pool.memset(m.zeros[:, :], 0.0).then_inc(zeros_ready, 1)
                pool.wait_ge(zeros_ready, 4)
                pool.affine_select(out=m.ident[:, :], in_=m.ident[:, :], compare_op=ALU.not_equal, fill=1.0,
                                   base=0, pattern=[[-1, P]], channel_multiplier=1).then_inc(consts_ready, 1)
                pool.affine_select(out=m.triangle[:, :], in_=m.triangle[:, :], compare_op=ALU.is_gt, fill=0.0,
                                   base=0, pattern=[[1, P]], channel_multiplier=-1).then_inc(consts_ready, 1)
                pool.memset(m.ones[:, :], 1.0).then_inc(consts_ready, 1)
                pool.memset(m.resets[:, :, 0:1], 0.0).then_inc(consts_ready, 1)
                pool.wait_ge(consts_ready, 1)
                pool.tensor_copy(m.by_expert[:, :].rearrange("p (e c) -> p e c", e=EC),
                                 m.ident[:, :].rearrange("p (c e) -> p e c", e=EC)).then_inc(consts_ready, 1)
            token = facts[:, :, :, NF * EC:]
            pool.iota(token[:, :, :, 0], pattern=[[0, NT], [0, NC]], base=0, channel_multiplier=1,
                      allow_small_or_imprecise_dtypes=True).then_inc(rest_ready, 1)
            pool.iota(token[:, :, :, 1], pattern=[[P, NT], [0, NC]], base=0, channel_multiplier=0,
                      allow_small_or_imprecise_dtypes=True).then_inc(rest_ready, 1)
            pool.memset(token[:, :, :, 2], 1.0).then_inc(rest_ready, 1)

            pool.wait_ge(xn_stored, 16 * NT)
            pool.wait_ge(slots_ready, 2)

            def gather(n):
                if n >= AHEAD:
                    pool.wait_ge(xgT_psum, n + 1 - AHEAD)
                pool.indirect_dma_start(
                    out=xg[n % AHEAD], out_offset=None, in_=xn_rows,
                    in_offset=bass.IndirectOffsetOnAxis(ap=gather_index[:, n:n + 1], axis=0),
                    bounds_check=T - 1, oob_is_err=False).then_inc(gathered[n % AHEAD], 16)

            for n in range(AHEAD):
                gather(n)
            for n in range(NC):
                if n + AHEAD < NC:
                    gather(n + AHEAD)
                pool.wait_ge(y_ready, n + 1)
                if n == 0:
                    pool.wait_ge(table_zeroed, 16 * NT)
                pool.indirect_dma_start(
                    out=w.table, out_offset=bass.IndirectOffsetOnAxis(ap=scatter_index[:, n:n + 1], axis=0),
                    in_=y[:, n % 2, :], in_offset=None,
                    bounds_check=T * TOPK - 1, oob_is_err=False).then_inc(scattered[n % 2], 16)

        @block.scalar
        def _(act):
            norm_scalar(act, m, s)
            if first:
                act.wait_ge(zeros_ready, 4)
            zero_table(act, range(NT // 2 if first else NT))
            act.wait_ge(logits_psum, 1)
            act.copy(logits[:, :, 0:E], logits_bank).then_inc(logits_sb, 1)
            act.wait_ge(shifted_ready, 1)
            act.activation(expl[:, :, :], shifted[:, :, :], ACT.Exp).then_inc(expl_ready, 1)

            def shared_silu(k):
                act.wait_ge(sh_up_psum, k + 1)
                if k >= 2:
                    act.wait_ge(sh_hT_ready, k - 1)
                rows = SH[k % 3]
                act.activation(sh_silu[0:rows, k % 2, :], sh_up_banks[k][0][0:rows, :], ACT.Silu)\
                   .then_inc(sh_silu_ready, 1)

            for k in range(4):
                shared_silu(k)

            def gate(n):
                par = n.c % 2
                act.wait_ge(gu_psum, n.times(1, 1))
                wait_count(act, h_ready, n.times(1, -1))
                act.activation(gsilu[:, par, :], gu_banks[par][:, 0:I], ACT.Silu).then_inc(silu_ready, 1)

            def weigh(n):
                par = n.c % 2
                act.wait_ge(y_psum, n.times(1, 1))
                wait_count(act, scattered[par], n.rounds(2, 16))
                act.activation(y[:, par, :], y_banks[par][:, 0:DM], ACT.Copy,
                               scale=slot_weight[:, bass.ds(n.times(1), 1)]).then_inc(y_ready, 1)

            def step(n):
                gate(n)
                if not n.below(1):
                    weigh(n.after(-1))

            for c in range(3):
                step(Chunk(0, 2, c))
                if c < 2:
                    shared_silu(4 + c)
            with act.Fori(0, (NC - 4) // 2) as i:
                for c in (3, 4):
                    step(Chunk(i, 2, c))
            step(Chunk(0, 2, NC - 1))
            weigh(Chunk(0, 2, NC - 1))

        @block.vector
        def _(vec):
            vec.memset(logits[:, :, E:E + 2], PAD).then_inc(pads_ready, 1)
            if first:
                vec.memset(m.own_mask[:, :], 0.0).then_inc(mask_ready, 1)
                vec.wait_ge(mask_ready, 1)
                for e in range(EC):
                    vec.memset(m.own_mask[e * CAP:(e + 1) * CAP, e:e + 1], 1.0).then_inc(mask_ready, 1)
                vec.wait_ge(mask_ready, 1 + EC)
                vec.wait_ge(x_loaded, 16 * NT)
            norm_vector(vec, m, s)
            vec.wait_ge(logits_sb, 1)
            vec.wait_ge(pads_ready, 1)
            for t in range(NT):
                vec.max(top[:, t, :], logits[:, t, :]).then_inc(top_ready, 1)
            for t in range(NT):
                vec.wait_ge(top_ready, t + 1)
                vec.match_replace(replaced[:, t, :], top[:, t, :], logits[:, t, :], -PAD).then_inc(replaced_ready, 1)
            vec.wait_ge(replaced_ready, NT)
            vec.tensor_scalar(chosen[:, :, :], replaced[:, :, 0:E], -PAD, None, ALU.is_equal).then_inc(chosen_ready, 1)
            vec.tensor_tensor(shifted[:, :, :], logits[:, :, 0:E], top[:, :, 2:3].to_broadcast([P, NT, E]),
                              ALU.subtract).then_inc(shifted_ready, 1)
            vec.wait_ge(chosen_ready, 1)
            flat_chosen = chosen[:, :, :].rearrange("p t e -> p (t e)")
            vec.tensor_tensor_scan(rank[:, :], m.resets[:, :, :].rearrange("p t e -> p (t e)"), flat_chosen, 0.0,
                                   ALU.mult, ALU.add).then_inc(scan_ready, 1)
            vec.tensor_scalar(unchosen[:, :], flat_chosen, -64.0, 64.0, ALU.mult, ALU.add)\
               .then_inc(unchosen_ready, 1)
            def shared_hidden(k):
                rows = SH[k % 3]
                vec.wait_ge(sh_silu_ready, k + 1)
                if k >= 3:
                    vec.wait_ge(sh_y_psum, 1)
                vec.tensor_tensor(sh_hT[0:rows, k % 3, :], sh_up_banks[k][1][0:rows, :],
                                  sh_silu[0:rows, k % 2, :], ALU.mult).then_inc(sh_hT_ready, 1)

            def shared_add(half):
                vec.wait_ge(sh_y_psum, half + 1)
                for b in range(2):
                    tiles = m.x[:, 4 * half + 2 * b:4 * half + 2 * b + 2, :].rearrange("p t d -> p (t d)")
                    vec.scalar_tensor_tensor(out=tiles, in0=sh_y_banks[half][b][:, :], scalar=0.5, in1=tiles,
                                             op0=ALU.mult, op1=ALU.add).then_inc(sh_added, 1)

            vec.wait_ge(expl_ready, 1)
            vec.tensor_reduce(esum[:, :], expl[:, :, :], AX_X, ALU.add).then_inc(esum_ready, 1)
            vec.wait_ge(esum_ready, 1)
            vec.reciprocal(rsum[:, :], esum[:, :]).then_inc(rsum_ready, 1)
            vec.wait_ge(rsum_ready, 1)
            vec.tensor_tensor(expl[:, :, :], expl[:, :, :], rsum[:, :].unsqueeze(2).to_broadcast([P, NT, E]),
                              ALU.mult).then_inc(probs_ready, 1)
            weight = expl[:, :, :].rearrange("p t (e n) -> p t n e", n=NC)

            vec.wait_ge(scan_ready, 1)
            vec.tensor_tensor(facts[:, :, :, 0:EC], rank[:, :].rearrange("p (t e n) -> p t n e", n=NC, e=EC),
                              chosen[:, :, :].rearrange("p t (e n) -> p t n e", n=NC),
                              ALU.subtract).then_inc(fact_ready, 1)
            for part in range(1, NF):
                vec.wait_ge(probs_ready, 2 * part - 1 if part > 1 else 1)
                f = facts[:, :, :, part * EC:(part + 1) * EC]
                vec.tensor_copy(f, weight).then_inc(fact_ready, 1)
                if part < NF - 1:
                    vec.wait_ge(fact_ready, part + 1)
                    vec.tensor_tensor(weight, weight, f, ALU.subtract).then_inc(probs_ready, 2)
            vec.wait_ge(counts_psum, 1)
            vec.wait_ge(unchosen_ready, 1)
            vec.scalar_tensor_tensor(out=place[:, :], in0=counts_bank[:, :], scalar=64.0, in1=unchosen[:, :],
                                     op0=ALU.min, op1=ALU.add).then_inc(place_ready, 1)
            vec.wait_ge(place_ready, 1)
            for c in range(CAP):
                vec.tensor_scalar(onehot[:, :, c, :], place[:, :].rearrange("p (t e) -> p t e", e=E), float(c), None,
                                  ALU.is_equal)\
                   .then_inc(onehot_ready, 1)
                if c in (7, 15):
                    shared_hidden(c // 8)
            shared_hidden(2)
            for bank_of_slots in (slots_bank, counts_bank):
                vec.wait_ge(slots_psum, 1 if bank_of_slots is slots_bank else 2)
                vec.tensor_copy(slot_sums[:, :, :], bank_of_slots[:, 0:NC * RW].rearrange("p (n r) -> p n r", r=RW))\
                   .then_inc(slot_sums_ready, 1)
            vec.wait_ge(slot_sums_ready, 2)
            vec.tensor_tensor(own[:, :, :].rearrange("p n (f e) -> p n f e", e=EC),
                              slot_sums[:, :, 0:NF * EC].rearrange("p n (f e) -> p n f e", e=EC),
                              m.own_mask[:, :].unsqueeze(1).unsqueeze(1).to_broadcast([P, NC, NF, EC]),
                              ALU.mult).then_inc(own_ready, 1)
            vec.wait_ge(own_ready, 1)
            vec.tensor_reduce(own_facts[:, :, :], own[:, :, :].rearrange("p n (f e) -> p n f e", e=EC), AX_X,
                              ALU.add).then_inc(slot_step, 1)
            vec.tensor_reduce(slot_token[:, :], slot_sums[:, :, NF * EC:NF * EC + 2], AX_X, ALU.add)\
               .then_inc(slot_step, 1)
            vec.tensor_scalar(slot_far[:, :], slot_sums[:, :, NF * EC + 2], -FAR, FAR, ALU.mult, ALU.add)\
               .then_inc(slot_step, 1)
            vec.wait_ge(slot_step, 3)
            vec.tensor_reduce(slot_weight[:, :], own_facts[:, :, 1:NF], AX_X, ALU.add).then_inc(slot_step, 1)
            vec.tensor_copy(gather_index[:, :], slot_token[:, :]).then_inc(slots_ready, 1)
            vec.scalar_tensor_tensor(out=slot_row[:, :], in0=slot_token[:, :], scalar=float(TOPK),
                                     in1=own_facts[:, :, 0], op0=ALU.mult, op1=ALU.add).then_inc(slot_step, 1)
            vec.wait_ge(slot_step, 5)
            vec.tensor_tensor(slot_row[:, :], slot_row[:, :], slot_far[:, :], ALU.add).then_inc(slot_step, 1)
            vec.wait_ge(slot_step, 6)
            vec.tensor_copy(scatter_index[:, :], slot_row[:, :]).then_inc(slots_ready, 1)

            shared_add(0)
            shared_hidden(3)

            def take_rows(n):
                par = n.c % 2
                vec.wait_ge(xgT_psum, n.times(1, 1))
                wait_count(vec, gu_psum, n.times(1, -1))
                vec.tensor_copy(xgT[:, par, :], rows_banks[par][:, 0:KC * P]).then_inc(xgT_ready, 1)

            def multiply(n):
                par = n.c % 2
                vec.wait_ge(silu_ready, n.times(1, 1))
                wait_count(vec, hT_psum, n.times(1, -1))
                vec.tensor_tensor(h[:, par, :], gu_banks[par][:, I:2 * I], gsilu[:, par, :], ALU.mult)\
                   .then_inc(h_ready, 1)

            def take_hidden(n):
                par = n.c % 2
                vec.wait_ge(hT_psum, n.times(1, 1))
                wait_count(vec, y_psum, n.times(1, -1))
                vec.tensor_copy(hT[:, par, 0:P], rows_banks[par][:, 2 * P:3 * P]).then_inc(hT_ready, 1)
                vec.tensor_copy(hT[0:IHI, par, P:2 * P], rows_banks[par][0:IHI, 3 * P:4 * P]).then_inc(hT_ready, 1)

            def step(n):
                multiply(n)
                if n.below(NC - 1) or not isinstance(n.i, int):
                    take_rows(n.after(1))
                take_hidden(n)

            take_rows(Chunk(0, 2, 0))
            for c in range(3):
                step(Chunk(0, 2, c))
                if c < 2:
                    shared_hidden(4 + c)
                else:
                    shared_add(1)
            with vec.Fori(0, (NC - 4) // 2) as i:
                for c in (3, 4):
                    step(Chunk(i, 2, c))
            step(Chunk(0, 2, NC - 1))

            vec.wait_ge(sh_added, 4)
            for t in range(NT):
                vec.wait_ge(choices_loaded[t % 4], 16 * (t // 4 + 1))
                if t >= 2:
                    vec.wait_ge(x_ready, t - 1)
                vec.tensor_reduce(total[:, t % 2, :], choice_rows[t % 4].rearrange("p (k d) -> p d k", k=TOPK),
                                  AX_X, ALU.add).then_inc(total_ready, 1)
                vec.wait_ge(total_ready, t + 1)
                vec.scalar_tensor_tensor(out=m.x[:, t, :], in0=total[:, t % 2, :], scalar=0.5, in1=m.x[:, t, :],
                                         op0=ALU.mult, op1=ALU.add).then_inc(x_ready, 1)

        @block.tensor
        def _(pe):
            if first:
                pe.wait_ge(consts_ready, 5)
            norm_tensor(pe, m, s)
            pe.wait_ge(s.xnT_vec, 2)
            pe.wait_ge(s.xnT_act, 2)
            if first:
                pe.wait_ge(small_loaded, 16 * 5)
            for t in range(NT):
                for c in range(KC):
                    ins = pe.matmul(logits_bank[:, t, :], m.xnT[:, c, t * P:t * P + P], m.gate[:, c, :],
                                    start=(c == 0), stop=(c == KC - 1))
            ins.then_inc(logits_psum, 1)

            def shared_up(k):
                half, part = k // 3, k % 3
                cols = slice(part * P, part * P + SH[part])
                if k >= 2:
                    pe.wait_ge(sh_hT_ready, k if k == 5 else k - 1)
                for weights, to in zip((m.sh_gate, m.sh_up), sh_up_banks[k]):
                    for c in range(KC):
                        ins = pe.matmul(to[0:SH[part], :], weights[:, c, cols],
                                        m.xnT[:, c, half * 512:half * 512 + 512], start=(c == 0), stop=(c == KC - 1))
                ins.then_inc(sh_up_psum, 1)

            def shared_down(half):
                pe.wait_ge(sh_hT_ready, 3 * half + 3)
                for t in range(4):
                    to = sh_y_banks[half][t // 2][:, t % 2 * DM:t % 2 * DM + DM]
                    for part in range(3):
                        ins = pe.matmul(to, sh_hT[0:SH[part], part, t * P:t * P + P],
                                        m.sh_down[0:SH[part], part, :], start=(part == 0), stop=(part == 2))
                ins.then_inc(sh_y_psum, 1)

            shared_up(0)
            pe.wait_ge(chosen_ready, 1)
            for t in range(NT):
                to = counts_bank[:, t * E:t * E + E]
                for before in range(t):
                    pe.matmul(to, m.ones[:, :], chosen[:, before, :], start=(before == 0), stop=False)
                ins = pe.matmul(to, m.triangle[:, :], chosen[:, t, :], start=(t == 0), stop=True)
            ins.then_inc(counts_psum, 1)
            shared_up(1)
            shared_up(2)
            pe.wait_ge(onehot_ready, CAP)
            pe.wait_ge(fact_ready, NF)
            pe.wait_ge(rest_ready, 3)
            for n in range(NC):
                for t in range(NT):
                    ins = pe.matmul(slots_bank[:, n * RW:n * RW + RW],
                                    onehot[:, t, :, :].rearrange("p c (e n) -> p n (c e)", n=NC)[:, n, :],
                                    facts[:, t, n, :], start=(t == 0), stop=(t == NT - 1))
            ins.then_inc(slots_psum, 1)
            pe.wait_ge(slot_sums_ready, 1)
            pe.matmul(counts_bank[:, 0:NC * RW], m.by_expert[:, :], slot_sums[:, :, :].rearrange("p n r -> p (n r)"),
                      start=True, stop=True).then_inc(slots_psum, 1)
            pe.wait_ge(logits_sb, 1)
            shared_down(0)
            shared_up(3)

            def rows_in(n):
                par = n.c % 2
                pe.wait_ge(gathered[n.c % AHEAD], n.rounds(AHEAD, 16, 1))
                wait_count(pe, xgT_ready, n.times(1, -1))
                for c in range(KC):
                    ins = pe.transpose(rows_banks[par][:, c * P:c * P + P], xg[n.c % AHEAD][:, c * P:c * P + P],
                                       m.ident[:, :])
                ins.then_inc(xgT_psum, 1)

            def up(n):
                par, slot = n.c % 2, n.c % RING
                pe.wait_ge(xgT_ready, n.times(1, 1))
                pe.wait_ge(weights_loaded[slot], n.rounds(RING, 48, 1))
                wait_count(pe, h_ready, n.times(1, -1))
                wgu = slots[slot].gu.rearrange("p (e c i) -> p e c i", c=KC, i=2 * I)
                for e in range(EC):
                    rows = slice(e * CAP, (e + 1) * CAP)
                    for c in range(KC):
                        ins = pe.matmul(gu_banks[par][rows, 0:2 * I], xgT[:, par, c * P + e * CAP:c * P + (e + 1) * CAP],
                                        wgu[:, e, c, :], start=(c == 0), stop=(c == KC - 1))
                ins.then_inc(gu_psum, 1)

            def hidden(n):
                par = n.c % 2
                pe.wait_ge(h_ready, n.times(1, 1))
                wait_count(pe, hT_ready, n.times(2, -1))
                pe.transpose(rows_banks[par][:, 2 * P:3 * P], h[:, par, 0:ILO], m.ident[:, :])
                pe.transpose(rows_banks[par][0:IHI, 3 * P:4 * P], h[:, par, ILO:I], m.ident[:, :]).then_inc(hT_psum, 1)

            def down(n):
                par, slot = n.c % 2, n.c % RING
                pe.wait_ge(hT_ready, n.times(2, 1))
                wait_count(pe, y_ready, n.times(1, -1))
                for e in range(EC):
                    rows = slice(e * CAP, (e + 1) * CAP)
                    wide = slice(e * DM, (e + 1) * DM)
                    pe.matmul(y_banks[par][rows, 0:DM], hT[:, par, e * CAP:(e + 1) * CAP], slots[slot].lo[:, wide],
                              start=True, stop=False)
                    ins = pe.matmul(y_banks[par][rows, 0:DM], hT[0:IHI, par, P + e * CAP:P + (e + 1) * CAP],
                                    slots[slot].hi[:, wide], start=False, stop=True)
                ins.then_inc(y_psum, 1)

            def step(n):
                up(n)
                if not n.below(1):
                    down(n.after(-1))
                if n.below(NC - 1) or not isinstance(n.i, int):
                    rows_in(n.after(1))
                hidden(n)

            rows_in(Chunk(0, RING, 0))
            pe.wait_ge(sh_hT_ready, 4)
            for c in range(3):
                step(Chunk(0, RING, c))
                if c == 0:
                    pe.wait_ge(slot_sums_ready, 2)
                    pe.wait_ge(sh_added, 2)
                if c < 2:
                    shared_up(4 + c)
                else:
                    shared_down(1)
            with pe.Fori(0, (NC - 4) // RING) as i:
                for c in range(3, RING + 3):
                    step(Chunk(i, RING, c))
            step(Chunk(0, RING, NC - 1))
            down(Chunk(0, RING, NC - 1))


def attention(nc, w, m, used, next_weights_loaded):
    with ExitStack() as ctx:
        def sb(name, shape, dt=F32):
            return ctx.enter_context(nc.sbuf_tensor(f"at_{name}", shape, dt))

        def sem(name):
            return ctx.enter_context(nc.semaphore(f"at_{name}"))

        w_qkv = sb("w_qkv", [P, KC, 3 * DM])
        w_o = sb("w_o", [P, KC, DM])
        rope_cos = sb("rope_cos", [P, 2, 2, HD])
        rope_sin = sb("rope_sin", [P, 2, 2, HD])
        qk = sb("qk", [P, NT, 2, DM])
        v = sb("v", [P, NT, NH, HD + 1])
        bias_rows = sb("bias_rows", [NH, MAXB + S])
        bias = sb("bias", [P, 2, 8, S])
        offset = sb("offset", [P, NH])
        neg_offset = sb("neg_offset", [P, NH])
        qk_pad = sb("qk_pad", [P, 2, 2, 2, 4, 32])
        v_quad = sb("v_quad", [P, 2, 2, 4, 32])
        qkT = sb("qkT", [P, 2, 2, 2, P])
        neg_scores = sb("neg_scores", [P, 4, P + S])
        neg_max = sb("neg_max", [P, 8, 2])
        probs = sb("probs", [P, 4, P + S])
        by_cos, by_sin = (buffer[:, :, :].rearrange("p k j -> p (k j)")[:, 0:2 * 2 * DM]
                          .rearrange("p (t n) -> p t n", t=2) for buffer in (neg_scores, probs))
        probsT = sb("probsT", [P, 8, P + S])
        heads_outT = sb("heads_outT", [P, 2, S])
        off_shift = sb("off_shift", [P, 2, 2, 4])
        off_exp = sb("off_exp", [P, 2, 2, 4])
        denom = sb("denom", [P, 2, 4])
        rdenom = sb("rdenom", [P, 2, 4])
        heads_out = sb("heads_out", [P, 2, 2, 4 * HD])
        attn, attnT = m.xn, m.xnT

        s = NormSems(sem)
        (small_loaded, rows_masked, rows_loaded, rows_stored, pad_ready, neg_off_ready,
         ones_ready, qkv_psum, cos_done, sin_done, qk_ready, v_ready, staged, v_staged, qkT_psum, qkT_ready,
         s_psum, scored, exp_done, pT_psum, pT_vec, pT_act, pv_psum, outT_ready, turned_psum, off_in, off_ready,
         den_ready, rden_ready,
         quad_out, attn_stored, attnT_psum, attnT_vec, attnT_act, o_psum, x_ready) = [sem(n) for n in (
             "small_loaded rows_masked rows_loaded rows_stored pad_ready neg_off_ready "
             "ones_ready qkv_psum cos_done sin_done qk_ready v_ready staged v_staged qkT_psum qkT_ready "
             "s_psum scored exp_done pT_psum pT_vec pT_act pv_psum outT_ready turned_psum off_in off_ready "
             "den_ready rden_ready "
             "quad_out attn_stored attnT_psum attnT_vec attnT_act o_psum x_ready").split()]
        bias_loaded = [sem(f"bias_loaded{i}") for i in range(2)]
        bank = m.bank
        score_banks, probs_banks, out_bank, qk_bank = bank[0:4], bank[4:6], bank[6], bank[7]
        outT_sums = out_bank[:, 0:S]
        sums = out_bank[:, S:2 * S].rearrange("p (t g d) -> p t g d", t=2, g=4)

        block = ctx.enter_context(nc.Block())

        @block.sync
        def _(sp):
            sp.dma_start(w_qkv[:, :, :], w.w_qkv.rearrange("(c p) n -> p c n", p=P)).then_inc(small_loaded, 16)
            sp.dma_start(w_o[:, :, :], w.w_o.rearrange("(c p) n -> p c n", p=P)).then_inc(small_loaded, 16)
            sp.dma_start(rope_cos[:, :, :, :].rearrange("p t q c -> p (t q c)"), w.rope_cos).then_inc(small_loaded, 16)
            sp.dma_start(rope_sin[:, :, :, :].rearrange("p t q c -> p (t q c)"), w.rope_sin).then_inc(small_loaded, 16)
            sp.dma_start(offset[:, :], w.offset.partition_broadcast(P)).then_inc(small_loaded, 16)
            sp.wait_ge(rows_masked, 2)
            sp.dma_start(bias_rows[:, P:2 * P], w.bias_reversed).then_inc(rows_loaded, 16)
            sp.wait_ge(rows_loaded, 16)
            sp.dma_start(w.bias_dram.rearrange("p h r -> h p r"),
                         bias_rows[:, :].unsqueeze(1).to_broadcast([NH, P, 3 * P])).then_inc(rows_stored, 16)
            sp.wait_ge(rows_stored, 16)
            for o in range(NH // 8):
                wait_count(sp, scored, (o - 1) * B * 8 * 2)
                skewed = bass.AP(w.bias_dram.tensor, o * 8 * 3 * P + P - 1, [[NH * 3 * P - 1, P], [3 * P, 8], [1, S]])
                sp.dma_start(bias[:, o % 2, :, :], skewed).then_inc(bias_loaded[o % 2], 16)
                if o == 1:
                    first_chunks(sp, w, m, next_weights_loaded)

        @block.gpsimd
        def _(pool):
            pool.sem_clear(range(min(used), max(used) + 1))
            pool.memset(bias_rows[:, 0:P], 0.0).then_inc(rows_masked, 1)
            pool.memset(bias_rows[:, 2 * P:3 * P], MASKED).then_inc(rows_masked, 1)
            pool.memset(qk_pad[:, :, :, :, :, :], 0.0).then_inc(pad_ready, 1)
            pool.memset(v_quad[:, :, :, :, :], 0.0).then_inc(pad_ready, 1)
            pool.memset(v[:, :, :, HD:HD + 1], 1.0).then_inc(ones_ready, 1)
            pool.memset(heads_out[:, :, :, :], 0.0).then_inc(attn_stored, 1)
            for t in range(NT):
                pool.wait_ge(cos_done, t + 1)
                pool.wait_ge(sin_done, 2 * t + 2)
                pool.tensor_tensor(qk[:, t, :, :].rearrange("p q n -> p (q n)"), by_cos[:, t % 2, :],
                                   by_sin[:, t % 2, :], ALU.add).then_inc(qk_ready, 1)
            pool.wait_ge(qk_ready, NT)
            pool.wait_ge(v_ready, NT)
            pool.wait_ge(pad_ready, 2)
            pool.wait_ge(ones_ready, 1)

            def stage(o, b, q2, quad):
                wait_count(pool, qkT_psum, quad - 1)
                for tile in range(2):
                    src = qk[:, bass.ds(b * 2 + tile, 1), :, bass.ds(o * 64 + q2 * 32, 32)]\
                        .rearrange("p a q (g d) -> p (a q) g d", g=4)
                    pool.tensor_copy(qk_pad[:, q2, tile, :, :, 0:HD], src).then_inc(staged, 1)
                wait_count(pool, pv_psum, quad - 1)
                src = v[:, bass.ds(b * 2, 2), bass.ds(o * 8 + q2 * 4, 4), :]
                pool.tensor_copy(v_quad[:, q2, :, :, 0:HD + 1], src).then_inc(v_staged, 1)

            def store(o, b, q2, quad):
                pool.wait_ge(quad_out, quad + 1)
                pool.tensor_copy(attn[:, bass.ds(b * 2, 2), bass.ds(o * 64 + q2 * 32, 32)],
                                 heads_out[:, q2, :, :]).then_inc(attn_stored, 1)

            def octet(o):
                for j in range(2 * B):
                    stage(o, j // 2, j % 2, o * 8 + j)
                    if j >= 3:
                        store(o, (j - 3) // 2, (j - 3) % 2, o * 8 + (j - 3))
                    elif not isinstance(o, int):
                        store(o - 1, (j + 5) // 2, (j + 5) % 2, o * 8 + (j - 3))

            octet(0)
            with pool.Fori(1, NH // 8) as o:
                octet(o)
            for j in range(5, 8):
                store(NH // 8 - 1, j // 2, j % 2, NQUAD - 8 + j)

        def by_pairs(eng, pair):
            rounds = NQUAD // 2
            for o in range(NH // 8):
                if o == 0:
                    for p in range(4):
                        pair(0, p, o)
                with eng.Fori(max(1, B * o), min(rounds - 1, B * (o + 1))) as i:
                    for p in range(4):
                        pair(i, p, o)
            for p in range(4):
                pair(rounds - 1, p, o)

        def exists(i, p):
            return not isinstance(i, int) or i * 4 + p >= 0

        def last_round(i):
            return isinstance(i, int) and i == NQUAD // 2 - 1

        @block.scalar
        def _(act):
            norm_scalar(act, m, s)
            for t in range(NT):
                act.wait_ge(qkv_psum, t + 1)
                act.copy(v[:, t, :, 0:HD], bank[6 + t % 2][:, 0:DM].rearrange("p (h d) -> p h d", d=HD))\
                   .then_inc(v_ready, 1)

            def take_qkT(quad, q2):
                act.wait_ge(qkT_psum, quad + 1)
                wait_count(act, s_psum, quad * 2 - 2)
                act.copy(qkT[:, q2, :, :, :].rearrange("p t q n -> p (t q n)"), qk_bank[:, :])\
                   .then_inc(qkT_ready, 1)

            def take_off(quad, q2):
                act.wait_ge(off_in, quad + 1)
                act.activation(off_exp[:, q2, :, :], off_shift[:, q2, :, :], ACT.Exp).then_inc(off_ready, 1)

            def take_outT(quad, q2):
                act.wait_ge(pv_psum, quad + 1)
                wait_count(act, turned_psum, quad - 1)
                act.copy(heads_outT[:, q2, :], outT_sums).then_inc(outT_ready, 1)

            def take_probsT(i, p):
                wait_count(act, pv_psum, i * 2 + (p // 2 - 1))
                act.wait_ge(pT_psum, i * 8 + (2 * p + 2))
                act.copy(probsT[:, (2 * p + 1) % 8, :], probs_banks[1][:, 0:P + S]).then_inc(pT_act, 1)

            def pair(i, p, o):
                n = i * 4 + p
                if p % 2 == 0 and exists(i, p - 1):
                    take_off(i * 2 + (p // 2 - 1), 1 - p // 2)
                if p == 1 or p == 3 and not last_round(i):
                    take_qkT(i * 2 + (p + 1) // 2, (p + 1) // 2 % 2)
                wait_count(act, pT_psum, n * 2 - 2)
                for k in (2 * p, 2 * p + 1):
                    act.wait_ge(scored, i * 16 + (2 * k + 2))
                    act.activation(probs[:, k % 4, 0:P], neg_scores[:, k % 4, 0:P], ACT.Exp,
                                   bias=neg_max[:, k, 0:1], scale=-1.0).then_inc(exp_done, 1)
                    act.activation(probs[:, k % 4, P:P + S], neg_scores[:, k % 4, P:P + S], ACT.Exp,
                                   bias=neg_max[:, k, 1:2], scale=-1.0).then_inc(exp_done, 1)
                if p % 2 == 1 and exists(i, p - 2):
                    take_outT(i * 2 + (p // 2 - 1), 1 - p // 2)
                if exists(i, p - 1):
                    take_probsT(i, p - 1)

            take_qkT(0, 0)
            by_pairs(act, pair)
            take_off(NQUAD - 1, 1)
            take_probsT(NQUAD // 2, -1)
            take_outT(NQUAD - 1, 1)
            for half in range(2):
                act.wait_ge(attnT_psum, 2 * half + 1)
                act.copy(attnT[:, 0, half * 512:half * 512 + 512], bank[2 * half][:, :]).then_inc(attnT_act, 1)

        @block.vector
        def _(vec):
            norm_vector(vec, m, s)
            vec.wait_ge(small_loaded, 16 * 5)
            vec.tensor_scalar(neg_offset[:, :], offset[:, :], -1.0, None, ALU.mult).then_inc(neg_off_ready, 1)
            for t in range(NT):
                vec.wait_ge(qkv_psum, t + 1)
                if t >= 2:
                    vec.wait_ge(qk_ready, t - 1)
                src = bank[4 + t % 2][:, :].rearrange("p (q h d) -> p q h d", q=2, d=HD)
                cos = rope_cos[:, t % 2, :, :].unsqueeze(2)
                sin = rope_sin[:, t % 2, :, :].unsqueeze(2)
                to_cos = by_cos[:, t % 2, :].rearrange("p (q h d) -> p q h d", q=2, d=HD)
                to_sin = by_sin[:, t % 2, :].rearrange("p (q h d) -> p q h d", q=2, d=HD)
                half = HD // 2
                vec.tensor_tensor(to_sin[:, :, :, 0:half], src[:, :, :, half:HD],
                                  sin[:, :, :, 0:half].to_broadcast([P, 2, NH, half]), ALU.mult).then_inc(sin_done, 1)
                vec.tensor_tensor(to_sin[:, :, :, half:HD], src[:, :, :, 0:half],
                                  sin[:, :, :, half:HD].to_broadcast([P, 2, NH, half]), ALU.mult).then_inc(sin_done, 1)
                vec.tensor_tensor(to_cos, src, cos.to_broadcast([P, 2, NH, HD]), ALU.mult).then_inc(cos_done, 1)

            def take_probsT(i, p):
                n = i * 4 + p
                wait_count(vec, pv_psum, i * 2 + (p // 2 - 1))
                vec.wait_ge(pT_psum, n * 2 + 1)
                vec.tensor_copy(probsT[:, 2 * p % 8, :], probs_banks[0][:, 0:P + S]).then_inc(pT_vec, 1)

            def finish_quad(quad, q2):
                vec.wait_ge(turned_psum, quad + 1)
                vec.wait_ge(off_ready, quad + 1)
                vec.tensor_tensor(denom[:, :, :], sums[:, :, :, HD], off_exp[:, q2, :, :], ALU.add)\
                   .then_inc(den_ready, 1)
                vec.wait_ge(den_ready, quad + 1)
                vec.reciprocal(rdenom[:, :, :], denom[:, :, :]).then_inc(rden_ready, 1)
                vec.wait_ge(rden_ready, quad + 1)
                vec.wait_ge(attn_stored, 1 if isinstance(quad, int) and quad == 0 else quad)
                vec.tensor_tensor(heads_out[:, q2, :, :].rearrange("p t (g d) -> p t g d", d=HD),
                                  sums[:, :, :, 0:HD],
                                  rdenom[:, :, :].unsqueeze(3).to_broadcast([P, 2, 4, HD]),
                                  ALU.mult).then_inc(quad_out, 1)

            def pair(i, p, o):
                n = i * 4 + p
                due, free = n + 1, n * 4 - 4
                if not isinstance(i, int):
                    due, free = vec.to_reg(due), vec.to_reg(free)
                vec.wait_ge(bias_loaded[o % 2], 16 * (o // 2 + 1))
                vec.wait_ge(s_psum, due)
                wait_count(vec, exp_done, free)
                for k in (2 * p, 2 * p + 1):
                    scores, tiles = score_banks[k % 4], bias[:, o % 2, k, :]
                    off = neg_offset[:, 8 * o + k:8 * o + k + 1]
                    vec.tensor_tensor_reduce(neg_scores[:, k % 4, 0:P], scores[:, 0:P], tiles[:, P:2 * P], -1.0,
                                             off, ALU.add, ALU.min, neg_max[:, k, 0:1]).then_inc(scored, 1)
                    vec.tensor_tensor_reduce(neg_scores[:, k % 4, P:P + S], scores[:, P:P + S], tiles, -1.0,
                                             off, ALU.add, ALU.min, neg_max[:, k, 1:2]).then_inc(scored, 1)
                if p % 2 == 1:
                    q2 = p // 2
                    vec.wait_ge(scored, n * 4 + 4)
                    wait_count(vec, off_ready, i * 2 + (q2 - 1))
                    vec.tensor_tensor(off_shift[:, q2, :, :],
                                      neg_max[:, 4 * q2:4 * q2 + 4, :].rearrange("p g t -> p t g"),
                                      neg_offset[:, 8 * o + 4 * q2:8 * o + 4 * q2 + 4].unsqueeze(1)
                                      .to_broadcast([P, 2, 4]),
                                      ALU.subtract).then_inc(off_in, 1)
                elif exists(i, p - 4):
                    finish_quad(i * 2 + (p // 2 - 2), p // 2)
                if exists(i, p - 1):
                    take_probsT(i, p - 1)

            vec.wait_ge(neg_off_ready, 1)
            by_pairs(vec, pair)
            finish_quad(NQUAD - 2, 0)
            take_probsT(NQUAD // 2, -1)
            finish_quad(NQUAD - 1, 1)
            for half in range(2):
                vec.wait_ge(attnT_psum, 2 * half + 2)
                vec.tensor_copy(attnT[:, 1, half * 512:half * 512 + 512], bank[2 * half + 1][:, :])\
                   .then_inc(attnT_vec, 1)
            for t in range(NT):
                vec.wait_ge(o_psum, t + 1)
                vec.tensor_tensor(m.x[:, t, :], bank[4 + t % 2][:, 0:DM], m.x[:, t, :], ALU.add).then_inc(x_ready, 1)

        @block.tensor
        def _(pe):
            norm_tensor(pe, m, s)
            pe.wait_ge(s.xnT_vec, 2)
            pe.wait_ge(s.xnT_act, 2)
            pe.wait_ge(small_loaded, 16 * 5)
            for t in range(NT):
                if t >= 2:
                    pe.wait_ge(cos_done, t - 1)
                    pe.wait_ge(v_ready, t - 1)
                rows = slice(t * P, t * P + P)
                for c in range(KC):
                    pe.matmul(bank[4 + t % 2][:, :], m.xnT[:, c, rows], w_qkv[:, c, 0:2 * DM],
                              start=(c == 0), stop=(c == KC - 1))
                for c in range(KC):
                    ins = pe.matmul(bank[6 + t % 2][:, 0:DM], m.xnT[:, c, rows], w_qkv[:, c, 2 * DM:3 * DM],
                                    start=(c == 0), stop=(c == KC - 1))
                ins.then_inc(qkv_psum, 1)
            pe.wait_ge(cos_done, NT)
            pe.wait_ge(v_ready, NT)

            def turn_heads(quad, q2):
                pe.wait_ge(staged, quad * 2 + 2)
                wait_count(pe, qkT_ready, quad)
                for tile in range(2):
                    for which in range(2):
                        at = (2 * tile + which) * P
                        ins = pe.transpose(qk_bank[:, at:at + P],
                                           qk_pad[:, q2, tile, which, :, :].rearrange("p g r -> p (g r)"),
                                           m.ident[:, :])
                ins.then_inc(qkT_psum, 1)

            def score(i, p):
                q2 = p // 2
                pe.wait_ge(qkT_ready, i * 2 + (q2 + 1))
                wait_count(pe, scored, i * 16 + (4 * p - 4))
                for tile in range(2):
                    for a in range(2):
                        g = 2 * (p % 2) + a
                        rows = slice(32 * g, 32 * g + HD)
                        ins = pe.matmul(score_banks[g][:, 0:P] if tile == 0 else score_banks[g][:, P:P + S],
                                        qkT[rows, q2, tile, 0, :],
                                        qkT[rows, q2, 0, 1, :] if tile == 0 else qkT[rows, q2, :, 1, :],
                                        start=True, stop=True)
                ins.then_inc(s_psum, 1)

            def turn_probs(i, p):
                for a in range(2):
                    pe.wait_ge(exp_done, i * 16 + (4 * p + 2 * a + 2))
                    wait_count(pe, (pT_vec, pT_act)[a], i * 4 + p)
                    for j in range(3):
                        ins = pe.transpose(probs_banks[a][:, j * P:j * P + P],
                                           probs[:, (2 * p + a) % 4, j * P:j * P + P], m.ident[:, :])
                    ins.then_inc(pT_psum, 1)

            def weigh_values(quad, q2):
                pe.wait_ge(v_staged, quad + 1)
                pe.wait_ge(pT_vec, quad * 2 + 2)
                pe.wait_ge(pT_act, quad * 2 + 2)
                wait_count(pe, outT_ready, quad)
                wait_count(pe, quad_out, quad)
                for tile in range(2):
                    for g in range(4):
                        ins = pe.matmul(outT_sums[32 * g:32 * g + 32, tile * P:S], v_quad[:, q2, tile, g, :],
                                        probsT[:, 4 * q2 + g, tile * S:tile * P + S],
                                        start=(tile == 0), stop=(tile == 1))
                ins.then_inc(pv_psum, 1)

            def turn_outputs(quad, q2):
                pe.wait_ge(outT_ready, quad + 1)
                for tile in range(2):
                    ins = pe.transpose(out_bank[:, S + tile * P:S + tile * P + P],
                                       heads_outT[:, q2, tile * P:tile * P + P], m.ident[:, :])
                ins.then_inc(turned_psum, 1)

            def pair(i, p, o):
                score(i, p)
                if p % 2 == 0:
                    if exists(i, p - 1):
                        turn_probs(i, p - 1)
                    if exists(i, p - 4):
                        turn_outputs(i * 2 + (p // 2 - 2), p // 2)
                    if p == 0 or not last_round(i):
                        turn_heads(i * 2 + (p // 2 + 1), 1 - p // 2)
                else:
                    if exists(i, p - 2):
                        weigh_values(i * 2 + (p // 2 - 1), 1 - p // 2)
                    turn_probs(i, p - 1)

            turn_heads(0, 0)
            by_pairs(pe, pair)
            turn_outputs(NQUAD - 2, 0)
            turn_probs(NQUAD // 2, -1)
            weigh_values(NQUAD - 1, 1)
            turn_outputs(NQUAD - 1, 1)
            pe.wait_ge(attn_stored, NQUAD + 1)
            for half in range(2):
                for q in range(4):
                    for c in range(KC):
                        ins = pe.transpose(bank[2 * half + c][:, q * P:q * P + P],
                                           attn[:, 4 * half + q, c * P:c * P + P], m.ident[:, :])
                        if q == 3:
                            ins.then_inc(attnT_psum, 1)
            pe.wait_ge(attnT_vec, 2)
            pe.wait_ge(attnT_act, 2)
            for t in range(NT):
                if t >= 2:
                    pe.wait_ge(x_ready, t - 1)
                for c in range(KC):
                    ins = pe.matmul(bank[4 + t % 2][:, 0:DM], attnT[:, c, t * P:t * P + P], w_o[:, c, :],
                                    start=(c == 0), stop=(c == KC - 1))
                ins.then_inc(o_psum, 1)


class WeightSlot:

    def __init__(self, gu, lo, hi):
        self.gu, self.lo, self.hi = gu[:, :], lo[:, :], hi[:, :]


class OnChip:

    def __init__(self, sb, bank):
        self.bank = bank
        self.x = sb("x", [P, NT, DM])
        self.xn = sb("xn", [P, NT, DM])
        self.xnT = sb("xnT", [P, KC, T])
        self.stats = sb("stats", [P, NT, 6])
        self.moments = sb("moments", [P, NT, 2])
        self.var_eps = sb("var_eps", [P, NT])
        self.std = sb("std", [P, NT])
        self.rstd = sb("rstd", [P, NT])
        self.gate = sb("gate", [P, KC, E])
        self.sh_gate = sb("sh_gate", [P, KC, IS])
        self.sh_up = sb("sh_up", [P, KC, IS])
        self.sh_down = sb("sh_down", [P, 3, DM])
        self.slots = [WeightSlot(sb(f"w_gu{i}", [P, EC * KC * 2 * I]), sb(f"w_lo{i}", [ILO, EC * DM]),
                                 sb(f"w_hi{i}", [IHI, EC * DM])) for i in range(KEPT)]
        self.ident = sb("ident", [P, P])
        self.by_expert = sb("by_expert", [P, P])
        self.triangle = sb("triangle", [P, P], BF16)
        self.ones = sb("ones", [P, P], BF16)
        self.resets = sb("resets", [P, NT, E])
        self.own_mask = sb("own_mask", [P, EC])
        self.zeros = sb("zeros", [P, DM])


class Dram:

    def __init__(self, nc, given, out):
        self.x = given["x"]
        self.gate_t = given["gate_t"]
        self.w_gu, self.w_lo, self.w_hi = given["w_gu"], given["w_lo"], given["w_hi"]
        self.sw_gate, self.sw_up, self.sw_down = given["sw_gate"], given["sw_up"], given["sw_down"]
        self.w_qkv, self.w_o = given["w_qkv"], given["w_o"]
        self.bias_reversed, self.offset = given["bias_reversed"], given["offset"]
        self.rope_cos, self.rope_sin = given["rope_cos"], given["rope_sin"]
        self.out = out
        self.xn_dram = nc.dram_tensor("xn_rows", [T, DM], F32).ap()
        self.table = nc.dram_tensor("choice_table", [T * TOPK, DM], F32).ap()
        self.bias_dram = nc.dram_tensor("bias_rows_dram", [P, NH, 3 * P], F32).ap()


def build(nc, given, out):
    w = Dram(nc, given, out)
    with ExitStack() as ctx:
        def sb(name, shape, dt=F32):
            return ctx.enter_context(nc.sbuf_tensor(name, shape, dt))

        m = OnChip(sb, [ctx.enter_context(nc.psum_tensor(f"bank{i}", [P, 512], F32)) for i in range(8)])
        loaded = [[ctx.enter_context(nc.semaphore(f"ff{f}_weights{i}")) for i in range(RING)] for f in range(2)]
        gathered, scattered = ([[ctx.enter_context(nc.semaphore(f"ff{f}_{name}{i}")) for i in range(depth)]
                                for f in range(2)] for name, depth in (("gathered", AHEAD), ("scattered", 2)))
        ff_sems = {}

        def ff_sem(name):
            if name not in ff_sems:
                ff_sems[name] = ctx.enter_context(nc.semaphore(f"ff_{name}"))
            return ff_sems[name]

        feed_forward(nc, w, m, ff_sem, "ff0", loaded[0], gathered[0], scattered[0], True, False)
        attention(nc, w, m, [x.num for x in ff_sems.values()], loaded[1])
        feed_forward(nc, w, m, ff_sem, "ff1", loaded[1], gathered[1], scattered[1], False, True)


def rope_tables():
    half = HD // 2
    freq = 1.0 / 10000.0 ** (np.arange(half, dtype=np.float32) / np.float32(half))
    angle = np.outer(np.arange(S, dtype=np.float32), freq.astype(np.float32)).astype(np.float32)
    cos = np.concatenate([np.cos(angle), np.cos(angle)], axis=1)
    sin = np.concatenate([-np.sin(angle), np.sin(angle)], axis=1)
    scale = np.array([HD ** -0.5, 1.0], dtype=np.float32)

    def lay(table):
        table = table.astype(np.float32).reshape(2, P, 1, HD) * scale.reshape(1, 1, 2, 1)
        return np.ascontiguousarray(table.transpose(1, 0, 2, 3).reshape(P, 4 * HD).astype(np.float32))

    return lay(cos), lay(sin)


def kernel(**inputs):
    import concourse.bacc as bacc
    from concourse.bass_utils import run_bass_kernel_spmd

    a = {k: np.asarray(v) for k, v in inputs.items()}
    w_gu = np.concatenate([a["L0_ffn_w_gate"], a["L0_ffn_w_up"]], axis=2)
    w_gu = w_gu.reshape(EC, NC, KC, P, 2 * I).transpose(1, 3, 0, 2, 4).reshape(NC, P, EC * KC * 2 * I)
    w_dn = a["L0_ffn_w_down"].reshape(EC, NC, I, DM).transpose(1, 2, 0, 3).reshape(NC, I, EC * DM)
    rope_cos, rope_sin = rope_tables()
    laid = {
        "x": a["L0_attn_hidden_states"].reshape(T, DM),
        "gate_t": a["L0_ffn_gate_w"].T,
        "w_gu": w_gu, "w_lo": w_dn[:, :ILO], "w_hi": w_dn[:, ILO:],
        "sw_gate": a["L0_ffn_sw_gate"], "sw_up": a["L0_ffn_sw_up"], "sw_down": a["L0_ffn_sw_down"],
        "w_qkv": np.concatenate([a["L0_attn_Wq"].T, a["L0_attn_Wk"].T, a["L0_attn_Wv"].T], axis=1),
        "w_o": a["L0_attn_Wo"].T,
        "bias_reversed": a["L0_attn_learnable_bias"][:, ::-1],
        "offset": a["L0_attn_softmax_offset"],
        "rope_cos": rope_cos, "rope_sin": rope_sin,
    }
    nc = bacc.Bacc("TRN2", target_bir_lowering=False, num_devices=1)
    arrays, given = {}, {}
    for name, value in laid.items():
        value = np.ascontiguousarray(value)
        arrays[f"in_{name}"] = value
        given[name] = nc.dram_tensor(f"in_{name}", value.shape, mybir.dt.from_np(value.dtype),
                                     kind="ExternalInput").ap()
    build(nc, given, nc.dram_tensor("out_x", [B, S, DM], F32, kind="ExternalOutput").ap())
    r = run_bass_kernel_spmd(nc, [arrays], core_ids=[0])
    return r.results[0]["out_x"]
```

```python
from contextlib import ExitStack

import numpy as np
import concourse.bass as bass
from concourse import mybir

F32 = mybir.dt.float32
BF16 = mybir.dt.bfloat16
U32 = mybir.dt.uint32
ALU = mybir.AluOpType
ACT = mybir.ActivationFunctionType
AX_X = mybir.AxisListType.X

P = 128
B, S, DM = 4, 256, 256
T = B * S
NT = T // P
KC = DM // P
NH, HD = 32, 8
MAXB = 128
E, TOPK, I = 64, 6, 176
CAP = 32
IS = 2 * I
EC = P // CAP
NC = E // EC
KEPT = 4
RING = 6
AHEAD = 3
ILO, IHI = P, I - P
EARLY = 6
SCRATCH = NT * CAP * E // 2
EPS = 1e-5
PAD = 3.0e38
MASKED = -1.0e30
FAR = 100000.0
NF = 4
RW = NF * EC + 3
NQUAD = T // S * NH // 4
SH = [P, P, IS - 2 * P]


class Chunk:

    def __init__(self, i, scale, c):
        self.i, self.scale, self.c = i, scale, c

    def times(self, k, plus=0):
        return self.i * (self.scale * k) + k * (self.c + plus)

    def rounds(self, of, k, plus=0):
        return self.i * (self.scale // of * k) + k * (self.c // of + plus)

    def after(self, k):
        return Chunk(self.i, self.scale, self.c + k)

    def below(self, k):
        return isinstance(self.i, int) and self.c < k


def wait_count(eng, sem, value):
    if isinstance(value, int) and value <= 0:
        return
    eng.wait_ge(sem, value)


def norm_vector(vec, m, s):
    for t in range(NT):
        vec.bn_stats(m.stats[:, t, :], m.x[:, t, :]).then_inc(s.stats_done, 1)
    for t in range(NT):
        vec.wait_ge(s.stats_done, t + 1)
        vec.bn_aggr(m.moments[:, t, :], m.stats[:, t, :]).then_inc(s.moments_done, 1)
    vec.wait_ge(s.moments_done, NT)
    vec.tensor_scalar(m.var_eps[:, :], m.moments[:, :, 1], EPS, None, ALU.add).then_inc(s.var_ready, 1)
    vec.wait_ge(s.std_ready, 1)
    vec.reciprocal(m.rstd[:, :], m.std[:, :]).then_inc(s.rstd_ready, 1)
    vec.wait_ge(s.rstd_ready, 1)
    for t in range(NT):
        vec.tensor_scalar(m.xn[:, t, :], m.x[:, t, :], m.moments[:, t, 0:1], m.rstd[:, t:t + 1],
                          ALU.subtract, ALU.mult).then_inc(s.xn_ready, 1)
    for half in range(2):
        vec.wait_ge(s.xnT_psum, 2 * half + 2)
        vec.tensor_copy(m.xnT[:, 1, half * 512:half * 512 + 512], m.bank[2 * half + 1][:, :]).then_inc(s.xnT_vec, 1)


def norm_scalar(act, m, s):
    act.wait_ge(s.var_ready, 1)
    act.activation(m.std[:, :], m.var_eps[:, :], ACT.Sqrt).then_inc(s.std_ready, 1)
    for half in range(2):
        act.wait_ge(s.xnT_psum, 2 * half + 1)
        act.copy(m.xnT[:, 0, half * 512:half * 512 + 512], m.bank[2 * half][:, :]).then_inc(s.xnT_act, 1)


def norm_tensor(pe, m, s):
    for half in range(2):
        for q in range(4):
            t = 4 * half + q
            pe.wait_ge(s.xn_ready, t + 1)
            for c in range(KC):
                ins = pe.transpose(m.bank[2 * half + c][:, q * P:q * P + P],
                                   m.xn[:, t, c * P:c * P + P], m.ident[:, :])
                if q == 3:
                    ins.then_inc(s.xnT_psum, 1)


def norm_tile_moments(vec, m, s, t):
    vec.bn_stats(m.stats[:, t, :], m.x[:, t, :]).then_inc(s.stats_done, 1)
    vec.wait_ge(s.stats_done, t + 1)
    vec.bn_aggr(m.moments[:, t, :], m.stats[:, t, :]).then_inc(s.moments_done, 1)
    vec.wait_ge(s.moments_done, t + 1)
    vec.tensor_scalar(m.var_eps[:, t:t + 1], m.moments[:, t, 1:2], EPS, None, ALU.add).then_inc(s.var_ready, 1)


def norm_tile_scale(vec, m, s, t):
    vec.wait_ge(s.std_ready, t + 1)
    vec.reciprocal(m.rstd[:, t:t + 1], m.std[:, t:t + 1]).then_inc(s.rstd_ready, 1)
    vec.wait_ge(s.rstd_ready, t + 1)
    vec.scalar_tensor_tensor(out=m.shift[:, t:t + 1], in0=m.moments[:, t, 0:1], scalar=-1.0, in1=m.rstd[:, t:t + 1],
                             op0=ALU.mult, op1=ALU.mult).then_inc(s.shift_ready, 1)


def norm_tiles_scalar(act, m, s):
    def rows(t):
        act.wait_ge(s.shift_ready, t + 1)
        act.activation(m.xn[:, t, :], m.x[:, t, :], ACT.Identity, bias=m.shift[:, t:t + 1],
                       scale=m.rstd[:, t:t + 1]).then_inc(s.xn_ready, 1)

    def copies(half):
        for c in range(KC):
            act.wait_ge(s.xnT_psum, 2 * half + c + 1)
            act.copy(m.xnT[:, c, half * 512:half * 512 + 512], m.bank[2 * half + c][:, :])\
               .then_inc(s.xnT_act, 1)

    for t in range(NT):
        act.wait_ge(s.var_ready, t + 1)
        act.activation(m.std[:, t:t + 1], m.var_eps[:, t:t + 1], ACT.Sqrt).then_inc(s.std_ready, 1)
        if t > 0:
            rows(t - 1)
        if t == 5:
            copies(0)
    rows(NT - 1)
    copies(1)


def raw_qk(m, t):
    return m.slots[t // 4].gu[:, t % 4 * 2 * DM:(t % 4 + 1) * 2 * DM]


def raw_v(m, t, tiles=1):
    return m.slots[2].gu[:, t * DM:(t + tiles) * DM]


def roped_qk(m):
    return m.scratch[:, 0:NT * 2 * DM].rearrange("p (t q n) -> p t q n", t=NT, q=2)


def padded_qk(m):
    at = 4 * TOPK * DM
    return m.scratch[:, at - 2 * 2 * 2 * P:at].rearrange("p (e t q g r) -> p e t q g r", e=2, t=2, q=2, g=4)


def spread_heads(pool, m, o, j, staged):
    for tile in range(2):
        src = roped_qk(m)[:, bass.ds(j // 2 * 2 + tile, 1), :, bass.ds(o * 64 + j % 2 * 32, 32)]\
            .rearrange("p a q (g d) -> p (a q) g d", g=4)
        pool.tensor_copy(padded_qk(m)[:, j % 2, tile, :, :, 0:HD], src).then_inc(staged, 1)


def rotate_tiles(vec, m, tiles, copied, beside, sin_done, cos_done, qk_ready):
    def add(k):
        roped = roped_qk(m)[:, tiles[k], :, :].rearrange("p q n -> p (q n)")
        vec.wait_ge(sin_done, 2 * k + 2)
        vec.wait_ge(cos_done, k + 1)
        vec.tensor_tensor(roped, roped, by_sine(m, tiles[k]), ALU.add).then_inc(qk_ready, 1)

    for k, t in enumerate(tiles):
        copied(t)
        if k >= 3:
            vec.wait_ge(qk_ready, k - 2)
        rotation_products(vec, m, t, sin_done, cos_done)
        if k > 0:
            add(k - 1)
        else:
            beside()
    add(len(tiles) - 1)


def by_sine(m, t):
    return m.slots[3].gu[:, t % 3 * 2 * DM:(t % 3 + 1) * 2 * DM]


def rotation_products(vec, m, t, sin_done, cos_done):
    half = HD // 2
    by_sin = by_sine(m, t)
    roped = roped_qk(m)[:, t, :, :].rearrange("p q n -> p (q n)")
    src, to_sin, to_cos = (rows.rearrange("p (q h d) -> p q h d", q=2, d=HD)
                           for rows in (raw_qk(m, t), by_sin, roped))
    cos = m.rope_cos[:, t % 2, :, :].unsqueeze(2)
    sin = m.rope_sin[:, t % 2, :, :].unsqueeze(2)
    vec.tensor_tensor(to_sin[:, :, :, 0:half], src[:, :, :, half:HD],
                      sin[:, :, :, 0:half].to_broadcast([P, 2, NH, half]), ALU.mult).then_inc(sin_done, 1)
    vec.tensor_tensor(to_sin[:, :, :, half:HD], src[:, :, :, 0:half],
                      sin[:, :, :, half:HD].to_broadcast([P, 2, NH, half]), ALU.mult).then_inc(sin_done, 1)
    vec.tensor_tensor(to_cos, src, cos.to_broadcast([P, 2, NH, HD]), ALU.mult).then_inc(cos_done, 1)


def project_tiles_scalar(act, m, s, qkv_psum, qkv_copied):
    def turn(t):
        act.wait_ge(s.shift_ready, t + 1)
        act.activation(m.xn[:, t, :], m.x[:, t, :], ACT.Identity, bias=m.shift[:, t:t + 1],
                       scale=m.rstd[:, t:t + 1]).then_inc(s.xn_ready, 1)
        if t >= 2:
            take(t - 2)
        act.wait_ge(s.xnT_psum, t + 1)
        act.copy(m.xnT[:, :, t * P:t * P + P], m.bank[t % 2][:, 0:KC * P].rearrange("p (c n) -> p c n", c=KC))\
           .then_inc(s.xnT_act, 1)

    def take(t):
        act.wait_ge(qkv_psum, t + 1)
        act.copy(raw_qk(m, t), m.bank[2 + t % 2][:, :]).then_inc(qkv_copied, 1)
        act.copy(raw_v(m, t), m.bank[4 + t % 2][:, 0:DM]).then_inc(qkv_copied, 1)

    for t in range(NT):
        act.wait_ge(s.var_ready, t + 1)
        act.activation(m.std[:, t:t + 1], m.var_eps[:, t:t + 1], ACT.Sqrt).then_inc(s.std_ready, 1)
        if t >= 1:
            turn(t - 1)
    turn(NT - 1)
    take(NT - 2)
    take(NT - 1)


def project_tiles_tensor(pe, m, s, attention_loaded, sh_added, qkv_psum, qkv_copied):
    w_qkv, _ = attention_weights(m)
    pe.wait_ge(attention_loaded, 16 * 5)
    pe.wait_ge(sh_added, 4)

    def turn(t):
        pe.wait_ge(s.xn_ready, t + 1)
        for c in range(KC):
            ins = pe.transpose(m.bank[t % 2][:, c * P:c * P + P], m.xn[:, t, c * P:c * P + P], m.ident[:, :])
        ins.then_inc(s.xnT_psum, 1)

    turn(0)
    for t in range(NT):
        if t < NT - 1:
            turn(t + 1)
        pe.wait_ge(s.xnT_act, t + 1)
        if t >= 2:
            pe.wait_ge(qkv_copied, 2 * (t - 1))
        rows = slice(t * P, t * P + P)
        for c in range(KC):
            pe.matmul(m.bank[2 + t % 2][:, :], m.xnT[:, c, rows], w_qkv[:, c, 0:2 * DM],
                      start=(c == 0), stop=(c == KC - 1))
        for c in range(KC):
            ins = pe.matmul(m.bank[4 + t % 2][:, 0:DM], m.xnT[:, c, rows], w_qkv[:, c, 2 * DM:3 * DM],
                            start=(c == 0), stop=(c == KC - 1))
        ins.then_inc(qkv_psum, 1)


class NormSems:

    def __init__(self, sem):
        self.stats_done = sem("stats_done")
        self.moments_done = sem("moments_done")
        self.var_ready = sem("var_ready")
        self.std_ready = sem("std_ready")
        self.rstd_ready = sem("rstd_ready")
        self.shift_ready = sem("shift_ready")
        self.xn_ready = sem("xn_ready")
        self.xnT_psum = sem("xnT_psum")
        self.xnT_vec = sem("xnT_vec")
        self.xnT_act = sem("xnT_act")


def load_expert_chunk(sp, w, slot, loaded, n):
    chunk = slice(n, n + 1)
    sp.dma_start(slot.gu, w.w_gu[chunk].squeeze(0)).then_inc(loaded, 16)
    sp.dma_start(slot.lo, w.w_lo[chunk].squeeze(0)).then_inc(loaded, 16)
    sp.dma_start(slot.hi, w.w_hi[chunk].squeeze(0)).then_inc(loaded, 16)


def first_chunks(sp, w, m, loaded):
    for n in range(KEPT):
        load_expert_chunk(sp, w, m.slots[n], loaded[n], n)


def zero_table(eng, w, m, tiles, table_zeroed):
    table_tiles = w.table.rearrange("(t p k) d -> t p k d", p=P, k=TOPK)
    for t in tiles:
        eng.dma_start(table_tiles[t], m.zeros[:, :].unsqueeze(1).to_broadcast([P, TOPK, DM]))\
           .then_inc(table_zeroed, 16)


def feed_forward(nc, w, m, sems, tag, weights_loaded, gathered, scattered, table_zeroed, first,
                 attention_loaded, bias_stored):
    last = not first
    with ExitStack() as ctx:
        def sb(name, shape, dt=F32):
            return ctx.enter_context(nc.sbuf_tensor(f"{tag}_{name}", shape, dt))

        def sem(name):
            return sems(name)

        flat_onehot = m.scratch[:, :]
        onehot = flat_onehot.bitcast(BF16).rearrange("p (t c e) -> p t c e", t=NT, c=CAP)
        width, down_width = EC * KC * 2 * I, EC * DM
        slots = m.slots + [
            WeightSlot(sb("w_gu4", [P, width]), sb("w_lo4", [ILO, down_width]), sb("w_hi4", [IHI, down_width])),
            WeightSlot(flat_onehot[:, 0:width], flat_onehot[:, width:width + down_width],
                       flat_onehot[0:IHI, width + down_width:width + 2 * down_width])]
        choice_rows = [flat_onehot[:, i * TOPK * DM:(i + 1) * TOPK * DM] for i in range(4)]
        facts = sb("facts", [P, NT, NC, RW], BF16)
        logits = sb("logits", [P, NT, E + 2])
        replaced = sb("replaced", [P, NT, E + 2])
        top = sb("top", [P, NT, 8])
        chosen = sb("chosen", [P, NT, E], BF16)
        shifted = sb("shifted", [P, NT, E])
        expl = sb("expl", [P, NT, E])
        esum = sb("esum", [P, NT])
        rsum = sb("rsum", [P, NT])
        rank = sb("rank", [P, NT * E])
        unchosen = sb("unchosen", [P, NT * E])
        place = sb("place", [P, NT * E], BF16)
        slot_sums = sb("slot_sums", [P, NC, RW])
        own = sb("own", [P, NC, NF * EC])
        own_facts = sb("own_facts", [P, NC, NF])
        slot_weight = sb("slot_weight", [P, NC])
        slot_token = sb("slot_token", [P, NC])
        slot_far = sb("slot_far", [P, NC])
        slot_row = sb("slot_row", [P, NC])
        gather_index = sb("gather_index", [P, NC], U32)
        scatter_index = sb("scatter_index", [P, NC], U32)
        sh_silu = sb("sh_silu", [P, 2, 512])
        sh_hT = sb("sh_hT", [P, 3, 512])
        xg = [rank[:, 0:DM], rank[:, DM:2 * DM], unchosen[:, 0:DM]]
        xgT = sb("xgT", [P, 2, KC * P])
        gsilu = sb("gsilu", [P, 2, I])
        h = sb("h", [P, 2, I])
        hT = sb("hT", [P, 2, 2 * P])
        y = sb("y", [P, 2, DM])
        total = y

        s = NormSems(sem)
        after = NormSems(lambda name: sem(f"after_{name}")) if first else None
        (x_loaded, small_loaded, consts_ready, zeros_ready, pads_ready, xn_stored, logits_psum,
         logits_sb, top_ready, replaced_ready, chosen_ready, shifted_ready, expl_ready, esum_ready, rsum_ready,
         probs_ready, weight_ready, scan_ready, counts_psum, unchosen_ready, place_ready, onehot_ready, fact_ready,
         rest_ready, slots_psum, slot_sums_ready, own_ready, slot_step, slots_ready, sh_up_psum, sh_silu_ready,
         sh_hT_ready, sh_y_psum, sh_added, xgT_psum, xgT_ready, gu_psum, silu_ready, h_ready, hT_psum, hT_ready,
         y_psum, y_ready, total_ready, x_ready, out_stored, mask_ready,
         rows_masked, rows_loaded, qkv_psum, qkv_copied, sin_done, cos_done, qk_ready, pad_ready,
         staged) = [sem(n) for n in (
             "x_loaded small_loaded consts_ready zeros_ready pads_ready xn_stored logits_psum "
             "logits_sb top_ready replaced_ready chosen_ready shifted_ready expl_ready esum_ready rsum_ready "
             "probs_ready weight_ready scan_ready counts_psum unchosen_ready place_ready onehot_ready fact_ready "
             "rest_ready slots_psum slot_sums_ready own_ready slot_step slots_ready sh_up_psum sh_silu_ready "
             "sh_hT_ready sh_y_psum sh_added xgT_psum xgT_ready gu_psum silu_ready h_ready hT_psum hT_ready "
             "y_psum y_ready total_ready x_ready out_stored mask_ready "
             "rows_masked rows_loaded qkv_psum qkv_copied sin_done cos_done qk_ready pad_ready "
             "staged").split()]
        choices_loaded = [sem(f"choices_loaded{i}") for i in range(4)]

        bank = m.bank
        logits_bank = bank[4][:, :].rearrange("p (t e) -> p t e", e=E)
        counts_bank = bank[5]
        slots_bank = bank[6]
        sh_up_banks = [(bank[0], bank[1]), (bank[2], bank[3]), (bank[0], bank[1])] + [(bank[4], bank[5])] * 3
        sh_y_banks = [(bank[4], bank[7]), (bank[4], bank[5])]
        rows_banks, gu_banks, y_banks = bank[0:2], bank[2:4], bank[6:8]
        xn_rows = w.xn_dram
        table_tiles = w.table.rearrange("(t p k) d -> t p k d", p=P, k=TOPK)
        out_tiles = w.out.rearrange("b s d -> (b s) d").rearrange("(t p) d -> t p d", p=P)
        x_tiles = w.x.rearrange("(t p) d -> t p d", p=P)
        xn_tiles = w.xn_dram.rearrange("(t p) d -> t p d", p=P)

        block = ctx.enter_context(nc.Block())

        @block.sync
        def _(sp):
            if first:
                for t in range(NT):
                    sp.dma_start(m.x[:, t, :], x_tiles[t]).then_inc(x_loaded, 16)
                sp.dma_start(m.gate[:, :, :], w.gate_t.rearrange("(c p) e -> p c e", p=P)).then_inc(small_loaded, 16)
                sp.dma_start(m.sh_gate[:, :, :], w.sw_gate.rearrange("(c p) i -> p c i", p=P)).then_inc(small_loaded, 16)
                sp.dma_start(m.sh_up[:, :, :], w.sw_up.rearrange("(c p) i -> p c i", p=P)).then_inc(small_loaded, 16)
                sp.dma_start(m.sh_down[:, 0:2, :],
                             w.sw_down[0:2 * P, :].rearrange("(c p) d -> p c d", p=P)).then_inc(small_loaded, 16)
                sp.dma_start(m.sh_down[0:SH[2], 2, :], w.sw_down[2 * P:IS, :]).then_inc(small_loaded, 16)
                sp.dma_start(m.rope_cos[:, :, :, :].rearrange("p t q c -> p (t q c)"), w.rope_cos)\
                  .then_inc(attention_loaded, 16)
                sp.dma_start(m.rope_sin[:, :, :, :].rearrange("p t q c -> p (t q c)"), w.rope_sin)\
                  .then_inc(attention_loaded, 16)
                sp.dma_start(m.offset[:, :], w.offset.partition_broadcast(P)).then_inc(attention_loaded, 16)
                first_chunks(sp, w, m, weights_loaded)
                sp.wait_ge(rows_masked, 2)
                sp.dma_start(m.bias_rows[:, P:2 * P], w.bias_reversed).then_inc(rows_loaded, 16)
            else:
                load_expert_chunk(sp, w, slots[4], weights_loaded[4], 4)
            for t in range(NT):
                if first:
                    sp.wait_ge(s.xn_ready, t + 1)
                sp.dma_start(xn_tiles[t], m.xn[:, t, :]).then_inc(xn_stored, 16)
            if first:
                sp.wait_ge(gathered[AHEAD - 1], 16)
                zero_table(sp, w, m, range(NT // 2, NT), table_zeroed)
                load_expert_chunk(sp, w, slots[4], weights_loaded[4], 4)
            sp.wait_ge(slots_psum, 1)
            if first:
                w_qkv, w_o = attention_weights(m)
                sp.dma_start(w_qkv, w.w_qkv.rearrange("(c p) n -> p c n", p=P)).then_inc(attention_loaded, 16)
                sp.dma_start(w_o, w.w_o.rearrange("(c p) n -> p c n", p=P)).then_inc(attention_loaded, 16)
            load_expert_chunk(sp, w, slots[5], weights_loaded[5], 5)
            for n in range(RING, NC):
                sp.wait_ge(weights_loaded[n % RING], 48 * (n // RING))
                sp.wait_ge(y_psum, n + 1 - RING)
                load_expert_chunk(sp, w, slots[n % RING], weights_loaded[n % RING], n)
            for p in range(2):
                sp.wait_ge(scattered[p], 16 * (NC // 2))
            for t in range(NT):
                if t >= 4:
                    sp.wait_ge(total_ready, t - 3)
                sp.dma_start(choice_rows[t % 4], table_tiles[t].rearrange("p k d -> p (k d)"))\
                  .then_inc(choices_loaded[t % 4], 16)
            if first:
                sp.wait_ge(rows_loaded, 16)
                sp.dma_start(w.bias_dram.rearrange("p h r -> h p r"),
                             m.bias_rows[:, :].unsqueeze(1).to_broadcast([NH, P, 3 * P])).then_inc(bias_stored, 16)
            if last:
                for t in range(NT):
                    sp.wait_ge(x_ready, t + 1)
                    sp.dma_start(out_tiles[t], m.x[:, t, :]).then_inc(out_stored, 16)
                sp.wait_ge(out_stored, 16 * NT)

        @block.gpsimd
        def _(pool):
            if first:
                pool.memset(m.ident[:, :], 0.0).then_inc(zeros_ready, 1)
                pool.memset(m.triangle[:, :], 1.0).then_inc(zeros_ready, 1)
                pool.memset(m.resets[:, :, :], 1.0).then_inc(zeros_ready, 1)
                pool.memset(m.zeros[:, :], 0.0).then_inc(zeros_ready, 1)
                pool.wait_ge(zeros_ready, 4)
                pool.affine_select(out=m.ident[:, :], in_=m.ident[:, :], compare_op=ALU.not_equal, fill=1.0,
                                   base=0, pattern=[[-1, P]], channel_multiplier=1).then_inc(consts_ready, 1)
                pool.affine_select(out=m.triangle[:, :], in_=m.triangle[:, :], compare_op=ALU.is_gt, fill=0.0,
                                   base=0, pattern=[[1, P]], channel_multiplier=-1).then_inc(consts_ready, 1)
                pool.memset(m.ones[:, :], 1.0).then_inc(consts_ready, 1)
                pool.memset(m.resets[:, :, 0:1], 0.0).then_inc(consts_ready, 1)
                pool.wait_ge(consts_ready, 1)
                pool.tensor_copy(m.by_expert[:, :].rearrange("p (e c) -> p e c", e=EC),
                                 m.ident[:, :].rearrange("p (c e) -> p e c", e=EC)).then_inc(consts_ready, 1)
                pool.memset(m.bias_rows[:, 0:P], 0.0).then_inc(rows_masked, 1)
                pool.memset(m.bias_rows[:, 2 * P:3 * P], MASKED).then_inc(rows_masked, 1)
            token = facts[:, :, :, NF * EC:]
            pool.iota(token[:, :, :, 0], pattern=[[0, NT], [0, NC]], base=0, channel_multiplier=1,
                      allow_small_or_imprecise_dtypes=True).then_inc(rest_ready, 1)
            pool.iota(token[:, :, :, 1], pattern=[[P, NT], [0, NC]], base=0, channel_multiplier=0,
                      allow_small_or_imprecise_dtypes=True).then_inc(rest_ready, 1)
            pool.memset(token[:, :, :, 2], 1.0).then_inc(rest_ready, 1)

            weight = expl[:, :, :].rearrange("p t (e n) -> p t n e", n=NC)

            pool.wait_ge(scan_ready, 1)
            pool.tensor_tensor(facts[:, :, :, 0:EC], rank[:, :].rearrange("p (t e n) -> p t n e", n=NC, e=EC),
                              chosen[:, :, :].rearrange("p t (e n) -> p t n e", n=NC),
                              ALU.subtract).then_inc(fact_ready, 1)
            for part in range(1, NF):
                pool.wait_ge(probs_ready, 2 * part - 1 if part > 1 else 1)
                f = facts[:, :, :, part * EC:(part + 1) * EC]
                pool.tensor_copy(f, weight).then_inc(fact_ready, 1)
                if part < NF - 1:
                    pool.wait_ge(fact_ready, part + 1)
                    pool.tensor_tensor(weight, weight, f, ALU.subtract).then_inc(probs_ready, 2)

            pool.wait_ge(xn_stored, 16 * NT)
            pool.wait_ge(slots_ready, 2)

            def gather(n):
                if n >= AHEAD:
                    pool.wait_ge(xgT_psum, n + 1 - AHEAD)
                pool.indirect_dma_start(
                    out=xg[n % AHEAD], out_offset=None, in_=xn_rows,
                    in_offset=bass.IndirectOffsetOnAxis(ap=gather_index[:, n:n + 1], axis=0),
                    bounds_check=T - 1, oob_is_err=False).then_inc(gathered[n % AHEAD], 16)

            for n in range(AHEAD):
                gather(n)
            for n in range(NC):
                if n + AHEAD < NC:
                    gather(n + AHEAD)
                pool.wait_ge(y_ready, n + 1)
                if n == 0:
                    pool.wait_ge(table_zeroed, 16 * NT)
                pool.indirect_dma_start(
                    out=w.table, out_offset=bass.IndirectOffsetOnAxis(ap=scatter_index[:, n:n + 1], axis=0),
                    in_=y[:, n % 2, :], in_offset=None,
                    bounds_check=T * TOPK - 1, oob_is_err=False).then_inc(scattered[n % 2], 16)
            if first:
                for t in range(NT):
                    pool.wait_ge(total_ready, t + 1)
                    pool.tensor_tensor(m.x[:, t, :], total[:, t % 2, :], m.x[:, t, :], ALU.add).then_inc(x_ready, 1)
                pool.memset(padded_qk(m), 0.0).then_inc(pad_ready, 1)
                pool.wait_ge(pad_ready, 1)
                pool.wait_ge(qk_ready, 2)
                for j in range(2):
                    spread_heads(pool, m, 0, j, staged)

        @block.scalar
        def _(act):
            if first:
                norm_scalar(act, m, s)
                act.wait_ge(zeros_ready, 4)
                zero_table(act, w, m, range(NT // 2), table_zeroed)
            act.wait_ge(logits_psum, 1)
            act.copy(logits[:, :, 0:E], logits_bank).then_inc(logits_sb, 1)
            act.wait_ge(shifted_ready, 1)
            act.activation(expl[:, :, :], shifted[:, :, :], ACT.Exp).then_inc(expl_ready, 1)

            def shared_silu(k):
                act.wait_ge(sh_up_psum, k + 1)
                if k >= 2:
                    act.wait_ge(sh_hT_ready, k - 1)
                rows = SH[k % 3]
                act.activation(sh_silu[0:rows, k % 2, :], sh_up_banks[k][0][0:rows, :], ACT.Silu)\
                   .then_inc(sh_silu_ready, 1)

            for k in range(3):
                shared_silu(k)

            def gate(n):
                par = n.c % 2
                act.wait_ge(gu_psum, n.times(1, 1))
                wait_count(act, h_ready, n.times(1, -1))
                act.activation(gsilu[:, par, :], gu_banks[par][:, 0:I], ACT.Silu).then_inc(silu_ready, 1)

            def weigh(n):
                par = n.c % 2
                act.wait_ge(y_psum, n.times(1, 1))
                wait_count(act, scattered[par], n.rounds(2, 16))
                act.activation(y[:, par, :], y_banks[par][:, 0:DM], ACT.Copy,
                               scale=slot_weight[:, bass.ds(n.times(1), 1)]).then_inc(y_ready, 1)

            def step(n):
                gate(n)
                if not n.below(1):
                    weigh(n.after(-1))

            for c in range(3):
                step(Chunk(0, 2, c))
                shared_silu(3 + c)
            with act.Fori(0, (NC - 4) // 2) as i:
                for c in (3, 4):
                    step(Chunk(i, 2, c))
            step(Chunk(0, 2, NC - 1))
            weigh(Chunk(0, 2, NC - 1))
            if first:
                project_tiles_scalar(act, m, after, qkv_psum, qkv_copied)

        @block.vector
        def _(vec):
            vec.memset(logits[:, :, E:E + 2], PAD).then_inc(pads_ready, 1)
            if first:
                vec.memset(m.own_mask[:, :], 0.0).then_inc(mask_ready, 1)
                vec.wait_ge(mask_ready, 1)
                for e in range(EC):
                    vec.memset(m.own_mask[e * CAP:(e + 1) * CAP, e:e + 1], 1.0).then_inc(mask_ready, 1)
                vec.wait_ge(mask_ready, 1 + EC)
                vec.wait_ge(x_loaded, 16 * NT)
                norm_vector(vec, m, s)
            vec.wait_ge(logits_sb, 1)
            vec.wait_ge(pads_ready, 1)
            for t in range(NT):
                vec.max(top[:, t, :], logits[:, t, :]).then_inc(top_ready, 1)
            for t in range(NT):
                vec.wait_ge(top_ready, t + 1)
                vec.match_replace(replaced[:, t, :], top[:, t, :], logits[:, t, :], -PAD).then_inc(replaced_ready, 1)
            vec.wait_ge(replaced_ready, NT)
            vec.tensor_scalar(chosen[:, :, :], replaced[:, :, 0:E], -PAD, None, ALU.is_equal).then_inc(chosen_ready, 1)
            vec.tensor_tensor(shifted[:, :, :], logits[:, :, 0:E], top[:, :, 2:3].to_broadcast([P, NT, E]),
                              ALU.subtract).then_inc(shifted_ready, 1)
            vec.wait_ge(chosen_ready, 1)
            flat_chosen = chosen[:, :, :].rearrange("p t e -> p (t e)")
            vec.tensor_tensor_scan(rank[:, :], m.resets[:, :, :].rearrange("p t e -> p (t e)"), flat_chosen, 0.0,
                                   ALU.mult, ALU.add).then_inc(scan_ready, 1)
            vec.tensor_scalar(unchosen[:, :], flat_chosen, -64.0, 64.0, ALU.mult, ALU.add)\
               .then_inc(unchosen_ready, 1)
            def shared_hidden(k):
                rows = SH[k % 3]
                vec.wait_ge(sh_silu_ready, k + 1)
                if k >= 3:
                    vec.wait_ge(sh_y_psum, 1)
                vec.tensor_tensor(sh_hT[0:rows, k % 3, :], sh_up_banks[k][1][0:rows, :],
                                  sh_silu[0:rows, k % 2, :], ALU.mult).then_inc(sh_hT_ready, 1)

            def shared_add(half):
                vec.wait_ge(sh_y_psum, half + 1)
                for b in range(2):
                    tiles = m.x[:, 4 * half + 2 * b:4 * half + 2 * b + 2, :].rearrange("p t d -> p (t d)")
                    vec.scalar_tensor_tensor(out=tiles, in0=sh_y_banks[half][b][:, :], scalar=0.5, in1=tiles,
                                             op0=ALU.mult, op1=ALU.add).then_inc(sh_added, 1)

            vec.wait_ge(expl_ready, 1)
            vec.tensor_reduce(esum[:, :], expl[:, :, :], AX_X, ALU.add).then_inc(esum_ready, 1)
            vec.wait_ge(esum_ready, 1)
            vec.reciprocal(rsum[:, :], esum[:, :]).then_inc(rsum_ready, 1)
            vec.wait_ge(rsum_ready, 1)
            vec.tensor_tensor(expl[:, :, :], expl[:, :, :], rsum[:, :].unsqueeze(2).to_broadcast([P, NT, E]),
                              ALU.mult).then_inc(probs_ready, 1)

            vec.wait_ge(counts_psum, 1)
            vec.wait_ge(unchosen_ready, 1)
            vec.scalar_tensor_tensor(out=place[:, :], in0=counts_bank[:, :], scalar=64.0, in1=unchosen[:, :],
                                     op0=ALU.min, op1=ALU.add).then_inc(place_ready, 1)
            vec.wait_ge(place_ready, 1)
            for c in range(CAP):
                vec.tensor_scalar(onehot[:, :, c, :], place[:, :].rearrange("p (t e) -> p t e", e=E), float(c), None,
                                  ALU.is_equal)\
                   .then_inc(onehot_ready, 1)
                if c in (7, 15):
                    shared_hidden(c // 8)
            shared_hidden(2)
            for bank_of_slots in (slots_bank, counts_bank):
                vec.wait_ge(slots_psum, 1 if bank_of_slots is slots_bank else 2)
                vec.tensor_copy(slot_sums[:, :, :], bank_of_slots[:, 0:NC * RW].rearrange("p (n r) -> p n r", r=RW))\
                   .then_inc(slot_sums_ready, 1)
            vec.wait_ge(slot_sums_ready, 2)
            vec.tensor_tensor(own[:, :, :].rearrange("p n (f e) -> p n f e", e=EC),
                              slot_sums[:, :, 0:NF * EC].rearrange("p n (f e) -> p n f e", e=EC),
                              m.own_mask[:, :].unsqueeze(1).unsqueeze(1).to_broadcast([P, NC, NF, EC]),
                              ALU.mult).then_inc(own_ready, 1)
            vec.wait_ge(own_ready, 1)
            vec.tensor_reduce(own_facts[:, :, :], own[:, :, :].rearrange("p n (f e) -> p n f e", e=EC), AX_X,
                              ALU.add).then_inc(slot_step, 1)
            vec.tensor_reduce(slot_token[:, :], slot_sums[:, :, NF * EC:NF * EC + 2], AX_X, ALU.add)\
               .then_inc(slot_step, 1)
            vec.tensor_scalar(slot_far[:, :], slot_sums[:, :, NF * EC + 2], -FAR, FAR, ALU.mult, ALU.add)\
               .then_inc(slot_step, 1)
            vec.wait_ge(slot_step, 3)
            vec.tensor_reduce(slot_weight[:, :], own_facts[:, :, 1:NF], AX_X, ALU.add).then_inc(slot_step, 1)
            vec.tensor_copy(gather_index[:, :], slot_token[:, :]).then_inc(slots_ready, 1)
            vec.scalar_tensor_tensor(out=slot_row[:, :], in0=slot_token[:, :], scalar=float(TOPK),
                                     in1=own_facts[:, :, 0], op0=ALU.mult, op1=ALU.add).then_inc(slot_step, 1)
            vec.wait_ge(slot_step, 5)
            vec.tensor_tensor(slot_row[:, :], slot_row[:, :], slot_far[:, :], ALU.add).then_inc(slot_step, 1)
            vec.tensor_scalar(slot_weight[:, :], slot_weight[:, :], 0.5, None, ALU.mult).then_inc(slot_step, 1)
            vec.wait_ge(slot_step, 7)
            vec.tensor_copy(scatter_index[:, :], slot_row[:, :]).then_inc(slots_ready, 1)

            shared_add(0)

            def take_rows(n):
                par = n.c % 2
                vec.wait_ge(xgT_psum, n.times(1, 1))
                wait_count(vec, gu_psum, n.times(1, -1))
                vec.tensor_copy(xgT[:, par, :], rows_banks[par][:, 0:KC * P]).then_inc(xgT_ready, 1)

            def multiply(n):
                par = n.c % 2
                vec.wait_ge(silu_ready, n.times(1, 1))
                wait_count(vec, hT_psum, n.times(1, -1))
                vec.tensor_tensor(h[:, par, :], gu_banks[par][:, I:2 * I], gsilu[:, par, :], ALU.mult)\
                   .then_inc(h_ready, 1)

            def take_hidden(n):
                par = n.c % 2
                vec.wait_ge(hT_psum, n.times(1, 1))
                wait_count(vec, y_psum, n.times(1, -1))
                vec.tensor_copy(hT[:, par, 0:P], rows_banks[par][:, 2 * P:3 * P]).then_inc(hT_ready, 1)
                vec.tensor_copy(hT[0:IHI, par, P:2 * P], rows_banks[par][0:IHI, 3 * P:4 * P]).then_inc(hT_ready, 1)

            def step(n):
                multiply(n)
                if n.below(NC - 1) or not isinstance(n.i, int):
                    take_rows(n.after(1))
                take_hidden(n)

            take_rows(Chunk(0, 2, 0))
            for c in range(3):
                step(Chunk(0, 2, c))
                shared_hidden(3 + c)
            with vec.Fori(0, (NC - 4) // 2) as i:
                for c in (3, 4):
                    step(Chunk(i, 2, c))
            step(Chunk(0, 2, NC - 1))

            shared_add(1)
            vec.wait_ge(sh_added, 4)
            for t in range(NT):
                vec.wait_ge(choices_loaded[t % 4], 16 * (t // 4 + 1))
                if t >= 2:
                    vec.wait_ge(x_ready, t - 1)
                vec.tensor_reduce(total[:, t % 2, :], choice_rows[t % 4].rearrange("p (k d) -> p d k", k=TOPK),
                                  AX_X, ALU.add).then_inc(total_ready, 1)
                if last:
                    vec.wait_ge(total_ready, t + 1)
                    vec.tensor_tensor(m.x[:, t, :], total[:, t % 2, :], m.x[:, t, :], ALU.add).then_inc(x_ready, 1)
                elif t > 0:
                    vec.wait_ge(x_ready, t)
                    norm_tile_moments(vec, m, after, t - 1)
                    if t > 1:
                        norm_tile_scale(vec, m, after, t - 2)
            if first:
                vec.wait_ge(x_ready, NT)
                norm_tile_moments(vec, m, after, NT - 1)
                norm_tile_scale(vec, m, after, NT - 2)
                vec.wait_ge(attention_loaded, 16 * 5)
                rotate_tiles(vec, m, range(EARLY),
                             lambda t: vec.wait_ge(qkv_copied, 2 * (t + 1)),
                             lambda: norm_tile_scale(vec, m, after, NT - 1), sin_done, cos_done, qk_ready)
                vec.wait_ge(qk_ready, EARLY)

        @block.tensor
        def _(pe):
            if first:
                pe.wait_ge(consts_ready, 5)
                norm_tensor(pe, m, s)
                pe.wait_ge(s.xnT_vec, 2)
                pe.wait_ge(s.xnT_act, 2)
                pe.wait_ge(small_loaded, 16 * 5)
            for t in range(NT):
                for c in range(KC):
                    ins = pe.matmul(logits_bank[:, t, :], m.xnT[:, c, t * P:t * P + P], m.gate[:, c, :],
                                    start=(c == 0), stop=(c == KC - 1))
            ins.then_inc(logits_psum, 1)

            def shared_up(k):
                half, part = k // 3, k % 3
                cols = slice(part * P, part * P + SH[part])
                if k >= 2:
                    pe.wait_ge(sh_hT_ready, k if k >= 4 else k - 1)
                for weights, to in zip((m.sh_gate, m.sh_up), sh_up_banks[k]):
                    for c in range(KC):
                        ins = pe.matmul(to[0:SH[part], :], weights[:, c, cols],
                                        m.xnT[:, c, half * 512:half * 512 + 512], start=(c == 0), stop=(c == KC - 1))
                ins.then_inc(sh_up_psum, 1)

            def shared_down(half):
                pe.wait_ge(sh_hT_ready, 3 * half + 3)
                for t in range(4):
                    to = sh_y_banks[half][t // 2][:, t % 2 * DM:t % 2 * DM + DM]
                    for part in range(3):
                        ins = pe.matmul(to, sh_hT[0:SH[part], part, t * P:t * P + P],
                                        m.sh_down[0:SH[part], part, :], start=(part == 0), stop=(part == 2))
                ins.then_inc(sh_y_psum, 1)

            shared_up(0)
            pe.wait_ge(chosen_ready, 1)
            for t in range(NT):
                to = counts_bank[:, t * E:t * E + E]
                for before in range(t):
                    pe.matmul(to, m.ones[:, :], chosen[:, before, :], start=(before == 0), stop=False)
                ins = pe.matmul(to, m.triangle[:, :], chosen[:, t, :], start=(t == 0), stop=True)
            ins.then_inc(counts_psum, 1)
            shared_up(1)
            shared_up(2)
            pe.wait_ge(onehot_ready, CAP)
            pe.wait_ge(fact_ready, NF)
            pe.wait_ge(rest_ready, 3)
            for n in range(NC):
                for t in range(NT):
                    ins = pe.matmul(slots_bank[:, n * RW:n * RW + RW],
                                    onehot[:, t, :, :].rearrange("p c (e n) -> p n (c e)", n=NC)[:, n, :],
                                    facts[:, t, n, :], start=(t == 0), stop=(t == NT - 1))
            ins.then_inc(slots_psum, 1)
            pe.wait_ge(slot_sums_ready, 1)
            pe.matmul(counts_bank[:, 0:NC * RW], m.by_expert[:, :], slot_sums[:, :, :].rearrange("p n r -> p (n r)"),
                      start=True, stop=True).then_inc(slots_psum, 1)
            pe.wait_ge(logits_sb, 1)
            shared_down(0)

            def rows_in(n):
                par = n.c % 2
                pe.wait_ge(gathered[n.c % AHEAD], n.rounds(AHEAD, 16, 1))
                wait_count(pe, xgT_ready, n.times(1, -1))
                for c in range(KC):
                    ins = pe.transpose(rows_banks[par][:, c * P:c * P + P], xg[n.c % AHEAD][:, c * P:c * P + P],
                                       m.ident[:, :])
                ins.then_inc(xgT_psum, 1)

            def up(n):
                par, slot = n.c % 2, n.c % RING
                pe.wait_ge(xgT_ready, n.times(1, 1))
                pe.wait_ge(weights_loaded[slot], n.rounds(RING, 48, 1))
                wait_count(pe, h_ready, n.times(1, -1))
                wgu = slots[slot].gu.rearrange("p (e c i) -> p e c i", c=KC, i=2 * I)
                for e in range(EC):
                    rows = slice(e * CAP, (e + 1) * CAP)
                    for c in range(KC):
                        ins = pe.matmul(gu_banks[par][rows, 0:2 * I], xgT[:, par, c * P + e * CAP:c * P + (e + 1) * CAP],
                                        wgu[:, e, c, :], start=(c == 0), stop=(c == KC - 1))
                ins.then_inc(gu_psum, 1)

            def hidden(n):
                par = n.c % 2
                pe.wait_ge(h_ready, n.times(1, 1))
                wait_count(pe, hT_ready, n.times(2, -1))
                pe.transpose(rows_banks[par][:, 2 * P:3 * P], h[:, par, 0:ILO], m.ident[:, :])
                pe.transpose(rows_banks[par][0:IHI, 3 * P:4 * P], h[:, par, ILO:I], m.ident[:, :]).then_inc(hT_psum, 1)

            def down(n):
                par, slot = n.c % 2, n.c % RING
                pe.wait_ge(hT_ready, n.times(2, 1))
                wait_count(pe, y_ready, n.times(1, -1))
                for e in range(EC):
                    rows = slice(e * CAP, (e + 1) * CAP)
                    wide = slice(e * DM, (e + 1) * DM)
                    pe.matmul(y_banks[par][rows, 0:DM], hT[:, par, e * CAP:(e + 1) * CAP], slots[slot].lo[:, wide],
                              start=True, stop=False)
                    ins = pe.matmul(y_banks[par][rows, 0:DM], hT[0:IHI, par, P + e * CAP:P + (e + 1) * CAP],
                                    slots[slot].hi[:, wide], start=False, stop=True)
                ins.then_inc(y_psum, 1)

            def step(n):
                up(n)
                if not n.below(1):
                    down(n.after(-1))
                if n.below(NC - 1) or not isinstance(n.i, int):
                    rows_in(n.after(1))
                hidden(n)

            rows_in(Chunk(0, RING, 0))
            for c in range(3):
                step(Chunk(0, RING, c))
                if c == 0:
                    pe.wait_ge(slot_sums_ready, 2)
                    pe.wait_ge(sh_added, 2)
                shared_up(3 + c)
            with pe.Fori(0, (NC - 4) // RING) as i:
                for c in range(3, RING + 3):
                    step(Chunk(i, RING, c))
            step(Chunk(0, RING, NC - 1))
            down(Chunk(0, RING, NC - 1))
            shared_down(1)
            if first:
                project_tiles_tensor(pe, m, after, attention_loaded, sh_added, qkv_psum, qkv_copied)


def attention_weights(m):
    at = SCRATCH - KC * 4 * DM
    return (m.scratch[:, at:at + KC * 3 * DM].rearrange("p (c n) -> p c n", c=KC),
            m.scratch[:, at + KC * 3 * DM:].rearrange("p (c n) -> p c n", c=KC))


def attention(nc, w, m, used, next_weights_loaded, next_table_zeroed, bias_stored):
    with ExitStack() as ctx:
        def sb(name, shape, dt=F32):
            return ctx.enter_context(nc.sbuf_tensor(f"at_{name}", shape, dt))

        def sem(name):
            return ctx.enter_context(nc.semaphore(f"at_{name}"))

        w_qkv, w_o = attention_weights(m)
        v = sb("v", [P, NT, NH, HD + 1])
        bias = sb("bias", [P, 2, 8, S])
        neg_offset = sb("neg_offset", [P, NH])
        qk_pad = padded_qk(m)
        v_quad = sb("v_quad", [P, 2, 2, 4, 32])
        qkT = sb("qkT", [P, 2, 2, 2, P])
        neg_scores = w_qkv.rearrange("p c n -> p (c n)").rearrange("p (k j) -> p k j", k=4)
        neg_max = sb("neg_max", [P, 8, 2])
        probs = sb("probs", [P, 8, P + S])
        probsT = sb("probsT", [P, 8, P + S])
        heads_outT = m.scratch[:, NT * 2 * DM:NT * 2 * DM + 2 * S].rearrange("p (q t) -> p q t", q=2)
        off_shift = sb("off_shift", [P, 2, 2, 4])
        off_exp = sb("off_exp", [P, 2, 2, 4])
        denom = sb("denom", [P, 2, 4])
        rdenom = sb("rdenom", [P, 2, 4])
        heads_out = sb("heads_out", [P, 2, 2, 4 * HD])
        attn, attnT = m.xn, m.xnT

        s = NormSems(sem)
        (pad_ready, neg_off_ready,
         ones_ready, cos_done, sin_done, qk_ready, v_ready, staged, v_staged, qkT_psum, qkT_ready,
         s_psum, scored, exp_done, pT_psum, pT_vec, pT_act, pv_psum, outT_ready, turned_psum, off_in, off_ready,
         den_ready, rden_ready,
         quad_out, attn_stored, attnT_psum, attnT_vec, attnT_act, o_psum, x_ready) = [sem(n) for n in (
             "pad_ready neg_off_ready "
             "ones_ready cos_done sin_done qk_ready v_ready staged v_staged qkT_psum qkT_ready "
             "s_psum scored exp_done pT_psum pT_vec pT_act pv_psum outT_ready turned_psum off_in off_ready "
             "den_ready rden_ready "
             "quad_out attn_stored attnT_psum attnT_vec attnT_act o_psum x_ready").split()]
        bias_loaded = [sem(f"bias_loaded{i}") for i in range(2)]
        bank = m.bank
        score_banks, probs_banks, out_bank, qk_bank = bank[0:4], bank[4:6], bank[6], bank[7]
        outT_sums = out_bank[:, 0:S]
        sums = out_bank[:, S:2 * S].rearrange("p (t g d) -> p t g d", t=2, g=4)

        block = ctx.enter_context(nc.Block())

        @block.sync
        def _(sp):
            sp.wait_ge(bias_stored, 16)
            for o in range(NH // 8):
                wait_count(sp, scored, (o - 1) * B * 8 * 2)
                skewed = bass.AP(w.bias_dram.tensor, o * 8 * 3 * P + P - 1, [[NH * 3 * P - 1, P], [3 * P, 8], [1, S]])
                sp.dma_start(bias[:, o % 2, :, :], skewed).then_inc(bias_loaded[o % 2], 16)
                if o == 1:
                    sp.wait_ge(qk_ready, NT - EARLY)
                    sp.wait_ge(v_ready, B)
                    first_chunks(sp, w, m, next_weights_loaded)
                    zero_table(sp, w, m, range(NT), next_table_zeroed)

        @block.gpsimd
        def _(pool):
            pool.sem_clear(range(min(used), max(used) + 1))

            def values_padded():
                pool.memset(v_quad[:, :, :, :, :], 0.0).then_inc(pad_ready, 1)
                pool.memset(v[:, :, :, HD:HD + 1], 1.0).then_inc(ones_ready, 1)
                pool.memset(heads_out[:, :, :, :], 0.0).then_inc(attn_stored, 1)
                pool.wait_ge(pad_ready, 1)
                pool.wait_ge(ones_ready, 1)

            def stage_heads(o, j):
                if isinstance(o, int) and j < 2:
                    return
                wait_count(pool, qkT_psum, o * 8 + (j - 1))
                spread_heads(pool, m, o, j, staged)

            def stage_values(o, j):
                wait_count(pool, pv_psum, o * 8 + (j - 1))
                src = v[:, j // 2 * 2:j // 2 * 2 + 2, bass.ds(o * 8 + j % 2 * 4, 4), :]
                pool.tensor_copy(v_quad[:, j % 2, :, :, 0:HD + 1], src).then_inc(v_staged, 1)

            def store(o, j):
                pool.wait_ge(quad_out, o * 8 + (j + 1))
                pool.tensor_copy(attn[:, j // 2 * 2:j // 2 * 2 + 2, bass.ds(o * 64 + j % 2 * 32, 32)],
                                 heads_out[:, j % 2, :, :]).then_inc(attn_stored, 1)

            def behind(step, o, j, lag):
                if j >= lag:
                    step(o, j - lag)
                elif not isinstance(o, int):
                    step(o - 1, j - lag + 8)

            def octet(o):
                for j in range(2 * B):
                    if isinstance(o, int) and j == EARLY:
                        pool.wait_ge(qk_ready, NT - EARLY)
                    if isinstance(o, int) and j == 2:
                        pool.wait_ge(v_ready, B)
                    stage_heads(o, j)
                    if isinstance(o, int) and j == 1:
                        values_padded()
                    behind(stage_values, o, j, 2)
                    behind(store, o, j, 4)

            octet(0)
            with pool.Fori(1, NH // 8) as o:
                octet(o)
            for j in (6, 7):
                stage_values(NH // 8 - 1, j)
            for j in range(4, 8):
                store(NH // 8 - 1, j)

        def by_pairs(eng, pair):
            rounds = NQUAD // 2
            for o in range(NH // 8):
                if o == 0:
                    for p in range(8):
                        pair(p // 4, p % 4, o)
                with eng.Fori(max(2, B * o), min(rounds - 1, B * (o + 1))) as i:
                    for p in range(4):
                        pair(i, p, o)
            for p in range(4):
                pair(rounds - 1, p, o)

        def exists(number):
            return not isinstance(number, int) or number >= 0

        def last_round(i):
            return isinstance(i, int) and i == NQUAD // 2 - 1

        @block.scalar
        def _(act):
            def take_qkT(quad, q2):
                act.wait_ge(qkT_psum, quad + 1)
                wait_count(act, s_psum, quad * 2 - 2)
                act.copy(qkT[:, q2, :, :, :].rearrange("p t q n -> p (t q n)"), qk_bank[:, :])\
                   .then_inc(qkT_ready, 1)

            def take_off(quad, q2):
                act.wait_ge(off_in, quad + 1)
                act.activation(off_exp[:, q2, :, :], off_shift[:, q2, :, :], ACT.Exp).then_inc(off_ready, 1)

            def take_outT(quad, q2):
                act.wait_ge(pv_psum, quad + 1)
                wait_count(act, turned_psum, quad - 1)
                act.copy(heads_outT[:, q2, :], outT_sums).then_inc(outT_ready, 1)

            def take_probsT(i, p):
                wait_count(act, pv_psum, i * 2 + (p // 2 - 1))
                act.wait_ge(pT_psum, i * 8 + (2 * p + 2))
                act.copy(probsT[:, (2 * p + 1) % 8, :], probs_banks[1][:, 0:P + S]).then_inc(pT_act, 1)

            def pair(i, p, o):
                n = i * 4 + p
                if p == 0 or p == 2 and not last_round(i):
                    take_qkT(i * 2 + (p // 2 + 1), 1 - p // 2)
                wait_count(act, pT_psum, n * 2 - 6)
                for k in (2 * p, 2 * p + 1):
                    act.wait_ge(scored, i * 16 + (2 * k + 2))
                    act.activation(probs[:, k, 0:P], neg_scores[:, k % 4, 0:P], ACT.Exp,
                                   bias=neg_max[:, k, 0:1], scale=-1.0).then_inc(exp_done, 1)
                    act.activation(probs[:, k, P:P + S], neg_scores[:, k % 4, P:P + S], ACT.Exp,
                                   bias=neg_max[:, k, 1:2], scale=-1.0).then_inc(exp_done, 1)
                if exists(n - 2):
                    take_probsT(i, p - 2)
                if p % 2 == 0:
                    if exists(i * 2 + (p // 2 - 2)):
                        take_outT(i * 2 + (p // 2 - 2), p // 2)
                    if exists(i * 2 + (p // 2 - 1)):
                        take_off(i * 2 + (p // 2 - 1), 1 - p // 2)

            take_qkT(0, 0)
            for b in range(B):
                act.copy(v[:, 2 * b:2 * b + 2, :, 0:HD],
                         raw_v(m, 2 * b, 2).rearrange("p (t h d) -> p t h d", t=2, d=HD)).then_inc(v_ready, 1)
            by_pairs(act, pair)
            take_probsT(NQUAD // 2, -2)
            take_outT(NQUAD - 2, 0)
            take_off(NQUAD - 1, 1)
            take_probsT(NQUAD // 2, -1)
            take_outT(NQUAD - 1, 1)
            for half in range(2):
                act.wait_ge(attnT_psum, 2 * half + 1)
                act.copy(attnT[:, 0, half * 512:half * 512 + 512], bank[2 * half][:, :]).then_inc(attnT_act, 1)
            norm_tiles_scalar(act, m, s)

        @block.vector
        def _(vec):
            vec.tensor_scalar(neg_offset[:, :], m.offset[:, :], -1.0, None, ALU.mult).then_inc(neg_off_ready, 1)
            def take_probsT(i, p):
                n = i * 4 + p
                wait_count(vec, pv_psum, i * 2 + (p // 2 - 1))
                vec.wait_ge(pT_psum, n * 2 + 1)
                vec.tensor_copy(probsT[:, 2 * p % 8, :], probs_banks[0][:, 0:P + S]).then_inc(pT_vec, 1)

            def finish_quad(quad, q2):
                vec.wait_ge(turned_psum, quad + 1)
                vec.wait_ge(off_ready, quad + 1)
                vec.tensor_tensor(denom[:, :, :], sums[:, :, :, HD], off_exp[:, q2, :, :], ALU.add)\
                   .then_inc(den_ready, 1)
                vec.wait_ge(den_ready, quad + 1)
                vec.reciprocal(rdenom[:, :, :], denom[:, :, :]).then_inc(rden_ready, 1)
                vec.wait_ge(rden_ready, quad + 1)
                vec.wait_ge(attn_stored, 1 if isinstance(quad, int) and quad == 0 else quad)
                vec.tensor_tensor(heads_out[:, q2, :, :].rearrange("p t (g d) -> p t g d", d=HD),
                                  sums[:, :, :, 0:HD],
                                  rdenom[:, :, :].unsqueeze(3).to_broadcast([P, 2, 4, HD]),
                                  ALU.mult).then_inc(quad_out, 1)

            def pair(i, p, o):
                n = i * 4 + p
                due, free = n + 1, n * 4 - 4
                if not isinstance(i, int):
                    due, free = vec.to_reg(due), vec.to_reg(free)
                vec.wait_ge(bias_loaded[o % 2], 16 * (o // 2 + 1))
                vec.wait_ge(s_psum, due)
                wait_count(vec, exp_done, free)
                for k in (2 * p, 2 * p + 1):
                    scores, tiles = score_banks[k % 4], bias[:, o % 2, k, :]
                    off = neg_offset[:, 8 * o + k:8 * o + k + 1]
                    vec.tensor_tensor_reduce(neg_scores[:, k % 4, 0:P], scores[:, 0:P], tiles[:, P:2 * P], -1.0,
                                             off, ALU.add, ALU.min, neg_max[:, k, 0:1]).then_inc(scored, 1)
                    vec.tensor_tensor_reduce(neg_scores[:, k % 4, P:P + S], scores[:, P:P + S], tiles, -1.0,
                                             off, ALU.add, ALU.min, neg_max[:, k, 1:2]).then_inc(scored, 1)
                if p % 2 == 1:
                    q2 = p // 2
                    vec.wait_ge(scored, n * 4 + 4)
                    wait_count(vec, off_ready, i * 2 + (q2 - 1))
                    vec.tensor_tensor(off_shift[:, q2, :, :],
                                      neg_max[:, 4 * q2:4 * q2 + 4, :].rearrange("p g t -> p t g"),
                                      neg_offset[:, 8 * o + 4 * q2:8 * o + 4 * q2 + 4].unsqueeze(1)
                                      .to_broadcast([P, 2, 4]),
                                      ALU.subtract).then_inc(off_in, 1)
                if exists(n - 2):
                    take_probsT(i, p - 2)
                if p % 2 == 1 and exists(i * 2 + (p // 2 - 2)):
                    finish_quad(i * 2 + (p // 2 - 2), p // 2)

            rotate_tiles(vec, m, range(EARLY, NT), lambda t: None, lambda: None, sin_done, cos_done, qk_ready)
            vec.wait_ge(neg_off_ready, 1)
            by_pairs(vec, pair)
            take_probsT(NQUAD // 2, -2)
            take_probsT(NQUAD // 2, -1)
            finish_quad(NQUAD - 2, 0)
            finish_quad(NQUAD - 1, 1)
            for half in range(2):
                vec.wait_ge(attnT_psum, 2 * half + 2)
                vec.tensor_copy(attnT[:, 1, half * 512:half * 512 + 512], bank[2 * half + 1][:, :])\
                   .then_inc(attnT_vec, 1)
            for t in range(NT):
                vec.wait_ge(o_psum, t + 1)
                vec.tensor_tensor(m.x[:, t, :], bank[4 + t % 2][:, 0:DM], m.x[:, t, :], ALU.add).then_inc(x_ready, 1)
                vec.wait_ge(x_ready, t + 1)
                norm_tile_moments(vec, m, s, t)
                if t > 0:
                    norm_tile_scale(vec, m, s, t - 1)
            norm_tile_scale(vec, m, s, NT - 1)

        @block.tensor
        def _(pe):
            def turn_heads(quad, q2):
                wait_count(pe, staged, quad * 2 - 2)
                wait_count(pe, qkT_ready, quad)
                for tile in range(2):
                    for which in range(2):
                        at = (2 * tile + which) * P
                        ins = pe.transpose(qk_bank[:, at:at + P],
                                           qk_pad[:, q2, tile, which, :, :].rearrange("p g r -> p (g r)"),
                                           m.ident[:, :])
                ins.then_inc(qkT_psum, 1)

            def score(i, p):
                q2 = p // 2
                pe.wait_ge(qkT_ready, i * 2 + (q2 + 1))
                wait_count(pe, scored, i * 16 + (4 * p - 4))
                for tile in range(2):
                    for a in range(2):
                        g = 2 * (p % 2) + a
                        rows = slice(32 * g, 32 * g + 32)
                        ins = pe.matmul(score_banks[g][:, 0:P] if tile == 0 else score_banks[g][:, P:P + S],
                                        qkT[rows, q2, tile, 0, :],
                                        qkT[rows, q2, 0, 1, :] if tile == 0 else qkT[rows, q2, :, 1, :],
                                        start=True, stop=True)
                ins.then_inc(s_psum, 1)

            def turn_probs(i, p):
                for a in range(2):
                    pe.wait_ge(exp_done, i * 16 + (4 * p + 2 * a + 2))
                    wait_count(pe, (pT_vec, pT_act)[a], i * 4 + p)
                    for j in range(3):
                        ins = pe.transpose(probs_banks[a][:, j * P:j * P + P],
                                           probs[:, (2 * p + a) % 8, j * P:j * P + P], m.ident[:, :])
                    ins.then_inc(pT_psum, 1)

            def weigh_values(quad, q2):
                pe.wait_ge(v_staged, quad + 1)
                pe.wait_ge(pT_vec, quad * 2 + 2)
                pe.wait_ge(pT_act, quad * 2 + 2)
                wait_count(pe, outT_ready, quad)
                wait_count(pe, quad_out, quad)
                for tile in range(2):
                    for g in range(4):
                        ins = pe.matmul(outT_sums[32 * g:32 * g + 32, tile * P:S], v_quad[:, q2, tile, g, :],
                                        probsT[:, 4 * q2 + g, tile * S:tile * P + S],
                                        start=(tile == 0), stop=(tile == 1))
                ins.then_inc(pv_psum, 1)

            def turn_outputs(quad, q2):
                pe.wait_ge(outT_ready, quad + 1)
                for tile in range(2):
                    ins = pe.transpose(out_bank[:, S + tile * P:S + tile * P + P],
                                       heads_outT[:, q2, tile * P:tile * P + P], m.ident[:, :])
                ins.then_inc(turned_psum, 1)

            def pair(i, p, o):
                score(i, p)
                if exists(i * 4 + (p - 2)):
                    turn_probs(i, p - 2)
                if exists(i * 2 + (p // 2 - 2)):
                    if p % 2 == 0:
                        weigh_values(i * 2 + (p // 2 - 2), p // 2)
                    else:
                        turn_outputs(i * 2 + (p // 2 - 2), p // 2)
                if p % 2 == 1 and not last_round(i):
                    turn_heads(i * 2 + (p // 2 + 2), p // 2)

            turn_heads(0, 0)
            turn_heads(1, 1)
            by_pairs(pe, pair)
            turn_probs(NQUAD // 2, -2)
            weigh_values(NQUAD - 2, 0)
            turn_probs(NQUAD // 2, -1)
            turn_outputs(NQUAD - 2, 0)
            weigh_values(NQUAD - 1, 1)
            turn_outputs(NQUAD - 1, 1)
            pe.wait_ge(attn_stored, NQUAD + 1)
            for half in range(2):
                for q in range(4):
                    for c in range(KC):
                        ins = pe.transpose(bank[2 * half + c][:, q * P:q * P + P],
                                           attn[:, 4 * half + q, c * P:c * P + P], m.ident[:, :])
                        if q == 3:
                            ins.then_inc(attnT_psum, 1)
            pe.wait_ge(attnT_vec, 2)
            pe.wait_ge(attnT_act, 2)
            for t in range(NT):
                if t >= 2:
                    pe.wait_ge(x_ready, t - 1)
                for c in range(KC):
                    ins = pe.matmul(bank[4 + t % 2][:, 0:DM], attnT[:, c, t * P:t * P + P], w_o[:, c, :],
                                    start=(c == 0), stop=(c == KC - 1))
                ins.then_inc(o_psum, 1)
            norm_tensor(pe, m, s)


class WeightSlot:

    def __init__(self, gu, lo, hi):
        self.gu, self.lo, self.hi = gu[:, :], lo[:, :], hi[:, :]


class OnChip:

    def __init__(self, sb, bank):
        self.bank = bank
        self.x = sb("x", [P, NT, DM])
        self.xn = sb("xn", [P, NT, DM])
        self.xnT = sb("xnT", [P, KC, T])
        self.stats = sb("stats", [P, NT, 6])
        self.moments = sb("moments", [P, NT, 2])
        self.var_eps = sb("var_eps", [P, NT])
        self.std = sb("std", [P, NT])
        self.rstd = sb("rstd", [P, NT])
        self.shift = sb("shift", [P, NT])
        self.gate = sb("gate", [P, KC, E])
        self.sh_gate = sb("sh_gate", [P, KC, IS])
        self.sh_up = sb("sh_up", [P, KC, IS])
        self.sh_down = sb("sh_down", [P, 3, DM])
        self.slots = [WeightSlot(sb(f"w_gu{i}", [P, EC * KC * 2 * I]), sb(f"w_lo{i}", [ILO, EC * DM]),
                                 sb(f"w_hi{i}", [IHI, EC * DM])) for i in range(KEPT)]
        self.scratch = sb("scratch", [P, SCRATCH])
        self.ident = sb("ident", [P, P])
        self.by_expert = sb("by_expert", [P, P])
        self.triangle = sb("triangle", [P, P], BF16)
        self.ones = sb("ones", [P, P], BF16)
        self.resets = sb("resets", [P, NT, E])
        self.own_mask = sb("own_mask", [P, EC])
        self.zeros = sb("zeros", [P, DM])
        self.rope_cos = sb("rope_cos", [P, 2, 2, HD])
        self.rope_sin = sb("rope_sin", [P, 2, 2, HD])
        self.offset = sb("offset", [P, NH])
        self.bias_rows = sb("bias_rows", [NH, MAXB + S])


class Dram:

    def __init__(self, nc, given, out):
        self.x = given["x"]
        self.gate_t = given["gate_t"]
        self.w_gu, self.w_lo, self.w_hi = given["w_gu"], given["w_lo"], given["w_hi"]
        self.sw_gate, self.sw_up, self.sw_down = given["sw_gate"], given["sw_up"], given["sw_down"]
        self.w_qkv, self.w_o = given["w_qkv"], given["w_o"]
        self.bias_reversed, self.offset = given["bias_reversed"], given["offset"]
        self.rope_cos, self.rope_sin = given["rope_cos"], given["rope_sin"]
        self.out = out
        self.xn_dram = nc.dram_tensor("xn_rows", [T, DM], F32).ap()
        self.table = nc.dram_tensor("choice_table", [T * TOPK, DM], F32).ap()
        self.bias_dram = nc.dram_tensor("bias_rows_dram", [P, NH, 3 * P], F32).ap()


def build(nc, given, out):
    w = Dram(nc, given, out)
    with ExitStack() as ctx:
        def sb(name, shape, dt=F32):
            return ctx.enter_context(nc.sbuf_tensor(name, shape, dt))

        m = OnChip(sb, [ctx.enter_context(nc.psum_tensor(f"bank{i}", [P, 512], F32)) for i in range(8)])
        loaded = [[ctx.enter_context(nc.semaphore(f"ff{f}_weights{i}")) for i in range(RING)] for f in range(2)]
        gathered, scattered = ([[ctx.enter_context(nc.semaphore(f"ff{f}_{name}{i}")) for i in range(depth)]
                                for f in range(2)] for name, depth in (("gathered", AHEAD), ("scattered", 2)))
        table_zeroed = [ctx.enter_context(nc.semaphore(f"ff{f}_table_zeroed")) for f in range(2)]
        ff_sems = {}

        def ff_sem(name):
            if name not in ff_sems:
                ff_sems[name] = ctx.enter_context(nc.semaphore(f"ff_{name}"))
            return ff_sems[name]

        attention_loaded = ctx.enter_context(nc.semaphore("attention_loaded"))
        bias_stored = ctx.enter_context(nc.semaphore("bias_stored"))
        feed_forward(nc, w, m, ff_sem, "ff0", loaded[0], gathered[0], scattered[0], table_zeroed[0],
                     True, attention_loaded, bias_stored)
        attention(nc, w, m, [x.num for x in ff_sems.values()], loaded[1], table_zeroed[1], bias_stored)
        feed_forward(nc, w, m, ff_sem, "ff1", loaded[1], gathered[1], scattered[1], table_zeroed[1],
                     False, attention_loaded, bias_stored)


def rope_tables():
    half = HD // 2
    freq = 1.0 / 10000.0 ** (np.arange(half, dtype=np.float32) / np.float32(half))
    angle = np.outer(np.arange(S, dtype=np.float32), freq.astype(np.float32)).astype(np.float32)
    cos = np.concatenate([np.cos(angle), np.cos(angle)], axis=1)
    sin = np.concatenate([-np.sin(angle), np.sin(angle)], axis=1)
    scale = np.array([HD ** -0.5, 1.0], dtype=np.float32)

    def lay(table):
        table = table.astype(np.float32).reshape(2, P, 1, HD) * scale.reshape(1, 1, 2, 1)
        return np.ascontiguousarray(table.transpose(1, 0, 2, 3).reshape(P, 4 * HD).astype(np.float32))

    return lay(cos), lay(sin)


def kernel(**inputs):
    import concourse.bacc as bacc
    from concourse.bass_utils import run_bass_kernel_spmd

    a = {k: np.asarray(v) for k, v in inputs.items()}
    w_gu = np.concatenate([a["L0_ffn_w_gate"], a["L0_ffn_w_up"]], axis=2)
    w_gu = w_gu.reshape(EC, NC, KC, P, 2 * I).transpose(1, 3, 0, 2, 4).reshape(NC, P, EC * KC * 2 * I)
    w_dn = a["L0_ffn_w_down"].reshape(EC, NC, I, DM).transpose(1, 2, 0, 3).reshape(NC, I, EC * DM)
    rope_cos, rope_sin = rope_tables()
    laid = {
        "x": a["L0_attn_hidden_states"].reshape(T, DM),
        "gate_t": a["L0_ffn_gate_w"].T,
        "w_gu": w_gu, "w_lo": w_dn[:, :ILO], "w_hi": w_dn[:, ILO:],
        "sw_gate": a["L0_ffn_sw_gate"], "sw_up": a["L0_ffn_sw_up"], "sw_down": a["L0_ffn_sw_down"],
        "w_qkv": np.concatenate([a["L0_attn_Wq"].T, a["L0_attn_Wk"].T, a["L0_attn_Wv"].T], axis=1),
        "w_o": a["L0_attn_Wo"].T,
        "bias_reversed": a["L0_attn_learnable_bias"][:, ::-1],
        "offset": a["L0_attn_softmax_offset"],
        "rope_cos": rope_cos, "rope_sin": rope_sin,
    }
    nc = bacc.Bacc("TRN2", target_bir_lowering=False, num_devices=1)
    arrays, given = {}, {}
    for name, value in laid.items():
        value = np.ascontiguousarray(value)
        arrays[f"in_{name}"] = value
        given[name] = nc.dram_tensor(f"in_{name}", value.shape, mybir.dt.from_np(value.dtype),
                                     kind="ExternalInput").ap()
    build(nc, given, nc.dram_tensor("out_x", [B, S, DM], F32, kind="ExternalOutput").ap())
    r = run_bass_kernel_spmd(nc, [arrays], core_ids=[0])
    return r.results[0]["out_x"]
```
